# Optimizing a Trainium2 kernel written in Bass

```python
import numpy as np
import jax
import jax.numpy as jnp

def _softmax(x, axis=-1):
    return jax.nn.softmax(x, axis=axis)

def _gelu(x):
    return jax.nn.gelu(x, approximate=True)

def _silu(x):
    return jax.nn.silu(x)

def _sigmoid(x):
    return jax.nn.sigmoid(x)

def _layernorm(x, axis=-1, eps=1e-05):
    m = jnp.mean(x, axis=axis, keepdims=True)
    v = jnp.var(x, axis=axis, keepdims=True)
    return (x - m) / jnp.sqrt(v + eps)

def _scatter_add(tgt, idx, src, axis=0):
    return tgt.at[idx].add(src)

def _segment_sum(src, seg, n):
    return jax.ops.segment_sum(src, seg, n)
kernel_name = 'mk_xattn_ffn_d2_seqx_r8_758b27'

def setup_inputs(seed: int=0):
    np.random.seed(seed)
    _w = jnp.asarray

    def _rec_inputs():
        import jax
        import jax.numpy as jnp
        _rk = jax.random.key(seed)
        x = -0.000125 + 0.9999 * jax.random.normal(jax.random.fold_in(_rk, 1), (32, 64, 512), jnp.float32)
        _lenS = 64 - jax.random.randint(jax.random.fold_in(_rk, 7), (32,), 0, max(1, 64 // 4) + 1, jnp.int32)
        _lenS2 = 64 - jax.random.randint(jax.random.fold_in(_rk, 8), (32,), 0, max(1, 64 // 4) + 1, jnp.int32)
        _ctx_4096P = jax.random.normal(jax.random.fold_in(_rk, 11), (32, 16, 512), jnp.float32)
        _ctx_4096c = jax.random.dirichlet(jax.random.fold_in(_rk, 511), 0.3 * jnp.ones((16,), jnp.float32), (32, 64))
        _ctx_4096t = jnp.einsum('bsk,bkd->bsd', _ctx_4096c, _ctx_4096P)
        _ctx_4096t = _ctx_4096t * jax.lax.rsqrt(jnp.mean(jnp.square(_ctx_4096t)) + 1e-12) * 0.953939
        ctx_4096 = -1.52775e-05 + 0.999936 * (_ctx_4096t + 0.3 * jax.random.normal(jax.random.fold_in(_rk, 611), (32, 64, 512), jnp.float32))
        return (x, ctx_4096)
    x, ctx_4096 = _rec_inputs()

    def _L0_xattn_setup():
        import jax, jax.numpy as jnp
        import numpy as np
        H = 8
        C = 2

        def _autocorrelation(Q, K, V):
            B, L, D = Q.shape
            d = D // H
            q = Q.reshape(B, L, H, d).transpose(0, 2, 1, 3)
            k = K.reshape(B, L, H, d).transpose(0, 2, 1, 3)
            v = V.reshape(B, L, H, d).transpose(0, 2, 1, 3)
            qf = jnp.fft.fft(q, axis=2)
            kf = jnp.fft.fft(k, axis=2)
            corr = jnp.fft.ifft(qf * jnp.conj(kf), axis=2).real
            topk = int(C * np.log(L))
            w, idx = jax.lax.top_k(corr.transpose(0, 1, 3, 2), topk)
            w = jax.nn.softmax(w, axis=-1)
            pos = jnp.arange(L)[:, None]
            out = jnp.zeros_like(v)
            for i in range(topk):
                g = jnp.minimum(idx[:, :, None, :, i] + pos, L - 1)
                out = out + w[:, :, None, :, i] * jnp.take_along_axis(v, g, axis=2)
            return out.transpose(0, 2, 1, 3).reshape(B, L, D)
        key = jax.random.key(seed)
        k1, k2, k3 = jax.random.split(key, 3)
        B, L, D = (16, 64, 512)
        Q = jax.random.normal(k1, (B, L, D), dtype=jnp.float32)
        K = jax.random.normal(k2, (B, L, D), dtype=jnp.float32)
        V = jax.random.normal(k3, (B, L, D), dtype=jnp.float32)
        return {'Q': Q, 'K': K, 'V': V}
    _L0_xattn_all = _L0_xattn_setup()
    _L0_xattn_in = {k: v for k, v in _L0_xattn_all.items() if k in ()}
    del _L0_xattn_all

    def _L0_ffn_setup():
        import jax, jax.numpy as jnp
        import numpy as np
        B_, S, D_IN, D_OUT = (4, 256, 512, 512)
        N, RANK, ALPHA = (8, 16, 32)
        SCALE = ALPHA / RANK
        key = jax.random.key(seed)
        kx, ka, kb, kw, kbias = jax.random.split(key, 5)
        x = jax.random.normal(kx, (B_, S, D_IN), dtype=jnp.float32)
        lora_A = jax.random.normal(ka, (N, RANK, D_IN), dtype=jnp.float32) * (1.0 / np.sqrt(D_IN))
        lora_B = jax.random.normal(kb, (N, D_OUT, RANK), dtype=jnp.float32) * (1.0 / np.sqrt(RANK))
        W = jax.random.normal(kw, (D_OUT, D_IN), dtype=jnp.float32) * (1.0 / np.sqrt(D_IN))
        bias = jax.random.normal(kbias, (D_OUT,), dtype=jnp.float32) * 0.01
        lora_weights = jnp.full((N,), 1.0 / N, dtype=jnp.float32)
        return {'x': x, 'lora_A': lora_A, 'lora_B': lora_B, 'W': W, 'bias': bias, 'lora_weights': lora_weights}
    _L0_ffn_all = _L0_ffn_setup()
    _L0_ffn_in = {k: v for k, v in _L0_ffn_all.items() if k in ('lora_A', 'lora_B', 'W', 'bias', 'lora_weights')}
    del _L0_ffn_all

    def _L1_xattn_setup():
        import jax, jax.numpy as jnp
        import numpy as np
        EMBED = 512
        NUM_Q = 32
        NUM_KV = 8
        GROUPS = NUM_Q // NUM_KV
        HEAD_DIM = EMBED // NUM_Q
        KV_DIM = HEAD_DIM * NUM_KV
        key = jax.random.key(seed)
        ks = jax.random.split(key, 12)
        B, S = (2, 256)
        s = 0.02
        return {'query': jax.random.normal(ks[0], (B, S, EMBED), jnp.float32), 'key': jax.random.normal(ks[1], (B, S, EMBED), jnp.float32), 'value': jax.random.normal(ks[2], (B, S, EMBED), jnp.float32), 'Wq': jax.random.normal(ks[3], (EMBED, EMBED), jnp.float32) * s, 'bq': jnp.zeros((EMBED,), jnp.float32), 'Wk': jax.random.normal(ks[4], (EMBED, KV_DIM), jnp.float32) * s, 'bk': jnp.zeros((KV_DIM,), jnp.float32), 'Wv': jax.random.normal(ks[5], (EMBED, KV_DIM), jnp.float32) * s, 'bv': jnp.zeros((KV_DIM,), jnp.float32), 'Wo': jax.random.normal(ks[6], (EMBED, EMBED), jnp.float32) * s, 'bo': jnp.zeros((EMBED,), jnp.float32)}
    _L1_xattn_all = _L1_xattn_setup()
    _L1_xattn_in = {k: v for k, v in _L1_xattn_all.items() if k in ('Wq', 'bq', 'Wk', 'bk', 'Wv', 'bv', 'Wo', 'bo')}
    del _L1_xattn_all

    def _L1_ffn_setup():
        import jax, jax.numpy as jnp
        import numpy as np
        HID, INT, LAT, NE, K = (512, 1024, 256, 8, 2)
        LN_EPS = 1e-05

        def _layernorm(x, gamma, beta):
            mu = jnp.mean(x, axis=-1, keepdims=True)
            var = jnp.var(x, axis=-1, keepdims=True)
            return (x - mu) * jax.lax.rsqrt(var + LN_EPS) * gamma + beta
        key = jax.random.key(seed)
        ks = jax.random.split(key, 8)
        s = lambda d: 1.0 / np.sqrt(d)
        return {'hidden_states': jax.random.normal(ks[0], (4, 256, HID), jnp.float32), 'gate_w': jax.random.normal(ks[1], (HID, NE), jnp.float32) * s(HID), 'up_w': jax.random.normal(ks[2], (HID, INT), jnp.float32) * s(HID), 'down_w': jax.random.normal(ks[3], (INT, HID), jnp.float32) * s(INT), 'fc1_w': jax.random.normal(ks[4], (HID, LAT), jnp.float32) * s(HID), 'fc2_w': jax.random.normal(ks[5], (LAT, HID), jnp.float32) * s(LAT), 'expert_w': jax.random.normal(ks[6], (LAT, LAT), jnp.float32), 'ln_gamma': jnp.ones((HID,), jnp.float32), 'ln_beta': jnp.zeros((HID,), jnp.float32)}
    _L1_ffn_all = _L1_ffn_setup()
    _L1_ffn_in = {k: v for k, v in _L1_ffn_all.items() if k in ('gate_w', 'up_w', 'down_w', 'fc1_w', 'fc2_w', 'expert_w', 'ln_gamma', 'ln_beta')}
    del _L1_ffn_all
    return {'x': x, 'ctx_4096': ctx_4096, 'L0_ffn_lora_A': _L0_ffn_in['lora_A'], 'L0_ffn_lora_B': _L0_ffn_in['lora_B'], 'L0_ffn_W': _L0_ffn_in['W'], 'L0_ffn_bias': _L0_ffn_in['bias'], 'L0_ffn_lora_weights': _L0_ffn_in['lora_weights'], 'L1_xattn_Wq': _L1_xattn_in['Wq'], 'L1_xattn_bq': _L1_xattn_in['bq'], 'L1_xattn_Wk': _L1_xattn_in['Wk'], 'L1_xattn_bk': _L1_xattn_in['bk'], 'L1_xattn_Wv': _L1_xattn_in['Wv'], 'L1_xattn_bv': _L1_xattn_in['bv'], 'L1_xattn_Wo': _L1_xattn_in['Wo'], 'L1_xattn_bo': _L1_xattn_in['bo'], 'L1_ffn_gate_w': _L1_ffn_in['gate_w'], 'L1_ffn_up_w': _L1_ffn_in['up_w'], 'L1_ffn_down_w': _L1_ffn_in['down_w'], 'L1_ffn_fc1_w': _L1_ffn_in['fc1_w'], 'L1_ffn_fc2_w': _L1_ffn_in['fc2_w'], 'L1_ffn_expert_w': _L1_ffn_in['expert_w'], 'L1_ffn_ln_gamma': _L1_ffn_in['ln_gamma'], 'L1_ffn_ln_beta': _L1_ffn_in['ln_beta']}

def reference(x, ctx_4096, L0_ffn_lora_A, L0_ffn_lora_B, L0_ffn_W, L0_ffn_bias, L0_ffn_lora_weights, L1_xattn_Wq, L1_xattn_bq, L1_xattn_Wk, L1_xattn_bk, L1_xattn_Wv, L1_xattn_bv, L1_xattn_Wo, L1_xattn_bo, L1_ffn_gate_w, L1_ffn_up_w, L1_ffn_down_w, L1_ffn_fc1_w, L1_ffn_fc2_w, L1_ffn_expert_w, L1_ffn_ln_gamma, L1_ffn_ln_beta):
    import jax
    import jax.numpy as jnp

    def _L0_xattn_ref(Q, K, V):
        import jax, jax.numpy as jnp
        import numpy as np
        H = 8
        C = 2

        def _autocorrelation(Q, K, V):
            B, L, D = Q.shape
            d = D // H
            q = Q.reshape(B, L, H, d).transpose(0, 2, 1, 3)
            k = K.reshape(B, L, H, d).transpose(0, 2, 1, 3)
            v = V.reshape(B, L, H, d).transpose(0, 2, 1, 3)
            qf = jnp.fft.fft(q, axis=2)
            kf = jnp.fft.fft(k, axis=2)
            corr = jnp.fft.ifft(qf * jnp.conj(kf), axis=2).real
            topk = int(C * np.log(L))
            w, idx = jax.lax.top_k(corr.transpose(0, 1, 3, 2), topk)
            w = jax.nn.softmax(w, axis=-1)
            pos = jnp.arange(L)[:, None]
            out = jnp.zeros_like(v)
            for i in range(topk):
                g = jnp.minimum(idx[:, :, None, :, i] + pos, L - 1)
                out = out + w[:, :, None, :, i] * jnp.take_along_axis(v, g, axis=2)
            return out.transpose(0, 2, 1, 3).reshape(B, L, D)
        return _autocorrelation(Q, K, V)

    def _L0_ffn_ref(x, lora_A, lora_B, W, bias, lora_weights):
        import jax, jax.numpy as jnp
        import numpy as np
        B_, S, D_IN, D_OUT = (4, 256, 512, 512)
        N, RANK, ALPHA = (8, 16, 32)
        SCALE = ALPHA / RANK
        h = jnp.einsum('bsd,nrd->nbsr', x, lora_A)
        coef = (SCALE * lora_weights)[:, None, None]
        lora_out = jnp.einsum('nbsr,nor->bso', h, lora_B * coef)
        base = jnp.einsum('bsd,od->bso', x, W) + bias
        return base + lora_out

    def _L1_xattn_ref(query, key, value, Wq, bq, Wk, bk, Wv, bv, Wo, bo):
        import jax, jax.numpy as jnp
        import numpy as np
        EMBED = 512
        NUM_Q = 32
        NUM_KV = 8
        GROUPS = NUM_Q // NUM_KV
        HEAD_DIM = EMBED // NUM_Q
        KV_DIM = HEAD_DIM * NUM_KV
        B, S, _ = query.shape
        Q = query @ Wq + bq
        K = key @ Wk + bk
        V = value @ Wv + bv
        Q = Q.reshape(B, S, NUM_KV, GROUPS, HEAD_DIM).transpose(0, 2, 3, 1, 4)
        K = K.reshape(B, S, NUM_KV, HEAD_DIM).transpose(0, 2, 1, 3)
        V = V.reshape(B, S, NUM_KV, HEAD_DIM).transpose(0, 2, 1, 3)
        scale = 1.0 / jnp.sqrt(jnp.asarray(HEAD_DIM, query.dtype))
        scores = jnp.einsum('bhgqd,bhkd->bhgqk', Q, K) * scale
        w = jax.nn.softmax(scores, axis=-1)
        y = jnp.einsum('bhgqk,bhkd->bhgqd', w, V)
        y = y.transpose(0, 3, 1, 2, 4).reshape(B, S, EMBED)
        return y @ Wo + bo

    def _L1_ffn_ref(hidden_states, gate_w, up_w, down_w, fc1_w, fc2_w, expert_w, ln_gamma, ln_beta):
        import jax, jax.numpy as jnp
        import numpy as np
        HID, INT, LAT, NE, K = (512, 1024, 256, 8, 2)
        LN_EPS = 1e-05

        def _layernorm(x, gamma, beta):
            mu = jnp.mean(x, axis=-1, keepdims=True)
            var = jnp.var(x, axis=-1, keepdims=True)
            return (x - mu) * jax.lax.rsqrt(var + LN_EPS) * gamma + beta
        logits = jnp.einsum('bsh,he->bse', hidden_states, gate_w)
        routing_weights, selected_experts = jax.lax.top_k(logits, K)
        h = jax.nn.relu(jnp.einsum('bsh,hi->bsi', hidden_states, up_w)) ** 2
        shared_out = jnp.einsum('bsi,ih->bsh', h, down_w)
        x_latent = jnp.einsum('bsh,hl->bsl', hidden_states, fc1_w)
        expert_out = jnp.einsum('bsl,lm->bsm', x_latent, expert_w)
        moe_out = expert_out * jnp.sum(routing_weights, axis=-1, keepdims=True)
        routed_out = jnp.einsum('bsl,lh->bsh', moe_out, fc2_w)
        return _layernorm(shared_out + routed_out, ln_gamma, ln_beta)
    x = x + _L0_xattn_ref(_layernorm(x, axis=-1), ctx_4096, ctx_4096)
    x = x + _L0_ffn_ref(_layernorm(x, axis=-1), L0_ffn_lora_A, L0_ffn_lora_B, L0_ffn_W, L0_ffn_bias, L0_ffn_lora_weights)
    x = x + _L1_xattn_ref(_layernorm(x, axis=-1), ctx_4096, ctx_4096, L1_xattn_Wq, L1_xattn_bq, L1_xattn_Wk, L1_xattn_bk, L1_xattn_Wv, L1_xattn_bv, L1_xattn_Wo, L1_xattn_bo)
    x = x + _L1_ffn_ref(_layernorm(x, axis=-1), L1_ffn_gate_w, L1_ffn_up_w, L1_ffn_down_w, L1_ffn_fc1_w, L1_ffn_fc2_w, L1_ffn_expert_w, L1_ffn_ln_gamma, L1_ffn_ln_beta)
    return x

_drawn_inputs = setup_inputs


def setup_inputs(seed=0):
    import zlib

    import numpy as np

    out = dict(_drawn_inputs(seed))
    spreads = {'L0_ffn_lora_weights': (0.125, 0.2),
     'L1_xattn_bq': (0.0, 0.8),
     'L1_xattn_bk': (0.0, 0.8),
     'L1_xattn_bv': (0.0, 0.356),
     'L1_xattn_bo': (0.0, 0.1),
     'L1_ffn_ln_gamma': (1.0, 0.2),
     'L1_ffn_ln_beta': (0.0, 0.1)}
    factors = {'L0_ffn_bias': 8.0, 'L1_xattn_Wq': 8.0, 'L1_xattn_Wk': 8.0}
    for name, (base, spread) in spreads.items():
        noise = np.random.default_rng([zlib.crc32(name.encode()), seed]).standard_normal(out[name].shape)
        drawn = base * np.exp(spread * noise) if base else spread * noise
        out[name] = jnp.asarray(drawn.astype(out[name].dtype))
    for name, factor in factors.items():
        out[name] = (out[name] * factor).astype(out[name].dtype)
    return out
```

```python
from contextlib import ExitStack

import concourse.bass as bass
import numpy as np
from concourse import mybir

ALU = mybir.AluOpType
ACT = mybir.ActivationFunctionType
AX = mybir.AxisListType
F32 = mybir.dt.float32
F32R = mybir.dt.float32r
BF16 = mybir.dt.bfloat16

P = 128
BATCHES, SEQ, D = 32, 64, 512
TOKENS = BATCHES * SEQ
NT = TOKENS // P
DC = D // P
TOP = 8
ADAPT, RANK = 8, 16
LORA_SCALE = 32 / RANK
NKV, GROUPS, HD = 8, 4, 16
KVW = NKV * HD
PAIRS = NKV // 2
INNER, LAT, EXPERTS = 1024, 256, 8
IC = INNER // P
EPS = 1e-5
REMOVED = -3.0e38
REMOVED_BELOW = -1.0e38

Q0, K0, V0, W0, DFT = 0, 256, 512, 1024, 1536
ICORR0, IOUT0, IDENT0, HEAD0, ONES0, SEL0, HALF0, EPS0, SMALL = 0, 64, 192, 320, 328, 360, 872, 873, 874


def correlation_rows(n):
    h = n // 2
    return [("rr", f) for f in range(h + 1)] + [(k, f) for k in ("ii", "ir", "ri") for f in range(1, h)]


def transform(n, inputs, factor, rows):
    m = np.zeros((inputs, rows))
    s = np.arange(inputs)
    for r, (kind, f) in enumerate(correlation_rows(n)):
        angle = 2 * np.pi * ((f * s) % n) / n
        m[:, r] = np.cos(angle) if kind[factor] == "r" else -np.sin(angle)
    return m


def inverse(n, outputs, rows):
    m = np.zeros((rows, outputs))
    s = np.arange(outputs)
    for r, (kind, f) in enumerate(correlation_rows(n)):
        weight = (1.0 if f in (0, n // 2) else 2.0) / n
        angle = 2 * np.pi * ((f * s) % n) / n
        m[r] = weight * {"rr": np.cos, "ii": np.cos, "ir": lambda a: -np.sin(a), "ri": np.sin}[kind](angle)
    return m


def constants():
    dft = np.zeros((P, DFT))
    tq, tk = transform(SEQ, SEQ, 0, P), transform(SEQ, SEQ, 1, P)
    tw = transform(2 * SEQ, SEQ, 1, 2 * P)
    tv = transform(2 * SEQ, 2 * SEQ - 1, 0, 2 * P)
    tv = np.concatenate([tv[:SEQ - 1], tv[SEQ - 1:].sum(0, keepdims=True)])
    for b in range(2):
        rows = slice(SEQ * b, SEQ * b + SEQ)
        dft[rows, Q0 + P * b:Q0 + P * b + P] = tq
        dft[rows, K0 + P * b:K0 + P * b + P] = tk
        dft[rows, V0 + 2 * P * b:V0 + 2 * P * (b + 1)] = tv
        dft[rows, W0 + 2 * P * b:W0 + 2 * P * (b + 1)] = tw
    small = np.zeros((P, SMALL))
    small[:, ICORR0:ICORR0 + SEQ] = inverse(SEQ, SEQ, P)
    iv = inverse(2 * SEQ, SEQ, 2 * P)
    small[:, IOUT0:IOUT0 + SEQ], small[:, IOUT0 + SEQ:IOUT0 + 2 * SEQ] = iv[:P], iv[P:]
    small[:, IDENT0:IDENT0 + P] = np.eye(P)
    small[:, HEAD0:HEAD0 + NKV] = np.repeat(np.eye(NKV), HD, axis=0)
    small[:, ONES0:ONES0 + 2 * HD] = np.kron(np.eye(2), np.ones((SEQ, HD)))
    for p in range(PAIRS):
        for h in range(2):
            small[2 * p + h, SEL0 + P * p + SEQ * h:SEL0 + P * p + SEQ * (h + 1)] = 1.0
    small[:, HALF0], small[:, EPS0] = -0.5, EPS
    return dft.astype(np.float32), small.astype(np.float32)


def wait(eng, sem, value):
    if not (isinstance(value, int) and value <= 0):
        eng.wait_ge(sem, value)


def build(nc, x, ctx_in, lora_a, lora_b, w0, b0, lora_w, wq, bq, wk, bk, wv, bv, wo, bo,
          gate_w, up_w, down_w, fc1_w, fc2_w, expert_w, gamma, beta, dft_in, small_in, out):
    x_rows = x.rearrange("b s d -> (b s) d")
    ctx_rows = ctx_in.rearrange("b s d -> (b s) d")
    out_rows = out.rearrange("b s d -> (b s) d")
    x2_rows = nc.dram_tensor("x2_rows", [TOKENS, D], F32, kind="Internal").ap()

    with ExitStack() as ctx:
        def sb(name, shape, dt=F32, stack=ctx):
            return stack.enter_context(nc.sbuf_tensor(name, shape, dt))

        def sem(name):
            return ctx.enter_context(nc.semaphore(name))

        bank = [ctx.enter_context(nc.psum_tensor(f"bank{i}", [P, 512], F32)) for i in range(6)]
        wide = ctx.enter_context(nc.psum_tensor("wide", [P, 1024], F32))
        bank += [wide[:, 0:512], wide[:, 512:1024]]

        small = sb("small", [P, SMALL])
        selb = sb("selb", [NKV, PAIRS * P], BF16)
        ident = small[:, IDENT0:IDENT0 + P]
        icorr = small[:, ICORR0:ICORR0 + SEQ]
        iout = [small[:, IOUT0 + SEQ * j:IOUT0 + SEQ * (j + 1)] for j in range(2)]
        ones_bd = small[:, ONES0:ONES0 + 2 * HD]
        half, eps = small[:, HALF0:HALF0 + 1], small[:, EPS0:EPS0 + 1]
        bq_all = sb("bq_all", [P, D])
        bkv_all = sb("bkv_all", [P, 2 * KVW])
        bo_all = sb("bo_all", [P, D])
        gamma_all = sb("gamma_all", [P, D])
        beta_all = sb("beta_all", [P, D])
        wq_h, wq_l = sb("wq_h", [P, DC * D], F32R), sb("wq_l", [P, DC * D], F32R)
        wkv_h, wkv_l = sb("wkv_h", [P, DC * 2 * KVW], F32R), sb("wkv_l", [P, DC * 2 * KVW], F32R)
        wo_h, wo_l = sb("wo_h", [P, DC * D], F32R), sb("wo_l", [P, DC * D], F32R)
        rt_h, rt_l = sb("rt_h", [P, DC * D], F32R), sb("rt_l", [P, DC * D], F32R)
        gate_h, gate_l = sb("gate_h", [P, DC * EXPERTS], F32R), sb("gate_l", [P, DC * EXPERTS], F32R)
        with ExitStack() as tmp:
            w0_raw = sb("w0_raw", [P, DC, D], stack=tmp)
            a_raw = sb("a_raw", [P, D], stack=tmp)
            b_raw = sb("b_raw", [P, DC, P], stack=tmp)
            b_t = sb("b_t", [P, D], stack=tmp)
            ex_raw = sb("ex_raw", [P, 2, LAT], stack=tmp)
            ex_t = sb("ex_t", [P, 2, LAT], stack=tmp)
            fc2_raw = sb("fc2_raw", [P, 2, D], stack=tmp)
            ex_fc2 = sb("ex_fc2", [P, 2, D], stack=tmp)
            fc1_raw = sb("fc1_raw", [P, DC, LAT], stack=tmp)
            fc1_t = w0_raw[:, 0:2, :]
            gate_raw = sb("gate_raw", [P, DC * EXPERTS], stack=tmp)
        up_h, up_l = sb("up_h", [P, DC * INNER], F32R), sb("up_l", [P, DC * INNER], F32R)

        pass1 = ExitStack()
        one = lambda name, shape, dt=F32: sb(name, shape, dt, pass1)
        stage = [one(f"stage{i}", [P, 2048]) for i in range(1)]
        dft_h, dft_l = one("dft_h", [P, DFT], F32R), one("dft_l", [P, DFT], F32R)
        w0_h, w0_l = one("w0_h", [P, DC * D], F32R), one("w0_l", [P, DC * D], F32R)
        b0_all = one("b0_all", [P, D])
        coef = one("coef", [P, 1])
        x_in, ctx_t = one("x_in", [P, D]), one("ctx_t", [P, D])
        xn1 = one("xn1", [P, D])
        x_h, x_l = one("x_h", [P, D], F32R), one("x_l", [P, D], F32R)
        c_h, c_l = one("c_h", [P, D], F32R), one("c_l", [P, D], F32R)
        qf = one("qf", [P, 2, D])
        prod = one("prod", [P, 2, D])
        m8 = one("m8", [P, 2 * DC, TOP])
        kept_not = one("kept_not", [P, 2 * DC, SEQ])
        shifted = one("shifted", [P, 2 * DC, SEQ + TOP])
        total, total_inv = one("total", [P, 2 * DC]), one("total_inv", [P, 2 * DC])
        wgt = one("wgt", [P, 2 * DC * SEQ])
        wt_h, wt_l = one("wt_h", [P, D], F32R), one("wt_l", [P, D], F32R)
        vf = one("vf", [P, 2, 2, D])
        prod2 = one("prod2", [P, 2, 2, D])
        x_res, x1 = one("x_res", [P, D]), one("x1", [P, D])
        x1b = one("x1b", [P, D])
        xn2 = one("xn2", [P, D])
        x1t_h, x1t_l = one("x1t_h", [P, D], F32R), one("x1t_l", [P, D], F32R)
        x2 = one("x2", [P, D])
        bn1, mv1, va1, rs1 = one("bn1", [P, 6]), one("mv1", [P, 2]), one("va1", [P, 1]), one("rs1", [P, 1])
        bn2, mv2, va2, rs2 = one("bn2", [P, 6]), one("mv2", [P, 2]), one("va2", [P, 1]), one("rs2", [P, 1])
        pass1.close()

        down_h, down_l = sb("down_h", [P, IC * D], F32R), sb("down_l", [P, IC * D], F32R)
        xn3, ctx2 = sb("xn3", [P, D]), sb("ctx2", [P, D])
        ct_h, ct_l = sb("ct_h", [P, D], F32R), sb("ct_l", [P, D], F32R)
        xt_h, xt_l = sb("xt_h", [P, D], F32R), sb("xt_l", [P, D], F32R)
        kv_sb, q_sb = sb("kv_sb", [P, 2 * KVW]), sb("q_sb", [P, D])
        qt_h, qt_l = sb("qt_h", [P, D], F32R), sb("qt_l", [P, D], F32R)
        qt_b = sb("qt_b", [P, D], BF16)
        kt_h, kt_l = sb("kt_h", [P, P], F32R), sb("kt_l", [P, P], F32R)
        kbd_h, kbd_l = sb("kbd_h", [P, 2, D], F32R), sb("kbd_l", [P, 2, D], F32R)
        kbd_b = sb("kbd_b", [P, 2, D], BF16)
        gmax = sb("gmax", [P, GROUPS * NKV])
        ngm = sb("ngm", [NKV, GROUPS * P], BF16)
        probs = sb("probs", [P, 2, PAIRS, GROUPS * SEQ])
        stage2 = probs[:].rearrange("p a b c -> p (a b c)")
        vbd = sb("vbd", [P, 2, PAIRS, 2, HD])
        y = sb("y", [P, GROUPS, 2, SEQ])
        y_h, y_l = sb("y_h", [P, D], F32R), sb("y_l", [P, D], F32R)
        x2_res, x3, x3b, x3c, xn4 = (sb(n, [P, D]) for n in ("x2_res", "x3", "x3b", "x3c", "xn4"))
        t4_h, t4_l = sb("t4_h", [P, D], F32R), sb("t4_l", [P, D], F32R)
        lg, rw = sb("lg", [P, TOP]), sb("rw", [P, 1])
        act2 = sb("act2", [P, INNER])
        routed = sb("routed", [P, D])
        ht_h, ht_l = sb("ht_h", [P, D], F32R), sb("ht_l", [P, D], F32R)
        z = sb("z", [P, D])
        bn3, mv3, va3, rs3 = (sb(n, [P, w]) for n, w in (("bn3", 6), ("mv3", 2), ("va3", 1), ("rs3", 1)))
        bn4, mv4, va4, rs4 = (sb(n, [P, w]) for n, w in (("bn4", 6), ("mv4", 2), ("va4", 1), ("rs4", 1)))
        bn5, mv5, va5, rs5 = (sb(n, [P, w]) for n, w in (("bn5", 6), ("mv5", 2), ("va5", 1), ("rs5", 1)))

        SEMS = """stage2_in stage2_hi stage2_lo vbd_zero
            tile_loaded ctx2_loaded res2_loaded out_stored
            bn3_s mv3_s va3_s rs3_s xn3_s bn4_s mv4_s va4_s rs4_s xn4_s bn5_s mv5_s va5_s rs5_s zn_s
            ct_ps ct_hi ct_lo kv_ps kv_s qx_ps qx_hi qx_lo qy_ps q_s
            qkt_ps kt_hi kt_lo qt_hi qt_lo qt_bs kbd_s vbd_s g_ps gmax_s gmt_ps ngm_s s_ps probs_s
            pv_ps den_s y_s y_hi y_lo wo_ps x2b_s x3_s x3b_s x3c_s
            t4_ps t4_hi t4_lo u_ps relu_s h_s gate_ps lg_s rw_s rt_out_ps routed_s
            ht_ps ht_hi ht_lo dn_ps z_s zg_s o_s
            const_in merge_in lora_in bcast_in stage_in dft_hi dft_lo sel_ready gate_split
            bt_ps coef_ready bt_ready ext_ps ext_ready ef_ps ef_ready w0_ps w0_hi w0_lo rt_ps rt_hi rt_lo
            fct_ps fct_ready stage_hi stage_lo
            x_loaded ctx_loaded res_loaded bn1_s mv1_s va1_s rs1_s xn1_s x_hi x_lo c_hi c_lo
            q_ps qf_s k_ps prod_s v_ps vf_s corr_ps tops_s rep_s shift_s exp_s mask_s sum_s inv_s wgt_s
            wt_ps wt_hi wt_lo wf_ps prod2_s o_ps x1_s bn2_s mv2_s va2_s rs2_s xn2_s x1b_s
            xt_ps xt_hi xt_lo ffn_ps x2_s x2_stored""".split()
        S = {name: sem(name) for name in SEMS}

        block = ctx.enter_context(nc.Block())

        def rows(dram, t):
            return dram[bass.ts(t, P), :]

        LEAD = 3

        def pass1_loop(eng, body, peeled):
            for i in range(-LEAD, 1):
                body(i)
                peeled(i)
            with eng.Fori(1, NT - LEAD) as i:
                body(i)
            for i in range(NT - LEAD, NT):
                body(i)
                peeled(i)

        def live(t):
            return not isinstance(t, int) or 0 <= t < NT

        def min_tiles(n, t):
            return n * (min(t, NT) if isinstance(t, int) else t)

        LEAD2 = 4

        def pass2_loop(eng, body, peeled):
            for i in range(-LEAD2, 2):
                peeled(i)
                body(i)
            with eng.Fori(2, NT - LEAD2) as i:
                body(i)
            for i in range(NT - LEAD2, NT + 1):
                body(i)

        wo_v = wo.rearrange("(h g d) n -> h d g n", h=NKV, g=GROUPS)
        up_v = up_w.rearrange("(c p) n -> p c n", p=P)
        down_v = down_w.rearrange("(c p) n -> p c n", p=P)
        stage3 = stage[0][:].rearrange("p (c n) -> p c n", c=DC)
        stage_kv = stage[0][:, 0:DC * 2 * KVW].rearrange("p (c n) -> p c n", c=DC)
        stage_up = stage[0][:].rearrange("p (c n) -> p c n", c=2)
        half_up = DC * INNER // 2
        WEIGHTS = {
            -1: ([(stage3, wq.rearrange("(c p) n -> p c n", p=P))], wq_h[:], wq_l[:]),
            0: ([(stage3[HD * h:HD * (h + 1)], wo_v[h]) for h in range(NKV)], wo_h[:], wo_l[:]),
            NT - 3: ([(stage_kv[:, :, 0:KVW], wk.rearrange("(c p) n -> p c n", p=P)),
                      (stage_kv[:, :, KVW:2 * KVW], wv.rearrange("(c p) n -> p c n", p=P))], wkv_h[:], wkv_l[:]),
            NT - 2: ([(stage_up, up_v[:, 0:2, :])], up_h[:, 0:half_up], up_l[:, 0:half_up]),
            NT - 1: ([(stage_up, up_v[:, 2:4, :])], up_h[:, half_up:], up_l[:, half_up:]),
        }
        STAGED = {i: n + 1 for n, i in enumerate(WEIGHTS)}
        LANDED = {i: 16 * sum(len(w[0]) for k, w in WEIGHTS.items() if k <= i) for i in WEIGHTS}
        MERGES = 16 * (2 + DC + ADAPT)

        @block.sync
        def _(sp):
            sp.dma_start(small[:], small_in).then_inc(S["const_in"], 16)
            sp.dma_start(stage[0][:, 0:DFT], dft_in).then_inc(S["const_in"], 16)

            def body(i):
                t = i + 3
                if live(t):
                    wait(sp, S["xn1_s"], t)
                    sp.dma_start(x_in[:], rows(x_rows, t)).then_inc(S["x_loaded"], 16)
                    wait(sp, S["c_lo"], t)
                    sp.dma_start(ctx_t[:], rows(ctx_rows, t)).then_inc(S["ctx_loaded"], 16)
                t = i + 1
                if live(t):
                    wait(sp, S["x1_s"], t)
                    sp.dma_start(x_res[:], rows(x_rows, t)).then_inc(S["res_loaded"], 16)
                t = i
                if live(t):
                    sp.wait_ge(S["x2_s"], t + 1)
                    sp.dma_start(rows(x2_rows, t), x2[:]).then_inc(S["x2_stored"], 16)

            def peeled(i):
                if i == -3:
                    sp.dma_start(w0_raw[:], w0.rearrange("(c p) d -> p c d", p=P)).then_inc(S["lora_in"], 16)
                    sp.dma_start(a_raw[:], lora_a.rearrange("n r d -> (n r) d")).then_inc(S["lora_in"], 16)
                    for c in range(DC):
                        sp.dma_start(b_raw[:, c, :].rearrange("p (n r) -> p n r", n=ADAPT),
                                     lora_b[:, c * P:(c + 1) * P, :].rearrange("n o r -> o n r")
                                     ).then_inc(S["lora_in"], 16)
                    for n in range(ADAPT):
                        sp.dma_start(coef[n * RANK:(n + 1) * RANK, :],
                                     lora_w[n:n + 1].rearrange("(a b) -> a b", a=1).to_broadcast([RANK, 1])
                                     ).then_inc(S["lora_in"], 16)
                    sp.dma_start(b0_all[:], b0.rearrange("(a n) -> a n", a=1).to_broadcast([P, D])
                                 ).then_inc(S["bcast_in"], 16)
                if i == -2:
                    sp.dma_start(ex_raw[:], expert_w.rearrange("(c p) n -> p c n", p=P)).then_inc(S["merge_in"], 16)
                    sp.dma_start(fc2_raw[:], fc2_w.rearrange("(c p) n -> p c n", p=P)).then_inc(S["merge_in"], 16)
                    sp.dma_start(fc1_raw[:], fc1_w.rearrange("(c p) n -> p c n", p=P)).then_inc(S["merge_in"], 16)
                    sp.dma_start(gate_raw[:].rearrange("p (c n) -> p c n", c=DC),
                                 gate_w.rearrange("(c p) n -> p c n", p=P)).then_inc(S["merge_in"], 16)
                    for tile, dram in ((bq_all[:], bq), (bkv_all[:, 0:KVW], bk), (bkv_all[:, KVW:2 * KVW], bv),
                                       (bo_all[:], bo), (gamma_all[:], gamma), (beta_all[:], beta)):
                        sp.dma_start(tile, dram.rearrange("(a n) -> a n", a=1).to_broadcast([P, tile.shape[1]])
                                     ).then_inc(S["bcast_in"], 16)
                if i in WEIGHTS:
                    sp.wait_ge(S["dft_lo"], 1)
                    wait(sp, S["stage_lo"], STAGED[i] - 1)
                    for tile, dram in WEIGHTS[i][0]:
                        sp.dma_start(tile, dram).then_inc(S["stage_in"], 16)

            pass1_loop(sp, body, peeled)
            sp.wait_ge(S["x2_stored"], 16 * NT)
            sp.wait_ge(S["stage_lo"], len(WEIGHTS))

            def body2(i):
                t = i + 4
                if live(t):
                    wait(sp, S["qx_ps"], t)
                    sp.dma_start(xn3[:], rows(x2_rows, t)).then_inc(S["tile_loaded"], 16)
                    wait(sp, S["ct_ps"], t)
                    sp.dma_start(ctx2[:], rows(ctx_rows, t)).then_inc(S["ctx2_loaded"], 16)
                t = i + 2
                if live(t):
                    wait(sp, S["x3_s"], t)
                    sp.dma_start(x2_res[:], rows(x2_rows, t)).then_inc(S["res2_loaded"], 16)
                t = i - 1
                if live(t):
                    sp.wait_ge(S["o_s"], t + 1)
                    sp.dma_start(rows(out_rows, t), z[:]).then_inc(S["out_stored"], 16)

            def peeled2(i):
                if i < 2 - LEAD2:
                    c = i + LEAD2
                    wait(sp, S["stage2_lo"], c)
                    sp.dma_start(stage2.rearrange("p (c n) -> p c n", c=DC), down_v[:, DC * c:DC * (c + 1), :]
                                 ).then_inc(S["stage2_in"], 16)

            pass2_loop(sp, body2, peeled2)
            sp.wait_ge(S["out_stored"], 16 * NT)

        @block.scalar
        def _(act):
            act.wait_ge(S["const_in"], 32)
            act.activation(dft_h[:], stage[0][:, 0:DFT], ACT.Copy).then_inc(S["dft_hi"], 1)
            act.activation(selb[:], small[0:NKV, SEL0:SEL0 + PAIRS * P], ACT.Copy).then_inc(S["sel_ready"], 1)

            def body(i):
                t = i + 1
                if live(t):
                    act.wait_ge(S["wt_ps"], t + 1)
                    wait(act, S["wf_ps"], 4 * t)
                    act.activation(wt_h[:], bank[5][:], ACT.Copy).then_inc(S["wt_hi"], 1)
                t = i + 2
                if live(t):
                    wait(act, S["prod_s"], 2 * t)
                    for b in range(2):
                        act.wait_ge(S["q_ps"], 2 * t + b + 1)
                        act.activation(qf[:, b, :], bank[2 * b][:], ACT.Copy).then_inc(S["qf_s"], 1)
                t = i
                if live(t):
                    act.wait_ge(S["xt_ps"], t + 1)
                    wait(act, S["ffn_ps"], t)
                    act.activation(x1t_h[:], bank[6][:], ACT.Copy).then_inc(S["xt_hi"], 1)
                t = i + 2
                if live(t):
                    wait(act, S["prod2_s"], 4 * t)
                    for n in range(4):
                        act.wait_ge(S["v_ps"], 4 * t + n + 1)
                        act.activation(vf[:, n // 2, n % 2, :], bank[n][:], ACT.Copy).then_inc(S["vf_s"], 1)
                    act.wait_ge(S["shift_s"], t + 1)
                    act.activation(shifted[:], shifted[:], ACT.Exp).then_inc(S["exp_s"], 1)
                t = i + 3
                if live(t):
                    act.wait_ge(S["ctx_loaded"], 16 * (t + 1))
                    wait(act, S["v_ps"], 4 * t)
                    act.activation(c_h[:], ctx_t[:], ACT.Copy).then_inc(S["c_hi"], 1)
                    act.wait_ge(S["xn1_s"], t + 1)
                    wait(act, S["q_ps"], 2 * t)
                    act.activation(x_h[:], xn1[:], ACT.Copy).then_inc(S["x_hi"], 1)

            def peeled(i):
                if i == -2:
                    for c in range(DC):
                        act.wait_ge(S["w0_ps"], c + 1)
                        act.activation(w0_h[:, c * D:(c + 1) * D], bank[6 + c % 2][:], ACT.Copy
                                       ).then_inc(S["w0_hi"], 1)
                if i == -1:
                    act.wait_ge(S["merge_in"], 64)
                    act.activation(gate_h[:], gate_raw[:], ACT.Copy).then_inc(S["gate_split"], 1)
                    act.wait_ge(S["ext_ps"], 1)
                    act.activation(ex_t[:].rearrange("p a b -> p (a b)"), bank[7][:], ACT.Copy).then_inc(S["ext_ready"], 1)
                    for c in range(2):
                        act.wait_ge(S["ef_ps"], c + 1)
                        act.activation(ex_fc2[:, c, :], bank[6 + c][:], ACT.Copy).then_inc(S["ef_ready"], 1)
                    for c in range(2):
                        act.wait_ge(S["fct_ps"], c + 1)
                        act.activation(fc1_t[:, c, :], bank[6 + c][:], ACT.Copy).then_inc(S["fct_ready"], 1)
                if i == 0:
                    for c in range(DC):
                        act.wait_ge(S["rt_ps"], c + 1)
                        act.activation(rt_h[:, c * D:(c + 1) * D], bank[6 + c % 2][:], ACT.Copy
                                       ).then_inc(S["rt_hi"], 1)
                if i in WEIGHTS:
                    act.wait_ge(S["stage_in"], LANDED[i])
                    if i > 0:
                        act.wait_ge(S["rt_lo"], DC)
                    target = WEIGHTS[i][1]
                    act.activation(target, stage[0][:, 0:target.shape[1]], ACT.Copy).then_inc(S["stage_hi"], 1)

            pass1_loop(act, body, peeled)
            act.wait_ge(S["x2_stored"], 16 * NT)

            def body2(i):
                t = i + 3
                if live(t):
                    act.wait_ge(S["qkt_ps"], t + 1)
                    wait(act, S["kbd_s"], 6 * t)
                    act.activation(kt_h[:], bank[1][:, 0:P], ACT.Copy).then_inc(S["kt_hi"], 1)
                    wait(act, S["s_ps"], 2 * t)
                    act.activation(qt_h[:], bank[0][:], ACT.Copy).then_inc(S["qt_hi"], 1)
                    wait(act, S["g_ps"], 4 * t)
                    act.activation(qt_b[:], bank[0][:], ACT.Copy).then_inc(S["qt_bs"], 1)
                t = i + 1
                if live(t):
                    act.wait_ge(S["t4_ps"], t + 1)
                    wait(act, S["rt_out_ps"], t)
                    act.activation(t4_h[:], bank[4][:], ACT.Copy).then_inc(S["t4_hi"], 1)
                t = i
                if live(t):
                    act.wait_ge(S["ht_ps"], 2 * t + 1)
                    wait(act, S["dn_ps"], 2 * t)
                    act.activation(ht_h[:], bank[5][:], ACT.Copy).then_inc(S["ht_hi"], 1)
                    wait(act, S["o_s"], t)
                    act.wait_ge(S["x3b_s"], t + 1)
                    act.activation(x3c[:], x3b[:], ACT.Copy).then_inc(S["x3c_s"], 1)
                t = i + 4
                if live(t):
                    act.wait_ge(S["ct_ps"], t + 1)
                    wait(act, S["kv_ps"], t)
                    act.activation(ct_h[:], bank[7][:], ACT.Copy).then_inc(S["ct_hi"], 1)
                t = i + 2
                if live(t):
                    act.wait_ge(S["y_s"], 2 * t + 2)
                    wait(act, S["wo_ps"], t)
                    act.activation(y_h[:], y[:].rearrange("p g b q -> p (g b q)"), ACT.Copy).then_inc(S["y_hi"], 1)
                t = i + 1
                if live(t):
                    wait(act, S["ht_ps"], 2 * t)
                    for c in range(2):
                        act.wait_ge(S["u_ps"], 2 * t + c + 1)
                        act.activation(act2[:, c * D:(c + 1) * D], bank[6 + c][:], ACT.Relu).then_inc(S["relu_s"], 1)
                t = i
                if live(t):
                    act.wait_ge(S["ht_ps"], 2 * t + 2)
                    act.wait_ge(S["dn_ps"], 2 * t + 1)
                    act.activation(ht_h[:], bank[5][:], ACT.Copy).then_inc(S["ht_hi"], 1)
                t = i + 4
                if live(t):
                    act.wait_ge(S["qx_ps"], t + 1)
                    wait(act, S["qy_ps"], t)
                    act.activation(xt_h[:], bank[5][:], ACT.Copy).then_inc(S["qx_hi"], 1)
                t = i + 3
                if live(t):
                    act.wait_ge(S["gmt_ps"], t + 1)
                    wait(act, S["s_ps"], 2 * t)
                    act.activation(ngm[:], bank[1][0:NKV, :], ACT.Copy, scale=-1.0).then_inc(S["ngm_s"], 1)
                    act.wait_ge(S["s_ps"], 2 * t + 1)
                    wait(act, S["pv_ps"], 2 * t)
                    act.activation(probs[:, 0].rearrange("p a b -> p (a b)"), wide[:], ACT.Exp, scale=HD ** -0.5
                                   ).then_inc(S["probs_s"], 1)
                t = i + 1
                if live(t):
                    act.wait_ge(S["rt_out_ps"], t + 1)
                    act.wait_ge(S["rw_s"], t + 1)
                    wait(act, S["z_s"], t)
                    act.activation(routed[:], bank[4][:], ACT.Copy, scale=rw[:]).then_inc(S["routed_s"], 1)
                t = i + 3
                if live(t):
                    act.wait_ge(S["s_ps"], 2 * t + 2)
                    act.activation(probs[:, 1].rearrange("p a b -> p (a b)"), wide[:], ACT.Exp, scale=HD ** -0.5
                                   ).then_inc(S["probs_s"], 1)

            def peeled2(i):
                if i < 2 - LEAD2:
                    c = i + LEAD2
                    act.wait_ge(S["stage2_in"], 16 * (c + 1))
                    act.activation(down_h[:, DC * D * c:DC * D * (c + 1)], stage2, ACT.Copy).then_inc(S["stage2_hi"], 1)

            pass2_loop(act, body2, peeled2)

        @block.gpsimd
        def _(pool):
            def body(i):
                t = i + 1
                if live(t):
                    pool.wait_ge(S["x1_s"], t + 1)
                    wait(pool, S["x2_s"], t)
                    pool.tensor_tensor(x1b[:], x1[:], b0_all[:], ALU.add).then_inc(S["x1b_s"], 1)
                    pool.wait_ge(S["mv2_s"], t + 1)
                    pool.tensor_tensor(va2[:], mv2[:, 1:2], eps, ALU.add).then_inc(S["va2_s"], 1)
                    pool.wait_ge(S["va2_s"], t + 1)
                    pool.tensor_tensor(rs2[:], va2[:], half, ALU.pow).then_inc(S["rs2_s"], 1)
                t = i + 2
                if live(t):
                    pool.wait_ge(S["inv_s"], t + 1)
                    wait(pool, S["wt_ps"], t)
                    pool.tensor_tensor(wgt[:].rearrange("p (c s) -> p c s", s=SEQ), kept_not[:],
                                       total_inv[:].unsqueeze(2).to_broadcast([P, 2 * DC, SEQ]), ALU.mult
                                       ).then_inc(S["wgt_s"], 1)
                t = i + 3
                if live(t):
                    pool.wait_ge(S["c_hi"], t + 1)
                    wait(pool, S["v_ps"], 4 * t)
                    pool.tensor_tensor(c_l[:], ctx_t[:], c_h[:].bitcast(F32), ALU.subtract).then_inc(S["c_lo"], 1)
                    pool.wait_ge(S["mv1_s"], t + 1)
                    pool.tensor_tensor(va1[:], mv1[:, 1:2], eps, ALU.add).then_inc(S["va1_s"], 1)
                    pool.wait_ge(S["va1_s"], t + 1)
                    pool.tensor_tensor(rs1[:], va1[:], half, ALU.pow).then_inc(S["rs1_s"], 1)
                    pool.wait_ge(S["x_hi"], t + 1)
                    wait(pool, S["q_ps"], 2 * t)
                    pool.tensor_tensor(x_l[:], xn1[:], x_h[:].bitcast(F32), ALU.subtract).then_inc(S["x_lo"], 1)

            def peeled(i):
                if i in WEIGHTS:
                    pool.wait_ge(S["stage_hi"], STAGED[i])
                    hi, lo = WEIGHTS[i][1:]
                    pool.tensor_tensor(lo, stage[0][:, 0:lo.shape[1]], hi.bitcast(F32), ALU.subtract
                                       ).then_inc(S["stage_lo"], 1)

            pass1_loop(pool, body, peeled)
            pool.wait_ge(S["x2_stored"], 16 * NT)

            def rstd(t, mv, var, rs, n):
                pool.wait_ge(S[f"mv{n}_s"], t + 1)
                pool.tensor_tensor(var[:], mv[:, 1:2], eps, ALU.add).then_inc(S[f"va{n}_s"], 1)
                pool.wait_ge(S[f"va{n}_s"], t + 1)
                pool.tensor_tensor(rs[:], var[:], half, ALU.pow).then_inc(S[f"rs{n}_s"], 1)

            heads = small[:, HEAD0:HEAD0 + NKV].unsqueeze(2).to_broadcast([P, NKV, SEQ])

            def body2(i):
                t = i - 1
                if live(t):
                    pool.wait_ge(S["zn_s"], t + 1)
                    pool.tensor_tensor(z[:], z[:], gamma_all[:], ALU.mult).then_inc(S["zg_s"], 1)
                    pool.wait_ge(S["zg_s"], t + 1)
                    pool.wait_ge(S["x3c_s"], t + 1)
                    pool.tensor_tensor(z[:], z[:], x3c[:], ALU.add).then_inc(S["o_s"], 1)
                t = i + 1
                if live(t):
                    pool.wait_ge(S["x3_s"], t + 1)
                    wait(pool, S["x3c_s"], t)
                    pool.tensor_tensor(x3b[:], x3[:], beta_all[:], ALU.add).then_inc(S["x3b_s"], 1)
                t = i + 3
                if live(t):
                    def spread(out, kt, b):
                        k = kt[:, SEQ * b:SEQ * (b + 1)].bitcast(F32).unsqueeze(1).to_broadcast([P, NKV, SEQ])
                        pool.tensor_tensor(out[:, b, :].rearrange("p (h k) -> p h k", h=NKV), k, heads, ALU.mult
                                           ).then_inc(S["kbd_s"], 1)

                    pool.wait_ge(S["kt_hi"], t + 1)
                    wait(pool, S["g_ps"], 4 * t)
                    spread(kbd_b, kt_h, 0)
                    spread(kbd_b, kt_h, 1)
                    wait(pool, S["s_ps"], 2 * t)
                    spread(kbd_h, kt_h, 0)
                    spread(kbd_h, kt_h, 1)
                    pool.wait_ge(S["kt_lo"], t + 1)
                    spread(kbd_l, kt_l, 0)
                    spread(kbd_l, kt_l, 1)
                t = i + 2
                if live(t):
                    pool.wait_ge(S["res2_loaded"], 16 * (t + 1))
                    pool.tensor_tensor(x2_res[:], x2_res[:], bo_all[:], ALU.add).then_inc(S["x2b_s"], 1)
                    pool.wait_ge(S["y_hi"], t + 1)
                    wait(pool, S["wo_ps"], t)
                    pool.tensor_tensor(y_l[:], y[:].rearrange("p g b q -> p (g b q)"), y_h[:].bitcast(F32),
                                       ALU.subtract).then_inc(S["y_lo"], 1)
                t = i + 4
                if live(t):
                    rstd(t, mv3, va3, rs3, 3)
                t = i + 2
                if live(t):
                    rstd(t, mv4, va4, rs4, 4)
                t = i + 1
                if live(t):
                    pool.wait_ge(S["relu_s"], 2 * t + 2)
                    pool.tensor_tensor(act2[:], act2[:], act2[:], ALU.mult).then_inc(S["h_s"], 1)
                t = i
                if live(t):
                    rstd(t, mv5, va5, rs5, 5)

            def peeled2(i):
                if i < 2 - LEAD2:
                    c = i + LEAD2
                    part = slice(DC * D * c, DC * D * (c + 1))
                    pool.wait_ge(S["stage2_hi"], c + 1)
                    pool.tensor_tensor(down_l[:, part], stage2, down_h[:, part].bitcast(F32), ALU.subtract
                                       ).then_inc(S["stage2_lo"], 1)

            pass2_loop(pool, body2, peeled2)


        def wait_alone(eng, sem, value, done, times):
            value = value if isinstance(value, int) else eng.snap(eng.to_reg(value))
            eng.wait_ge(done, times)
            wait(eng, sem, value)

        @block.vector
        def _(dve):
            dve.wait_ge(S["dft_hi"], 1)
            dve.tensor_tensor(dft_l[:], stage[0][:, 0:DFT], dft_h[:].bitcast(F32), ALU.subtract
                              ).then_inc(S["dft_lo"], 1)

            def body(i):
                t = i + 1
                if live(t):
                    dve.wait_ge(S["wt_hi"], t + 1)
                    wait(dve, S["wf_ps"], 4 * t)
                    dve.tensor_tensor(wt_l[:], bank[5][:], wt_h[:].bitcast(F32), ALU.subtract
                                      ).then_inc(S["wt_lo"], 1)
                t = i + 2
                if live(t):
                    wait(dve, S["corr_ps"], t)
                    for b in range(2):
                        dve.wait_ge(S["k_ps"], 2 * t + b + 1)
                        dve.wait_ge(S["qf_s"], 2 * t + b + 1)
                        dve.tensor_tensor(prod[:, b, :], bank[2 * b + 1][:], qf[:, b, :], ALU.mult
                                          ).then_inc(S["prod_s"], 1)
                t = i
                if live(t):
                    dve.wait_ge(S["xt_hi"], t + 1)
                    wait(dve, S["ffn_ps"], t)
                    dve.tensor_tensor(x1t_l[:], bank[6][:], x1t_h[:].bitcast(F32), ALU.subtract
                                      ).then_inc(S["xt_lo"], 1)
                t = i + 1
                if live(t):
                    wait(dve, S["o_ps"], t)
                    dve.wait_ge(S["vf_s"], 4 * t + 4)
                    for n in range(4):
                        dve.wait_ge(S["wf_ps"], 4 * t + n + 1)
                        dve.tensor_tensor(prod2[:, n // 2, n % 2, :], bank[n][:], vf[:, n // 2, n % 2, :],
                                          ALU.mult).then_inc(S["prod2_s"], 1)
                t = i + 2
                if live(t):
                    corr = bank[4][:].rearrange("p (c s) -> p c s", s=SEQ)
                    wait_alone(dve, S["corr_ps"], t + 1, S["dft_lo"], 1)
                    for c in range(2 * DC):
                        top = dve.max(m8[:, c, :], corr[:, c, :])
                    top.then_inc(S["tops_s"], 1)
                    wait(dve, S["wgt_s"], t)
                    dve.wait_ge(S["tops_s"], t + 1)
                    best = m8[:, :, 0:1]
                    dve.tensor_tensor(shifted[:, :, 0:SEQ], corr, best.to_broadcast([P, 2 * DC, SEQ]),
                                      ALU.subtract)
                    dve.tensor_tensor(shifted[:, :, SEQ:SEQ + TOP], m8[:], best.to_broadcast([P, 2 * DC, TOP]),
                                      ALU.subtract).then_inc(S["shift_s"], 1)
                    for c in range(2 * DC):
                        rep = dve.match_replace(kept_not[:, c, :], m8[:, c, :], corr[:, c, :], REMOVED)
                    rep.then_inc(S["rep_s"], 1)
                t = i
                if live(t):
                    dve.wait_ge(S["ffn_ps"], t + 1)
                    dve.wait_ge(S["x1b_s"], t + 1)
                    wait(dve, S["x2_stored"], 16 * t)
                    dve.tensor_tensor(x2[:], bank[7][:], x1b[:], ALU.add).then_inc(S["x2_s"], 1)
                t = i + 2
                if live(t):
                    dve.wait_ge(S["exp_s"], t + 1)
                    dve.wait_ge(S["rep_s"], t + 1)
                    dve.scalar_tensor_tensor(kept_not[:], kept_not[:], REMOVED_BELOW, shifted[:, :, 0:SEQ],
                                             ALU.is_lt, ALU.mult).then_inc(S["mask_s"], 1)
                    dve.tensor_reduce(total[:], shifted[:, :, SEQ:SEQ + TOP], AX.X, ALU.add).then_inc(S["sum_s"], 1)
                    dve.wait_ge(S["sum_s"], t + 1)
                    wait(dve, S["wgt_s"], t)
                    dve.reciprocal(total_inv[:], total[:]).then_inc(S["inv_s"], 1)
                t = i + 1
                if live(t):
                    dve.wait_ge(S["o_ps"], t + 1)
                    dve.wait_ge(S["res_loaded"], 16 * (t + 1))
                    wait(dve, S["x1b_s"], t)
                    dve.tensor_tensor(x1[:], bank[4][:], x_res[:], ALU.add).then_inc(S["x1_s"], 1)
                    dve.wait_ge(S["x1_s"], t + 1)
                    dve.bn_stats(bn2[:], x1[:]).then_inc(S["bn2_s"], 1)
                    wait_alone(dve, S["bn2_s"], t + 1, S["dft_lo"], 1)
                    dve.bn_aggr(mv2[:], bn2[:]).then_inc(S["mv2_s"], 1)
                t = i + 3
                if live(t):
                    dve.wait_ge(S["x_loaded"], 16 * (t + 1))
                    dve.bn_stats(bn1[:], x_in[:]).then_inc(S["bn1_s"], 1)
                    wait_alone(dve, S["bn1_s"], t + 1, S["dft_lo"], 1)
                    dve.bn_aggr(mv1[:], bn1[:]).then_inc(S["mv1_s"], 1)
                t = i + 1
                if live(t):
                    dve.wait_ge(S["rs2_s"], t + 1)
                    wait(dve, S["xt_ps"], t)
                    dve.tensor_scalar(xn2[:], x1[:], mv2[:, 0:1], rs2[:], ALU.subtract, ALU.mult
                                      ).then_inc(S["xn2_s"], 1)
                t = i + 3
                if live(t):
                    dve.wait_ge(S["rs1_s"], t + 1)
                    wait(dve, S["x_lo"], t)
                    dve.tensor_scalar(xn1[:], x_in[:], mv1[:, 0:1], rs1[:], ALU.subtract, ALU.mult
                                      ).then_inc(S["xn1_s"], 1)

            def peeled(i):
                if i == -2:
                    dve.wait_ge(S["bt_ps"], 1)
                    dve.tensor_scalar(b_t[:], bank[6][:], coef[:], LORA_SCALE, ALU.mult, ALU.mult
                                      ).then_inc(S["bt_ready"], 1)
                    for c in range(DC):
                        dve.wait_ge(S["w0_hi"], c + 1)
                        dve.tensor_tensor(w0_l[:, c * D:(c + 1) * D], bank[6 + c % 2][:],
                                          w0_h[:, c * D:(c + 1) * D].bitcast(F32), ALU.subtract
                                          ).then_inc(S["w0_lo"], 1)
                if i == -1:
                    dve.wait_ge(S["gate_split"], 1)
                    dve.tensor_tensor(gate_l[:], gate_raw[:], gate_h[:].bitcast(F32), ALU.subtract
                                      ).then_inc(S["gate_split"], 1)
                if i == 0:
                    for c in range(DC):
                        dve.wait_ge(S["rt_hi"], c + 1)
                        dve.tensor_tensor(rt_l[:, c * D:(c + 1) * D], bank[6 + c % 2][:],
                                          rt_h[:, c * D:(c + 1) * D].bitcast(F32), ALU.subtract
                                          ).then_inc(S["rt_lo"], 1)

            pass1_loop(dve, body, peeled)
            dve.wait_ge(S["x2_stored"], 16 * NT)
            dve.wait_ge(S["bcast_in"], 16 * 7)
            dve.memset(vbd[:], 0.0).then_inc(S["vbd_zero"], 1)
            dve.wait_ge(S["vbd_zero"], 1)

            def body2(i):
                t = i + 3
                if live(t):
                    dve.wait_ge(S["kt_hi"], t + 1)
                    wait(dve, S["kbd_s"], 6 * t)
                    dve.tensor_tensor(kt_l[:], bank[1][:, 0:P], kt_h[:].bitcast(F32), ALU.subtract).then_inc(S["kt_lo"], 1)
                    dve.wait_ge(S["qt_bs"], t + 1)
                    wait(dve, S["s_ps"], 2 * t)
                    dve.tensor_tensor(qt_l[:], bank[0][:], qt_h[:].bitcast(F32), ALU.subtract).then_inc(S["qt_lo"], 1)
                    wait(dve, S["pv_ps"], 2 * t)
                    dve.wait_ge(S["kv_s"], t + 1)
                    for b in range(2):
                        for h in range(2):
                            v = kv_sb[SEQ * b:SEQ * (b + 1), KVW:2 * KVW].rearrange("k (p h d) -> k p h d", p=PAIRS, h=2)
                            last = dve.tensor_copy(vbd[SEQ * h:SEQ * (h + 1), b, :, h, :], v[:, :, h, :])
                    last.then_inc(S["vbd_s"], 1)
                t = i + 1
                if live(t):
                    dve.wait_ge(S["t4_hi"], t + 1)
                    wait(dve, S["rt_out_ps"], t)
                    dve.tensor_tensor(t4_l[:], bank[4][:], t4_h[:].bitcast(F32), ALU.subtract).then_inc(S["t4_lo"], 1)
                t = i
                if live(t):
                    dve.wait_ge(S["ht_hi"], 2 * t + 1)
                    wait(dve, S["dn_ps"], 2 * t)
                    dve.tensor_tensor(ht_l[:], bank[5][:], ht_h[:].bitcast(F32), ALU.subtract).then_inc(S["ht_lo"], 1)
                t = i + 4
                if live(t):
                    dve.wait_ge(S["ct_hi"], t + 1)
                    wait(dve, S["kv_ps"], t)
                    dve.tensor_tensor(ct_l[:], bank[7][:], ct_h[:].bitcast(F32), ALU.subtract).then_inc(S["ct_lo"], 1)
                    dve.wait_ge(S["tile_loaded"], 16 * (t + 1))
                    dve.bn_stats(bn3[:], xn3[:]).then_inc(S["bn3_s"], 1)
                    wait_alone(dve, S["bn3_s"], t + 1, S["dft_lo"], 1)
                    dve.bn_aggr(mv3[:], bn3[:]).then_inc(S["mv3_s"], 1)
                t = i + 2
                if live(t):
                    wait(dve, S["y_lo"], t)
                    for b in range(2):
                        part = bank[2 + b][:].rearrange("p (n g q) -> p n g q", n=2, g=GROUPS)
                        dve.wait_ge(S["pv_ps"], 2 * t + b + 1)
                        dve.reciprocal(y[:, :, b, :], part[:, 1]).then_inc(S["den_s"], 1)
                        dve.wait_ge(S["den_s"], 2 * t + b + 1)
                        dve.tensor_tensor(y[:, :, b, :], part[:, 0], y[:, :, b, :], ALU.mult).then_inc(S["y_s"], 1)
                t = i + 4
                if live(t):
                    dve.wait_ge(S["rs3_s"], t + 1)
                    dve.tensor_scalar(xn3[:], xn3[:], mv3[:, 0:1], rs3[:], ALU.subtract, ALU.mult
                                      ).then_inc(S["xn3_s"], 1)
                t = i + 1
                if live(t):
                    wait_alone(dve, S["gate_ps"], t + 1, S["dft_lo"], 1)
                    dve.max(lg[:], bank[0][:, 0:EXPERTS]).then_inc(S["lg_s"], 1)
                    dve.wait_ge(S["lg_s"], t + 1)
                    wait(dve, S["routed_s"], t)
                    dve.tensor_tensor(rw[:], lg[:, 0:1], lg[:, 1:2], ALU.add).then_inc(S["rw_s"], 1)
                t = i + 2
                if live(t):
                    dve.wait_ge(S["wo_ps"], t + 1)
                    dve.wait_ge(S["x2b_s"], t + 1)
                    wait(dve, S["x3b_s"], t)
                    dve.tensor_tensor(x3[:], bank[2][:], x2_res[:], ALU.add).then_inc(S["x3_s"], 1)
                    dve.wait_ge(S["x3_s"], t + 1)
                    dve.bn_stats(bn4[:], x3[:]).then_inc(S["bn4_s"], 1)
                    wait_alone(dve, S["bn4_s"], t + 1, S["dft_lo"], 1)
                    dve.bn_aggr(mv4[:], bn4[:]).then_inc(S["mv4_s"], 1)
                t = i + 3
                if live(t):
                    wait(dve, S["gmt_ps"], t)
                    for g in range(GROUPS):
                        dve.wait_ge(S["g_ps"], 4 * t + g + 1)
                        dve.tensor_reduce(gmax[:, NKV * g:NKV * (g + 1)],
                                          bank[g % 2][:].rearrange("p (h k) -> p h k", h=NKV), AX.X, ALU.max
                                          ).then_inc(S["gmax_s"], 1)
                t = i + 2
                if live(t):
                    dve.wait_ge(S["rs4_s"], t + 1)
                    wait(dve, S["t4_ps"], t)
                    dve.tensor_scalar(xn4[:], x3[:], mv4[:, 0:1], rs4[:], ALU.subtract, ALU.mult
                                      ).then_inc(S["xn4_s"], 1)
                t = i
                if live(t):
                    dve.wait_ge(S["ht_hi"], 2 * t + 2)
                    dve.wait_ge(S["dn_ps"], 2 * t + 1)
                    dve.tensor_tensor(ht_l[:], bank[5][:], ht_h[:].bitcast(F32), ALU.subtract).then_inc(S["ht_lo"], 1)
                t = i + 4
                if live(t):
                    dve.wait_ge(S["kv_ps"], t + 1)
                    wait(dve, S["qkt_ps"], t)
                    dve.tensor_tensor(kv_sb[:], bank[2][:, 0:2 * KVW], bkv_all[:], ALU.add).then_inc(S["kv_s"], 1)
                    dve.wait_ge(S["qx_hi"], t + 1)
                    wait(dve, S["qy_ps"], t)
                    dve.tensor_tensor(xt_l[:], bank[5][:], xt_h[:].bitcast(F32), ALU.subtract).then_inc(S["qx_lo"], 1)
                t = i
                if live(t):
                    dve.wait_ge(S["dn_ps"], 2 * t + 2)
                    dve.wait_ge(S["routed_s"], t + 1)
                    wait(dve, S["out_stored"], 16 * t)
                    dve.tensor_tensor(z[:], bank[3][:], routed[:], ALU.add).then_inc(S["z_s"], 1)
                    dve.wait_ge(S["z_s"], t + 1)
                    dve.bn_stats(bn5[:], z[:]).then_inc(S["bn5_s"], 1)
                    wait_alone(dve, S["bn5_s"], t + 1, S["dft_lo"], 1)
                    dve.bn_aggr(mv5[:], bn5[:]).then_inc(S["mv5_s"], 1)
                t = i + 4
                if live(t):
                    dve.wait_ge(S["qy_ps"], t + 1)
                    wait(dve, S["qkt_ps"], t)
                    dve.tensor_tensor(q_sb[:].rearrange("p (g h d) -> p h g d", g=GROUPS, h=NKV),
                                      bank[0][:].rearrange("p (h g d) -> p h g d", g=GROUPS, h=NKV),
                                      bq_all[:].rearrange("p (h g d) -> p h g d", g=GROUPS, h=NKV), ALU.add
                                      ).then_inc(S["q_s"], 1)
                t = i
                if live(t):
                    dve.wait_ge(S["rs5_s"], t + 1)
                    dve.tensor_scalar(z[:], z[:], mv5[:, 0:1], rs5[:], ALU.subtract, ALU.mult).then_inc(S["zn_s"], 1)

            pass2_loop(dve, body2, lambda i: None)

        @block.tensor
        def _(pe):
            def split_product(out_ps, w_hi, w_lo, m_hi, m_lo, first, last):
                pe.matmul(out_ps, w_hi, m_hi, start=first, stop=False)
                pe.matmul(out_ps, w_hi, m_lo, start=False, stop=False)
                return pe.matmul(out_ps, w_lo, m_hi, start=False, stop=last)

            pe.wait_ge(S["dft_lo"], 1)

            def body(i):
                t = i + 1
                if live(t):
                    pe.wait_ge(S["wgt_s"], t + 1)
                    wait(pe, S["wt_lo"], t)
                    for c in range(DC):
                        last = pe.transpose(bank[5][:, c * P:(c + 1) * P], wgt[:, c * P:(c + 1) * P], ident)
                    last.then_inc(S["wt_ps"], 1)
                t = i + 2
                if live(t):
                    pe.wait_ge(S["x_lo"], t + 1)
                    pe.wait_ge(S["c_lo"], t + 1)
                    wait(pe, S["vf_s"], 4 * t)
                    for b in range(2):
                        q, k = slice(Q0 + P * b, Q0 + P * b + P), slice(K0 + P * b, K0 + P * b + P)
                        split_product(bank[2 * b][:], dft_h[:, q], dft_l[:, q], x_h[:], x_l[:], True, True
                                      ).then_inc(S["q_ps"], 1)
                        split_product(bank[2 * b + 1][:], dft_h[:, k], dft_l[:, k], c_h[:], c_l[:], True, True
                                      ).then_inc(S["k_ps"], 1)
                t = i
                if live(t):
                    pe.wait_ge(S["xn2_s"], t + 1)
                    wait(pe, S["xt_lo"], t)
                    if isinstance(t, int) and t == 0:
                        pe.wait_ge(S["fct_ready"], 2)
                    elif isinstance(t, int) and t > 1:
                        pe.wait_ge(S["rt_lo"], DC)
                    for c in range(DC):
                        last = pe.transpose(bank[6][:, c * P:(c + 1) * P], xn2[:, c * P:(c + 1) * P], ident)
                    last.then_inc(S["xt_ps"], 1)
                t = i + 1
                if live(t):
                    pe.wait_ge(S["wt_lo"], t + 1)
                    wait(pe, S["prod_s"], min_tiles(2, t + 2))
                    for n in range(4):
                        w = slice(W0 + P * n, W0 + P * n + P)
                        split_product(bank[n][:], dft_h[:, w], dft_l[:, w], wt_h[:], wt_l[:], True, True
                                      ).then_inc(S["wf_ps"], 1)
                t = i
                if live(t):
                    pe.wait_ge(S["xt_lo"], t + 1)
                    wait(pe, S["x2_s"], t)
                    for c in range(DC):
                        k = slice(c * P, (c + 1) * P)
                        n = slice(c * D, (c + 1) * D)
                        last = split_product(bank[7][:], x1t_h[:, k], x1t_l[:, k], w0_h[:, n], w0_l[:, n],
                                             c == 0, c == DC - 1)
                    last.then_inc(S["ffn_ps"], 1)
                t = i + 2
                if live(t):
                    pe.wait_ge(S["prod_s"], 2 * (t + 1))
                    wait(pe, S["x1_s"], t - 1)
                    for c in range(DC):
                        for b in range(2):
                            o = (2 * c + b) * SEQ
                            last = pe.matmul(bank[4][:, o:o + SEQ], prod[:, b, c * P:(c + 1) * P], icorr,
                                             start=True, stop=True)
                    last.then_inc(S["corr_ps"], 1)
                    wait(pe, S["prod2_s"], min_tiles(4, t))
                    for n in range(4):
                        v = slice(V0 + P * n, V0 + P * n + P)
                        split_product(bank[n][:], dft_h[:, v], dft_l[:, v], c_h[:], c_l[:], True, True
                                      ).then_inc(S["v_ps"], 1)
                t = i + 1
                if live(t):
                    pe.wait_ge(S["prod2_s"], 4 * (t + 1))
                    wait(pe, S["rep_s"], min_tiles(1, t + 2))
                    for j in range(2):
                        for b in range(2):
                            last = pe.matmul(bank[4][SEQ * b:SEQ * (b + 1), :], iout[j], prod2[:, b, j, :],
                                             start=(j == 0), stop=(j == 1))
                    last.then_inc(S["o_ps"], 1)

            def peeled(i):
                if i == -3:
                    pe.wait_ge(S["const_in"], 32)
                    pe.wait_ge(S["lora_in"], 16 * (2 + DC + ADAPT))
                    for c in range(DC):
                        last = pe.transpose(bank[6][:, c * P:(c + 1) * P], b_raw[:, c, :], ident)
                    last.then_inc(S["bt_ps"], 1)
                if i == -2:
                    pe.wait_ge(S["bt_ready"], 1)
                    for c in range(DC):
                        if c >= 2:
                            pe.wait_ge(S["w0_lo"], c - 1)
                        ps = bank[6 + c % 2]
                        for o in range(DC):
                            pe.matmul(ps[:, o * P:(o + 1) * P], w0_raw[:, o, c * P:(c + 1) * P], ident,
                                      start=(o == 0), stop=False, skip_group_check=True)
                        pe.matmul(ps[:], a_raw[:, c * P:(c + 1) * P], b_t[:], start=False, stop=True,
                                  skip_group_check=True).then_inc(S["w0_ps"], 1)
                if i == -1:
                    pe.wait_ge(S["merge_in"], 64)
                    pe.wait_ge(S["w0_lo"], DC)
                    for m in range(2):
                        for c in range(2):
                            last = pe.transpose(bank[7][:, LAT * m + P * c:LAT * m + P * (c + 1)],
                                                ex_raw[:, c, P * m:P * (m + 1)], ident)
                    last.then_inc(S["ext_ps"], 1)
                    pe.wait_ge(S["ext_ready"], 1)
                    for c in range(2):
                        for m in range(2):
                            last = pe.matmul(bank[6 + c][:], ex_t[:, m, P * c:P * (c + 1)], fc2_raw[:, m, :],
                                             start=(m == 0), stop=(m == 1))
                        last.then_inc(S["ef_ps"], 1)
                    for c in range(2):
                        pe.wait_ge(S["ef_ready"], c + 1)
                        for k in range(DC):
                            last = pe.transpose(bank[6 + c][:, P * k:P * (k + 1)], fc1_raw[:, k, P * c:P * (c + 1)], ident)
                        last.then_inc(S["fct_ps"], 1)
                if i == 0:
                    pe.wait_ge(S["xt_lo"], 1)
                    pe.wait_ge(S["x2_s"], 1)
                    for c in range(DC):
                        if c >= 2:
                            pe.wait_ge(S["rt_lo"], c - 1)
                        for k in range(2):
                            last = pe.matmul(bank[6 + c % 2][:], fc1_t[:, k, P * c:P * (c + 1)], ex_fc2[:, k, :],
                                             start=(k == 0), stop=(k == 1))
                        last.then_inc(S["rt_ps"], 1)
                    pe.wait_ge(S["rt_lo"], DC)

            pass1_loop(pe, body, peeled)
            pe.wait_ge(S["x2_stored"], 16 * NT)
            pe.wait_ge(S["stage_lo"], len(WEIGHTS))

            def cols(w, c, n):
                return w[:, c * n:(c + 1) * n]

            def capped(n, t):
                return n * (min(max(t, 0), NT) if isinstance(t, int) else t)

            def body2(i):
                t = i + 3
                if live(t):
                    pe.wait_ge(S["q_s"], t + 1)
                    pe.wait_ge(S["kv_s"], t + 1)
                    wait(pe, S["ngm_s"], t)
                    for g in range(GROUPS):
                        pe.transpose(cols(bank[0], g, P), cols(q_sb, g, P), ident)
                    pe.transpose(bank[1][:, 0:P], kv_sb[:, 0:KVW], ident).then_inc(S["qkt_ps"], 1)
                t = i + 1
                if live(t):
                    pe.wait_ge(S["xn4_s"], t + 1)
                    wait(pe, S["routed_s"], t)
                    for c in range(DC):
                        last = pe.transpose(cols(bank[4], c, P), cols(xn4, c, P), ident)
                    last.then_inc(S["t4_ps"], 1)
                t = i
                if live(t):
                    pe.wait_ge(S["h_s"], t + 1)
                    wait(pe, S["qx_lo"], capped(1, t + 4))
                    for c in range(DC):
                        last = pe.transpose(cols(bank[5], c, P), cols(act2, c, P), ident)
                    last.then_inc(S["ht_ps"], 1)
                t = i + 4
                if live(t):
                    pe.wait_ge(S["ctx2_loaded"], 16 * (t + 1))
                    wait(pe, S["probs_s"], 2 * (t - 1))
                    for c in range(DC):
                        last = pe.transpose(cols(bank[7], c, P), cols(ctx2, c, P), ident)
                    last.then_inc(S["ct_ps"], 1)
                t = i + 2
                if live(t):
                    pe.wait_ge(S["vbd_s"], t + 1)
                    wait(pe, S["kv_s"], capped(1, t + 2))
                    wait(pe, S["z_s"], t - 2)
                    for b in range(2):
                        pe.wait_ge(S["probs_s"], 2 * t + b + 1)
                        for n in range(2):
                            for p in range(PAIRS):
                                lhs = ones_bd if n else vbd[:, b, p].rearrange("k h d -> k (h d)")
                                last = pe.matmul(bank[2 + b][32 * p:32 * (p + 1), 256 * n:256 * (n + 1)], lhs,
                                                 probs[:, b, p, :], start=True, stop=True)
                        last.then_inc(S["pv_ps"], 1)
                t = i + 1
                if live(t):
                    pe.wait_ge(S["t4_lo"], t + 1)
                    wait(pe, S["probs_s"], capped(2, t + 2))
                    wait(pe, S["ct_lo"], capped(1, t + 4))
                    for n in range(2):
                        for c in range(DC):
                            w = slice(INNER * c + D * n, INNER * c + D * (n + 1))
                            last = split_product(bank[6 + n][:], cols(t4_h, c, P), cols(t4_l, c, P),
                                                 up_h[:, w], up_l[:, w], c == 0, c == DC - 1)
                        last.then_inc(S["u_ps"], 1)
                    wait(pe, S["qt_lo"], capped(1, t + 3))
                    wait(pe, S["qt_bs"], capped(1, t + 3))
                    for c in range(DC):
                        last = split_product(bank[0][:, 0:EXPERTS], cols(t4_h, c, P), cols(t4_l, c, P),
                                             cols(gate_h, c, EXPERTS), cols(gate_l, c, EXPERTS), c == 0, c == DC - 1)
                    last.then_inc(S["gate_ps"], 1)
                t = i + 2
                if live(t):
                    pe.wait_ge(S["y_lo"], t + 1)
                    for g in range(GROUPS):
                        last = split_product(bank[2][:], cols(y_h, g, P), cols(y_l, g, P),
                                             cols(wo_h, g, D), cols(wo_l, g, D), g == 0, g == GROUPS - 1)
                    last.then_inc(S["wo_ps"], 1)

                def down(t, part):
                    for c in range(DC):
                        last = split_product(bank[3][:], cols(ht_h, c, P), cols(ht_l, c, P),
                                             cols(down_h, DC * part + c, D), cols(down_l, DC * part + c, D),
                                             part == 0 and c == 0, part == 1 and c == DC - 1)
                    last.then_inc(S["dn_ps"], 1)

                t = i
                if live(t):
                    if isinstance(t, int) and t == 0:
                        pe.wait_ge(S["stage2_lo"], 2)
                    pe.wait_ge(S["ht_lo"], 2 * t + 1)
                    wait(pe, S["y_s"], capped(2, t + 3))
                    down(t, 0)
                t = i + 3
                if live(t):
                    pe.wait_ge(S["kbd_s"], 6 * t + 2)
                    pe.wait_ge(S["qt_bs"], t + 1)
                    pe.wait_ge(S["qt_lo"], t + 1)
                    wait(pe, S["lg_s"], t - 1)
                    pe.wait_ge(S["kt_lo"], t + 1)
                    for g in range(GROUPS):
                        if g >= 2:
                            pe.wait_ge(S["gmax_s"], 4 * t + g - 1)
                        for b in range(2):
                            last = pe.matmul(bank[g % 2][SEQ * b:SEQ * (b + 1), :],
                                             qt_b[:, P * g + SEQ * b:P * g + SEQ * (b + 1)], kbd_b[:, b, :],
                                             start=True, stop=True)
                        last.then_inc(S["g_ps"], 1)
                t = i
                if live(t):
                    for c in range(DC):
                        last = pe.transpose(cols(bank[5], c, P), cols(act2, DC + c, P), ident)
                    last.then_inc(S["ht_ps"], 1)
                t = i + 1
                if live(t):
                    for c in range(DC):
                        last = split_product(bank[4][:], cols(t4_h, c, P), cols(t4_l, c, P),
                                             cols(rt_h, c, D), cols(rt_l, c, D), c == 0, c == DC - 1)
                    last.then_inc(S["rt_out_ps"], 1)
                t = i + 4
                if live(t):
                    pe.wait_ge(S["ct_lo"], t + 1)
                    wait(pe, S["x3_s"], t - 1)
                    for c in range(DC):
                        last = split_product(bank[2][:, 0:2 * KVW], cols(ct_h, c, P), cols(ct_l, c, P),
                                             cols(wkv_h, c, 2 * KVW), cols(wkv_l, c, 2 * KVW), c == 0, c == DC - 1)
                    last.then_inc(S["kv_ps"], 1)
                    pe.wait_ge(S["xn3_s"], t + 1)
                    wait(pe, S["ht_lo"], 2 * (t - 3))
                    for c in range(DC):
                        last = pe.transpose(cols(bank[5], c, P), cols(xn3, c, P), ident)
                    last.then_inc(S["qx_ps"], 1)
                t = i + 3
                if live(t):
                    pe.wait_ge(S["gmax_s"], 4 * t + 4)
                    for g in range(GROUPS):
                        last = pe.transpose(bank[1][0:NKV, P * g:P * (g + 1)], cols(gmax, g, NKV), ident)
                    last.then_inc(S["gmt_ps"], 1)
                t = i
                if live(t):
                    pe.wait_ge(S["ht_lo"], 2 * t + 2)
                    down(t, 1)

                def scores(t, b):
                    for p in range(PAIRS):
                        ps = wide[:, 256 * p:256 * (p + 1)]
                        k = slice(P * p, P * (p + 1))
                        by_group = lambda a: a[:].rearrange("r (g b q) -> r g b q", g=GROUPS, b=2)[:, :, b, :]
                        split_product(ps, kbd_h[:, b, k], kbd_l[:, b, k], by_group(qt_h), by_group(qt_l), True, False)
                        last = pe.matmul(ps, selb[:, k], by_group(ngm), start=False, stop=True)
                    last.then_inc(S["s_ps"], 1)

                t = i + 3
                if live(t):
                    pe.wait_ge(S["kbd_s"], 6 * t + 6)
                    pe.wait_ge(S["qt_lo"], t + 1)
                    pe.wait_ge(S["ngm_s"], t + 1)
                    wait(pe, S["relu_s"], 2 * (t - 1))
                    scores(t, 0)
                t = i + 4
                if live(t):
                    pe.wait_ge(S["qx_lo"], t + 1)
                    wait(pe, S["gmax_s"], 4 * t)
                    for c in range(DC):
                        last = split_product(bank[0][:], cols(xt_h, c, P), cols(xt_l, c, P),
                                             cols(wq_h, c, D), cols(wq_l, c, D), c == 0, c == DC - 1)
                    last.then_inc(S["qy_ps"], 1)
                t = i + 3
                if live(t):
                    pe.wait_ge(S["probs_s"], 2 * t + 1)
                    scores(t, 1)

            pass2_loop(pe, body2, lambda i: None)


_INS = ["x", "ctx_4096", "L0_ffn_lora_A", "L0_ffn_lora_B", "L0_ffn_W", "L0_ffn_bias", "L0_ffn_lora_weights",
        "L1_xattn_Wq", "L1_xattn_bq", "L1_xattn_Wk", "L1_xattn_bk", "L1_xattn_Wv", "L1_xattn_bv",
        "L1_xattn_Wo", "L1_xattn_bo", "L1_ffn_gate_w", "L1_ffn_up_w", "L1_ffn_down_w", "L1_ffn_fc1_w",
        "L1_ffn_fc2_w", "L1_ffn_expert_w", "L1_ffn_ln_gamma", "L1_ffn_ln_beta"]


def kernel(**inputs):
    import numpy as _np
    import concourse.bacc as _bacc
    from concourse import mybir as _mybir
    from concourse.bass_utils import run_bass_kernel_spmd as _run

    nc = _bacc.Bacc("TRN2", target_bir_lowering=False, num_devices=1)
    arrays, args = {}, []
    dft, small = constants()
    named = [(name, _np.ascontiguousarray(inputs[name])) for name in _INS] + [("dft", dft), ("small", small)]
    for name, a in named:
        arrays[f"in_{name}"] = a
        args.append(nc.dram_tensor(f"in_{name}", a.shape, _mybir.dt.from_np(a.dtype), kind="ExternalInput").ap())
    out = nc.dram_tensor("out", (BATCHES, SEQ, D), _mybir.dt.float32, kind="ExternalOutput").ap()
    build(nc, *args, out)
    return _run(nc, [arrays], core_ids=[0]).results[0]["out"]
```

```python
from contextlib import ExitStack

import concourse.bass as bass
import numpy as np
from concourse import mybir

ALU = mybir.AluOpType
ACT = mybir.ActivationFunctionType
AX = mybir.AxisListType
F32 = mybir.dt.float32
F32R = mybir.dt.float32r
BF16 = mybir.dt.bfloat16

P = 128
BATCHES, SEQ, D = 32, 64, 512
TOKENS = BATCHES * SEQ
NT = TOKENS // P
DC = D // P
TOP = 8
ADAPT, RANK = 8, 16
LORA_SCALE = 32 / RANK
NKV, GROUPS, HD = 8, 4, 16
KVW = NKV * HD
PAIRS = NKV // 2
INNER, LAT, EXPERTS = 1024, 256, 8
IC = INNER // P
EPS = 1e-5
REMOVED = -3.0e38
REMOVED_BELOW = -1.0e38

Q0, K0, V0, W0, DFT = 0, P, 3 * P, 7 * P, 9 * P
ICORR0, IOUT0, SEL0, FIRST = 0, 256, 384, 896
IDENT0, HEAD0, ONES0, HALF0, EPS0, SMALL = 896, 1024, 1032, 1064, 1065, 1066


def transform(n, inputs, swapped):
    h = n // 2
    m = np.zeros((inputs, n))
    s = np.arange(inputs)
    for f in range(h + 1):
        m[:, f] = np.cos(2 * np.pi * ((f * s) % n) / n)
    for f in range(1, h):
        m[:, h + f] = -np.sin(2 * np.pi * ((f * s) % n) / n)
    return np.roll(m, h, axis=1) if swapped else m


def inverse(n, outputs, swapped, sign=0):
    h = n // 2
    m = np.zeros((n, outputs))
    s = np.arange(outputs)
    for f in range(h + 1):
        weight = (1.0 if f in (0, h) else 2.0) / n
        angle = 2 * np.pi * ((f * s) % n) / n
        if not swapped:
            m[f] = weight * np.cos(angle)
            if 0 < f < h:
                m[h + f] = weight * np.cos(angle)
        elif 0 < f < h:
            m[f], m[h + f] = sign * weight * np.sin(angle), -sign * weight * np.sin(angle)
    return m


def constants():
    dft = np.zeros((P, DFT))
    ends = lambda m: np.concatenate([m[:SEQ - 1], m[SEQ - 1:].sum(0, keepdims=True)])
    small = np.zeros((P, SMALL))
    for b in range(2):
        rows = slice(SEQ * b, SEQ * b + SEQ)
        dft[rows, Q0 + SEQ * b:Q0 + SEQ * (b + 1)] = transform(SEQ, SEQ, False)
        for j in range(2):
            dft[rows, K0 + P * j + SEQ * b:K0 + P * j + SEQ * (b + 1)] = transform(SEQ, SEQ, j)
            dft[rows, V0 + P * (2 * b + j):V0 + P * (2 * b + j + 1)] = ends(transform(2 * SEQ, 2 * SEQ - 1, j))
            small[rows, ICORR0 + P * j + SEQ * b:ICORR0 + P * j + SEQ * (b + 1)] = inverse(SEQ, SEQ, j, 1)
        dft[rows, W0 + P * b:W0 + P * (b + 1)] = transform(2 * SEQ, SEQ, False)
    for j in range(2):
        small[:, IOUT0 + SEQ * j:IOUT0 + SEQ * (j + 1)] = inverse(2 * SEQ, SEQ, j, -1)
    small[:, IDENT0:IDENT0 + P] = np.eye(P)
    small[:, HEAD0:HEAD0 + NKV] = np.repeat(np.eye(NKV), HD, axis=0)
    small[:, ONES0:ONES0 + 2 * HD] = np.kron(np.eye(2), np.ones((SEQ, HD)))
    for p in range(PAIRS):
        for h in range(2):
            small[2 * p + h, SEL0 + P * p + SEQ * h:SEL0 + P * p + SEQ * (h + 1)] = 1.0
    small[:, HALF0], small[:, EPS0] = -0.5, EPS
    return dft.astype(np.float32), small.astype(np.float32)


def wait(eng, sem, value):
    if not (isinstance(value, int) and value <= 0):
        eng.wait_ge(sem, value)


def build(nc, x, ctx_in, lora_a, lora_b, w0, b0, lora_w, wq, bq, wk, bk, wv, bv, wo, bo,
          gate_w, up_w, down_w, fc1_w, fc2_w, expert_w, gamma, beta, dft_in, small_in, out):
    x_rows = x.rearrange("b s d -> (b s) d")
    ctx_rows = ctx_in.rearrange("b s d -> (b s) d")
    out_rows = out.rearrange("b s d -> (b s) d")
    x2_rows = nc.dram_tensor("x2_rows", [TOKENS, D], F32, kind="Internal").ap()

    with ExitStack() as ctx:
        def sb(name, shape, dt=F32, stack=ctx):
            return stack.enter_context(nc.sbuf_tensor(name, shape, dt))

        def sem(name):
            return ctx.enter_context(nc.semaphore(name))

        bank = [ctx.enter_context(nc.psum_tensor(f"bank{i}", [P, 512], F32)) for i in range(6)]
        wide = ctx.enter_context(nc.psum_tensor("wide", [P, 1024], F32))
        bank += [wide[:, 0:512], wide[:, 512:1024]]

        small = sb("small", [P, SMALL - FIRST])
        selb = sb("selb", [NKV, PAIRS * P], BF16)
        ident = small[:, IDENT0 - FIRST:IDENT0 - FIRST + P]
        head_of = small[:, HEAD0 - FIRST:HEAD0 - FIRST + NKV]
        ones_bd = small[:, ONES0 - FIRST:ONES0 - FIRST + 2 * HD]
        half, eps = (small[:, c - FIRST:c - FIRST + 1] for c in (HALF0, EPS0))
        bq_all = sb("bq_all", [P, D])
        bkv_all = sb("bkv_all", [P, 2 * KVW])
        bo_all = sb("bo_all", [P, D])
        gamma_all = sb("gamma_all", [P, D])
        beta_all = sb("beta_all", [P, D])
        wq_h, wq_l = sb("wq_h", [P, DC * D], F32R), sb("wq_l", [P, DC * D], F32R)
        wkv_h, wkv_l = sb("wkv_h", [P, DC * 2 * KVW], F32R), sb("wkv_l", [P, DC * 2 * KVW], F32R)
        wo_h, wo_l = sb("wo_h", [P, DC * D], F32R), sb("wo_l", [P, DC * D], F32R)
        rt_h, rt_l = sb("rt_h", [P, DC * D], F32R), sb("rt_l", [P, DC * D], F32R)
        gate_hl = sb("gate_hl", [P, DC, 2, EXPERTS], F32R)
        with ExitStack() as tmp:
            w0_raw = sb("w0_raw", [P, DC, D], stack=tmp)
            a_raw = sb("a_raw", [P, D], stack=tmp)
            b_raw = sb("b_raw", [P, DC, P], stack=tmp)
            b_t = sb("b_t", [P, D], stack=tmp)
            ex_raw = sb("ex_raw", [P, 2, LAT], stack=tmp)
            ex_t = sb("ex_t", [P, 2, LAT], stack=tmp)
            fc2_raw = sb("fc2_raw", [P, 2, D], stack=tmp)
            ex_fc2 = sb("ex_fc2", [P, 2, D], stack=tmp)
            fc1_raw = sb("fc1_raw", [P, DC, LAT], stack=tmp)
            fc1_t = w0_raw[:, 0:2, :]
            gate_raw = sb("gate_raw", [P, DC, EXPERTS], stack=tmp)
        up_h, up_l = sb("up_h", [P, DC * INNER], F32R), sb("up_l", [P, DC * INNER], F32R)

        pass1 = ExitStack()
        one = lambda name, shape, dt=F32: sb(name, shape, dt, pass1)
        stage = [one(f"stage{i}", [P, 2048]) for i in range(1)]
        dft_h, dft_l = one("dft_h", [P, DFT], F32R), one("dft_l", [P, DFT], F32R)
        w0_h, w0_l = one("w0_h", [P, DC * D], F32R), one("w0_l", [P, DC * D], F32R)
        b0_all = one("b0_all", [P, D])
        first = one("first", [P, FIRST])
        icorr = [first[:, ICORR0 + P * j:ICORR0 + P * (j + 1)] for j in range(2)]
        iout = [first[:, IOUT0 + SEQ * j:IOUT0 + SEQ * (j + 1)] for j in range(2)]
        coef = one("coef", [P, 1])
        x_in, ctx_t = one("x_in", [P, D]), one("ctx_t", [P, D])
        xn1 = one("xn1", [P, D])
        x_h, x_l = one("x_h", [P, D], F32R), one("x_l", [P, D], F32R)
        c_h, c_l = one("c_h", [P, D], F32R), one("c_l", [P, D], F32R)
        qf = one("qf", [P, D])
        prod = one("prod", [P, 2, D])
        m8 = one("m8", [P, 2 * DC, TOP])
        kept_not = one("kept_not", [P, 2 * DC, SEQ])
        shifted = one("shifted", [P, 2 * DC, SEQ + TOP])
        total, total_inv = one("total", [P, 2 * DC]), one("total_inv", [P, 2 * DC])
        wgt = one("wgt", [P, 2 * DC * SEQ])
        wt_h, wt_l = one("wt_h", [P, D], F32R), one("wt_l", [P, D], F32R)
        vf = one("vf", [P, 2, 2, D])
        prod2 = one("prod2", [P, 2, 2, D])
        x_res, x1 = one("x_res", [P, D]), one("x1", [P, D])
        x1b = one("x1b", [P, D])
        xn2 = one("xn2", [P, D])
        x1t_h, x1t_l = one("x1t_h", [P, D], F32R), one("x1t_l", [P, D], F32R)
        x2 = one("x2", [P, D])
        bn1, mv1, va1, rs1 = one("bn1", [P, 6]), one("mv1", [P, 2]), one("va1", [P, 1]), one("rs1", [P, 1])
        bn2, mv2, va2, rs2 = one("bn2", [P, 6]), one("mv2", [P, 2]), one("va2", [P, 1]), one("rs2", [P, 1])
        pass1.close()

        down_h, down_l = sb("down_h", [P, IC * D], F32R), sb("down_l", [P, IC * D], F32R)
        xn3, ctx2 = sb("xn3", [P, D]), sb("ctx2", [P, D])
        ct_h, ct_l = sb("ct_h", [P, D], F32R), sb("ct_l", [P, D], F32R)
        xt_h, xt_l = sb("xt_h", [P, D], F32R), sb("xt_l", [P, D], F32R)
        kv_sb, q_sb = sb("kv_sb", [P, 2 * KVW]), sb("q_sb", [P, D])
        qt_h, qt_l = sb("qt_h", [P, D], F32R), sb("qt_l", [P, D], F32R)
        qt_b = sb("qt_b", [P, D], BF16)
        kt_h, kt_l = sb("kt_h", [P, P], F32R), sb("kt_l", [P, P], F32R)
        kbd_h, kbd_l = sb("kbd_h", [P, 2, D], F32R), sb("kbd_l", [P, 2, D], F32R)
        kbd_b = sb("kbd_b", [P, 2, D], BF16)
        gmax = sb("gmax", [P, GROUPS * NKV])
        ngm = sb("ngm", [NKV, GROUPS * P], BF16)
        probs = sb("probs", [P, 2, PAIRS, GROUPS * SEQ])
        vbd = sb("vbd", [P, 2, PAIRS, 2, HD])
        y = sb("y", [P, GROUPS, 2, SEQ])
        y_h, y_l = sb("y_h", [P, D], F32R), sb("y_l", [P, D], F32R)
        x2_res, x3, x3b, x3c, xn4 = (sb(n, [P, D]) for n in ("x2_res", "x3", "x3b", "x3c", "xn4"))
        t4_h, t4_l = sb("t4_h", [P, D], F32R), sb("t4_l", [P, D], F32R)
        logits, lg, rw = sb("logits", [P, EXPERTS]), sb("lg", [P, TOP]), sb("rw", [P, 1])
        stage2 = sb("stage2", [P, INNER + 2 * D])
        act2, routed, z = stage2[:, 0:INNER], stage2[:, INNER:INNER + D], stage2[:, INNER + D:]
        ht_h, ht_l = sb("ht_h", [P, D], F32R), sb("ht_l", [P, D], F32R)
        bn3, mv3, va3, rs3 = (sb(n, [P, w]) for n, w in (("bn3", 6), ("mv3", 2), ("va3", 1), ("rs3", 1)))
        bn4, mv4, va4, rs4 = (sb(n, [P, w]) for n, w in (("bn4", 6), ("mv4", 2), ("va4", 1), ("rs4", 1)))
        bn5, mv5, va5, rs5 = (sb(n, [P, w]) for n, w in (("bn5", 6), ("mv5", 2), ("va5", 1), ("rs5", 1)))

        SEMS = """stage2_in stage2_hi stage2_lo vbd_zero
            tile_loaded ctx2_loaded res2_loaded out_stored
            bn3_s mv3_s va3_s rs3_s xn3_s bn4_s mv4_s va4_s rs4_s xn4_s bn5_s mv5_s va5_s rs5_s zn_s
            ct_ps ct_hi ct_lo kv_ps kv_s qx_ps qx_hi qx_lo qy_ps q_s
            qkt_ps kt_hi kt_lo qt_hi qt_lo qt_bs kbd_s vbd_s g_ps gmax_s gmt_ps ngm_s s_ps probs_s
            pv_ps den_s y_s y_hi y_lo wo_ps x2b_s x3_s x3b_s x3c_s
            t4_ps t4_hi t4_lo u_ps relu_s h_s gate_ps lg_s top_s rw_s rt_out_ps routed_s
            ht_ps ht_hi ht_lo dn_ps z_s zg_s o_s
            const_in dft_loaded first_in merge_in lora_in bcast_in stage_in dft_hi dft_lo sel_ready gate_split
            bt_ps coef_ready bt_ready ext_ps ext_ready ef_ps ef_ready w0_ps w0_hi w0_lo rt_ps rt_hi rt_lo
            fct_ps fct_ready stage_hi stage_lo
            x_loaded ctx_loaded res_loaded bn1_s mv1_s va1_s rs1_s xn1_s x_hi x_lo c_hi c_lo
            q_ps qf_s k_ps prod_s v_ps vf_s corr_ps tops_s rep_s shift_s exp_s mask_s sum_s inv_s wgt_s
            wt_ps wt_hi wt_lo wf_ps prod2_s o_ps x1_s bn2_s mv2_s va2_s rs2_s xn2_s x1b_s
            xt_ps xt_hi xt_lo ffn_ps x2_s x2_stored""".split()
        S = {name: sem(name) for name in SEMS}

        block = ctx.enter_context(nc.Block())

        def rows(dram, t):
            return dram[bass.ts(t, P), :]

        LEAD, PEELED = 3, 4

        def pass1_loop(eng, body, peeled):
            for i in range(-LEAD, PEELED):
                body(i)
                peeled(i)
            with eng.Fori(PEELED, NT - LEAD - 1) as i:
                body(i)
            for i in range(NT - LEAD - 1, NT + 1):
                body(i)
                peeled(i)

        W_BANK, V_BANK = (3, 0), (1, 2, 3, 0)

        def live(t):
            return not isinstance(t, int) or 0 <= t < NT

        def min_tiles(n, t):
            return n * (min(t, NT) if isinstance(t, int) else t)

        LEAD2 = 4

        def pass2_loop(eng, body, peeled):
            for i in range(-LEAD2, 2):
                body(i)
                peeled(i)
            with eng.Fori(2, NT - LEAD2) as i:
                body(i)
            for i in range(NT - LEAD2, NT + 1):
                body(i)

        wo_v = wo.rearrange("(h g d) n -> h d g n", h=NKV, g=GROUPS)
        up_v = up_w.rearrange("(c p) n -> p c n", p=P)
        down_v = down_w.rearrange("(c p) n -> p c n", p=P)
        stage3 = stage[0][:].rearrange("p (c n) -> p c n", c=DC)
        stage_kv = stage[0][:, 0:DC * 2 * KVW].rearrange("p (c n) -> p c n", c=DC)
        stage_up = stage[0][:].rearrange("p (c n) -> p c n", c=2)
        half_up = DC * INNER // 2
        WEIGHTS = {
            -2: ([(stage3, wq.rearrange("(c p) n -> p c n", p=P))], wq_h[:], wq_l[:]),
            -1: ([(stage3[HD * h:HD * (h + 1)], wo_v[h]) for h in range(NKV)], wo_h[:], wo_l[:]),
            0: ([(stage_kv[:, :, 0:KVW], wk.rearrange("(c p) n -> p c n", p=P)),
                 (stage_kv[:, :, KVW:2 * KVW], wv.rearrange("(c p) n -> p c n", p=P))], wkv_h[:], wkv_l[:]),
            1: ([(stage_up, up_v[:, 0:2, :])], up_h[:, 0:half_up], up_l[:, 0:half_up]),
            2: ([(stage_up, up_v[:, 2:4, :])], up_h[:, half_up:], up_l[:, half_up:]),
        }
        STAGED = {i: n + 1 for n, i in enumerate(WEIGHTS)}
        LANDED = {i: 16 * sum(len(w[0]) for k, w in WEIGHTS.items() if k <= i) for i in WEIGHTS}

        def staged_before(i):
            return isinstance(i, int) and i - 1 in WEIGHTS


        @block.sync
        def _(sp):
            sp.dma_start(small[:], small_in[:, FIRST:SMALL]).then_inc(S["const_in"], 16)
            sp.dma_start(x_in[:], rows(x_rows, 0)).then_inc(S["x_loaded"], 16)
            sp.dma_start(stage[0][:, 0:DFT], dft_in).then_inc(S["dft_loaded"], 16)
            sp.dma_start(ctx_t[:], rows(ctx_rows, 0)).then_inc(S["ctx_loaded"], 16)
            sp.dma_start(first[:], small_in[:, 0:FIRST]).then_inc(S["first_in"], 16)

            def body(i):
                t = i + 1
                if live(t):
                    wait(sp, S["x1_s"], t)
                    sp.dma_start(x_res[:], rows(x_rows, t)).then_inc(S["res_loaded"], 16)
                t = i - 1
                if live(t):
                    sp.wait_ge(S["x2_s"], t + 1)
                    sp.dma_start(rows(x2_rows, t), x2[:]).then_inc(S["x2_stored"], 16)
                t = i + 4
                if live(t):
                    sp.wait_ge(S["xn1_s"], t)
                    sp.dma_start(x_in[:], rows(x_rows, t)).then_inc(S["x_loaded"], 16)
                t = i + 4
                if live(t):
                    sp.wait_ge(S["c_lo"], t)
                    sp.dma_start(ctx_t[:], rows(ctx_rows, t)).then_inc(S["ctx_loaded"], 16)

            def peeled(i):
                if i == -3:
                    sp.dma_start(w0_raw[:], w0.rearrange("(c p) d -> p c d", p=P)).then_inc(S["lora_in"], 16)
                    sp.dma_start(a_raw[:], lora_a.rearrange("n r d -> (n r) d")).then_inc(S["lora_in"], 16)
                    for c in range(DC):
                        sp.dma_start(b_raw[:, c, :].rearrange("p (n r) -> p n r", n=ADAPT),
                                     lora_b[:, c * P:(c + 1) * P, :].rearrange("n o r -> o n r")
                                     ).then_inc(S["lora_in"], 16)
                    for n in range(ADAPT):
                        sp.dma_start(coef[n * RANK:(n + 1) * RANK, :],
                                     lora_w[n:n + 1].rearrange("(a b) -> a b", a=1).to_broadcast([RANK, 1])
                                     ).then_inc(S["lora_in"], 16)
                    sp.dma_start(b0_all[:], b0.rearrange("(a n) -> a n", a=1).to_broadcast([P, D])
                                 ).then_inc(S["bcast_in"], 16)
                if i == -2:
                    sp.dma_start(ex_raw[:], expert_w.rearrange("(c p) n -> p c n", p=P)).then_inc(S["merge_in"], 16)
                    sp.dma_start(fc2_raw[:], fc2_w.rearrange("(c p) n -> p c n", p=P)).then_inc(S["merge_in"], 16)
                    sp.dma_start(fc1_raw[:], fc1_w.rearrange("(c p) n -> p c n", p=P)).then_inc(S["merge_in"], 16)
                    sp.dma_start(gate_raw[:], gate_w.rearrange("(c p) n -> p c n", p=P)).then_inc(S["merge_in"], 16)
                    for tile, dram in ((bq_all[:], bq), (bkv_all[:, 0:KVW], bk), (bkv_all[:, KVW:2 * KVW], bv),
                                       (bo_all[:], bo), (gamma_all[:], gamma), (beta_all[:], beta)):
                        sp.dma_start(tile, dram.rearrange("(a n) -> a n", a=1).to_broadcast([P, tile.shape[1]])
                                     ).then_inc(S["bcast_in"], 16)

                if i in WEIGHTS:
                    sp.wait_ge(S["dft_lo"], 1)
                    wait(sp, S["stage_lo"], 2 * (STAGED[i] - 1))
                    for tile, dram in WEIGHTS[i][0]:
                        sp.dma_start(tile, dram).then_inc(S["stage_in"], 16)

            pass1_loop(sp, body, peeled)
            sp.wait_ge(S["x2_stored"], 16 * NT)
            sp.wait_ge(S["stage_lo"], 2 * len(WEIGHTS))

            def body2(i):
                t = i + 4
                if live(t):
                    wait(sp, S["qx_ps"], t)
                    sp.dma_start(xn3[:], rows(x2_rows, t)).then_inc(S["tile_loaded"], 16)
                    wait(sp, S["ct_ps"], t)
                    sp.dma_start(ctx2[:], rows(ctx_rows, t)).then_inc(S["ctx2_loaded"], 16)
                t = i + 2
                if live(t):
                    wait(sp, S["x3_s"], t)
                    sp.dma_start(x2_res[:], rows(x2_rows, t)).then_inc(S["res2_loaded"], 16)
                t = i - 1
                if live(t):
                    sp.wait_ge(S["o_s"], t + 1)
                    sp.dma_start(rows(out_rows, t), z[:]).then_inc(S["out_stored"], 16)

            def peeled2(i):
                if i < 2 - LEAD2:
                    c = i + LEAD2
                    wait(sp, S["stage2_lo"], c)
                    sp.dma_start(stage2[:].rearrange("p (c n) -> p c n", c=DC), down_v[:, DC * c:DC * (c + 1), :]
                                 ).then_inc(S["stage2_in"], 16)

            pass2_loop(sp, body2, peeled2)
            sp.wait_ge(S["out_stored"], 16 * NT)

        @block.scalar
        def _(act):
            act.wait_ge(S["dft_loaded"], 16)
            act.activation(dft_h[:], stage[0][:, 0:DFT], ACT.Copy).then_inc(S["dft_hi"], 1)
            act.wait_ge(S["first_in"], 16)
            act.activation(selb[:], first[0:NKV, SEL0:SEL0 + PAIRS * P], ACT.Copy).then_inc(S["sel_ready"], 1)

            def value_spectrum(t, parts):
                for n in parts:
                    act.wait_ge(S["v_ps"], 4 * t + n + 1)
                    act.activation(vf[:, n // 2, n % 2, :], bank[V_BANK[n]][:], ACT.Copy).then_inc(S["vf_s"], 1)

            def body(i):
                t = i + 2
                if live(t):
                    act.wait_ge(S["q_ps"], t + 1)
                    wait(act, S["prod_s"], 2 * t)
                    act.activation(qf[:], bank[0][:], ACT.Copy).then_inc(S["qf_s"], 1)
                if staged_before(i):
                    act.wait_ge(S["stage_in"], LANDED[i - 1])
                    if i > 1:
                        act.wait_ge(S["rt_lo"], DC)
                    target = WEIGHTS[i - 1][1]
                    act.activation(target, stage[0][:, 0:target.shape[1]], ACT.Copy).then_inc(S["stage_hi"], 1)
                t = i
                if live(t):
                    act.wait_ge(S["xt_ps"], t + 1)
                    wait(act, S["ffn_ps"], t)
                    act.activation(x1t_h[:], bank[5][:], ACT.Copy).then_inc(S["xt_hi"], 1)
                t = i + 2
                if live(t):
                    wait(act, S["prod2_s"], 4 * t)
                    value_spectrum(t, (0, 1))
                t = i + 3
                if live(t):
                    act.wait_ge(S["xn1_s"], t + 1)
                    wait(act, S["q_ps"], t)
                    act.activation(x_h[:], xn1[:], ACT.Copy).then_inc(S["x_hi"], 1)
                t = i + 2
                if live(t):
                    act.wait_ge(S["shift_s"], t + 1)
                    act.activation(shifted[:], shifted[:], ACT.Exp).then_inc(S["exp_s"], 1)
                    value_spectrum(t, (2, 3))
                t = i + 3
                if live(t):
                    act.wait_ge(S["ctx_loaded"], 16 * (t + 1))
                    wait(act, S["v_ps"], 4 * t)
                    act.activation(c_h[:], ctx_t[:], ACT.Copy).then_inc(S["c_hi"], 1)
                t = i + 2
                if live(t):
                    act.wait_ge(S["wt_ps"], t + 1)
                    wait(act, S["wf_ps"], 2 * t)
                    act.activation(wt_h[:], bank[5][:], ACT.Copy).then_inc(S["wt_hi"], 1)

            def peeled(i):
                if i == -2:
                    for c in range(DC):
                        act.wait_ge(S["w0_ps"], c + 1)
                        act.activation(w0_h[:, c * D:(c + 1) * D], bank[6 + c % 2][:], ACT.Copy
                                       ).then_inc(S["w0_hi"], 1)
                if i == -1:
                    act.wait_ge(S["merge_in"], 64)
                    act.activation(gate_hl[:, :, 0, :], gate_raw[:], ACT.Copy).then_inc(S["gate_split"], 1)
                    act.wait_ge(S["ext_ps"], 1)
                    act.activation(ex_t[:].rearrange("p a b -> p (a b)"), bank[7][:], ACT.Copy).then_inc(S["ext_ready"], 1)
                    for c in range(2):
                        act.wait_ge(S["ef_ps"], c + 1)
                        act.activation(ex_fc2[:, c, :], bank[6 + c][:], ACT.Copy).then_inc(S["ef_ready"], 1)
                    for c in range(2):
                        act.wait_ge(S["fct_ps"], c + 1)
                        act.activation(fc1_t[:, c, :], bank[6 + c][:], ACT.Copy).then_inc(S["fct_ready"], 1)
                    for c in range(DC):
                        act.wait_ge(S["rt_ps"], c + 1)
                        act.activation(rt_h[:, c * D:(c + 1) * D], bank[6 + c % 2][:], ACT.Copy
                                       ).then_inc(S["rt_hi"], 1)

            pass1_loop(act, body, peeled)
            act.wait_ge(S["x2_stored"], 16 * NT)

            def body2(i):
                t = i + 1
                if live(t):
                    act.wait_ge(S["t4_ps"], t + 1)
                    wait(act, S["rt_out_ps"], t)
                    act.activation(t4_h[:], bank[4][:], ACT.Copy).then_inc(S["t4_hi"], 1)
                t = i + 3
                if live(t):
                    act.wait_ge(S["qkt_ps"], t + 1)
                    wait(act, S["kbd_s"], 6 * t)
                    act.activation(kt_h[:], bank[1][:, 0:P], ACT.Copy).then_inc(S["kt_hi"], 1)
                    wait(act, S["s_ps"], 2 * t)
                    act.activation(qt_h[:], bank[0][:], ACT.Copy).then_inc(S["qt_hi"], 1)
                    wait(act, S["g_ps"], 4 * t)
                    act.activation(qt_b[:], bank[0][:], ACT.Copy).then_inc(S["qt_bs"], 1)
                t = i
                if live(t):
                    act.wait_ge(S["ht_ps"], 2 * t + 1)
                    wait(act, S["dn_ps"], 2 * t)
                    act.activation(ht_h[:], bank[5][:], ACT.Copy).then_inc(S["ht_hi"], 1)
                    wait(act, S["o_s"], t)
                    act.wait_ge(S["x3b_s"], t + 1)
                    act.activation(x3c[:], x3b[:], ACT.Copy).then_inc(S["x3c_s"], 1)
                t = i + 4
                if live(t):
                    act.wait_ge(S["ct_ps"], t + 1)
                    wait(act, S["kv_ps"], t)
                    act.activation(ct_h[:], bank[7][:], ACT.Copy).then_inc(S["ct_hi"], 1)
                t = i + 2
                if live(t):
                    act.wait_ge(S["y_s"], 2 * t + 2)
                    wait(act, S["wo_ps"], t)
                    act.activation(y_h[:], y[:].rearrange("p g b q -> p (g b q)"), ACT.Copy).then_inc(S["y_hi"], 1)
                t = i + 1
                if live(t):
                    if isinstance(t, int) and t == 0:
                        act.wait_ge(S["stage2_lo"], 2)
                    wait(act, S["ht_ps"], 2 * t)
                    for c in range(2):
                        act.wait_ge(S["u_ps"], 2 * t + c + 1)
                        act.activation(act2[:, c * D:(c + 1) * D], bank[6 + c][:], ACT.Relu).then_inc(S["relu_s"], 1)
                t = i
                if live(t):
                    act.wait_ge(S["ht_ps"], 2 * t + 2)
                    act.wait_ge(S["dn_ps"], 2 * t + 1)
                    act.activation(ht_h[:], bank[5][:], ACT.Copy).then_inc(S["ht_hi"], 1)
                t = i + 4
                if live(t):
                    act.wait_ge(S["qx_ps"], t + 1)
                    wait(act, S["qy_ps"], t)
                    act.activation(xt_h[:], bank[5][:], ACT.Copy).then_inc(S["qx_hi"], 1)
                t = i + 3
                if live(t):
                    act.wait_ge(S["gmt_ps"], t + 1)
                    wait(act, S["s_ps"], 2 * t)
                    act.activation(ngm[:], bank[1][0:NKV, :], ACT.Copy, scale=-1.0).then_inc(S["ngm_s"], 1)
                    act.wait_ge(S["s_ps"], 2 * t + 1)
                    wait(act, S["pv_ps"], 2 * t)
                    act.activation(probs[:, 0].rearrange("p a b -> p (a b)"), wide[:], ACT.Exp, scale=HD ** -0.5
                                   ).then_inc(S["probs_s"], 1)
                t = i + 1
                if live(t):
                    act.wait_ge(S["rt_out_ps"], t + 1)
                    act.wait_ge(S["rw_s"], t + 1)
                    wait(act, S["z_s"], t)
                    act.activation(routed[:], bank[4][:], ACT.Copy, scale=rw[:]).then_inc(S["routed_s"], 1)
                t = i + 3
                if live(t):
                    act.wait_ge(S["s_ps"], 2 * t + 2)
                    act.activation(probs[:, 1].rearrange("p a b -> p (a b)"), wide[:], ACT.Exp, scale=HD ** -0.5
                                   ).then_inc(S["probs_s"], 1)

            def peeled2(i):
                if i < 2 - LEAD2:
                    c = i + LEAD2
                    act.wait_ge(S["stage2_in"], 16 * (c + 1))
                    act.activation(down_h[:, DC * D * c:DC * D * (c + 1)], stage2[:], ACT.Copy).then_inc(S["stage2_hi"], 1)

            pass2_loop(act, body2, peeled2)

        @block.gpsimd
        def _(pool):
            def rstd(t, mv, var, rs, n):
                pool.wait_ge(S[f"mv{n}_s"], t + 1)
                pool.tensor_tensor(var[:], mv[:, 1:2], eps, ALU.add).then_inc(S[f"va{n}_s"], 1)
                pool.wait_ge(S[f"va{n}_s"], t + 1)
                pool.tensor_tensor(rs[:], var[:], half, ALU.pow).then_inc(S[f"rs{n}_s"], 1)

            pool.wait_ge(S["const_in"], 16)

            def body(i):
                t = i + 3
                if live(t):
                    rstd(t, mv1, va1, rs1, 1)
                if staged_before(i):
                    low_half(i - 1, 0)
                if live(t):
                    pool.wait_ge(S["x_hi"], t + 1)
                    wait(pool, S["q_ps"], t)
                    pool.tensor_tensor(x_l[:], xn1[:], x_h[:].bitcast(F32), ALU.subtract).then_inc(S["x_lo"], 1)
                if staged_before(i):
                    low_half(i - 1, 1)
                t = i + 3
                if live(t):
                    pool.wait_ge(S["c_hi"], t + 1)
                    wait(pool, S["v_ps"], 4 * t)
                    pool.tensor_tensor(c_l[:], ctx_t[:], c_h[:].bitcast(F32), ALU.subtract).then_inc(S["c_lo"], 1)
                t = i + 1
                if live(t):
                    rstd(t, mv2, va2, rs2, 2)
                    pool.wait_ge(S["x1_s"], t + 1)
                    wait(pool, S["x2_s"], t)
                    pool.tensor_tensor(x1b[:], x1[:], b0_all[:], ALU.add).then_inc(S["x1b_s"], 1)

            def low_half(i, part):
                hi, lo = WEIGHTS[i][1:]
                n = lo.shape[1] // 2
                k = slice(n * part, n * (part + 1))
                pool.wait_ge(S["stage_hi"], STAGED[i])
                pool.tensor_tensor(lo[:, k], stage[0][:, k], hi[:, k].bitcast(F32), ALU.subtract
                                   ).then_inc(S["stage_lo"], 1)

            pass1_loop(pool, body, lambda i: None)
            pool.wait_ge(S["x2_stored"], 16 * NT)

            heads = head_of.unsqueeze(2).to_broadcast([P, NKV, SEQ])

            def body2(i):
                t = i - 1
                if live(t):
                    pool.wait_ge(S["zn_s"], t + 1)
                    pool.tensor_tensor(z[:], z[:], gamma_all[:], ALU.mult).then_inc(S["zg_s"], 1)
                    pool.wait_ge(S["zg_s"], t + 1)
                    pool.wait_ge(S["x3c_s"], t + 1)
                    pool.tensor_tensor(z[:], z[:], x3c[:], ALU.add).then_inc(S["o_s"], 1)
                t = i + 3
                if live(t):
                    def spread(out, kt, b):
                        k = kt[:, SEQ * b:SEQ * (b + 1)].bitcast(F32).unsqueeze(1).to_broadcast([P, NKV, SEQ])
                        pool.tensor_tensor(out[:, b, :].rearrange("p (h k) -> p h k", h=NKV), k, heads, ALU.mult
                                           ).then_inc(S["kbd_s"], 1)

                    pool.wait_ge(S["kt_hi"], t + 1)
                    wait(pool, S["g_ps"], 4 * t)
                    spread(kbd_b, kt_h, 0)
                    spread(kbd_b, kt_h, 1)
                t = i + 4
                if live(t):
                    rstd(t, mv3, va3, rs3, 3)
                t = i + 2
                if live(t):
                    pool.wait_ge(S["y_hi"], t + 1)
                    wait(pool, S["wo_ps"], t)
                    pool.tensor_tensor(y_l[:], y[:].rearrange("p g b q -> p (g b q)"), y_h[:].bitcast(F32),
                                       ALU.subtract).then_inc(S["y_lo"], 1)
                    pool.wait_ge(S["res2_loaded"], 16 * (t + 1))
                    pool.tensor_tensor(x2_res[:], x2_res[:], bo_all[:], ALU.add).then_inc(S["x2b_s"], 1)
                t = i + 1
                if live(t):
                    pool.wait_ge(S["x3_s"], t + 1)
                    wait(pool, S["x3c_s"], t)
                    pool.tensor_tensor(x3b[:], x3[:], beta_all[:], ALU.add).then_inc(S["x3b_s"], 1)
                t = i + 3
                if live(t):
                    wait(pool, S["s_ps"], 2 * t)
                    spread(kbd_h, kt_h, 0)
                    spread(kbd_h, kt_h, 1)
                    pool.wait_ge(S["kt_lo"], t + 1)
                    spread(kbd_l, kt_l, 0)
                    spread(kbd_l, kt_l, 1)
                t = i + 2
                if live(t):
                    rstd(t, mv4, va4, rs4, 4)
                t = i + 1
                if live(t):
                    pool.wait_ge(S["relu_s"], 2 * t + 2)
                    pool.tensor_tensor(act2[:], act2[:], act2[:], ALU.mult).then_inc(S["h_s"], 1)
                t = i
                if live(t):
                    rstd(t, mv5, va5, rs5, 5)

            def peeled2(i):
                if i < 2 - LEAD2:
                    c = i + LEAD2
                    part = slice(DC * D * c, DC * D * (c + 1))
                    pool.wait_ge(S["stage2_hi"], c + 1)
                    pool.tensor_tensor(down_l[:, part], stage2[:], down_h[:, part].bitcast(F32), ALU.subtract
                                       ).then_inc(S["stage2_lo"], 1)

            pass2_loop(pool, body2, peeled2)


        def wait_alone(eng, sem, value, done, times):
            value = value if isinstance(value, int) else eng.snap(eng.to_reg(value))
            eng.wait_ge(done, times)
            wait(eng, sem, value)

        @block.vector
        def _(dve):
            def body(i):
                t = i + 2
                if live(t):
                    dve.wait_ge(S["qf_s"], t + 1)
                    wait(dve, S["corr_ps"], t)
                    for j in range(2):
                        dve.wait_ge(S["k_ps"], 2 * t + j + 1)
                        dve.tensor_tensor(prod[:, j, :], bank[1 + j][:], qf[:], ALU.mult
                                          ).then_inc(S["prod_s"], 1)
                t = i
                if live(t):
                    dve.wait_ge(S["rs2_s"], t + 1)
                    wait(dve, S["xt_ps"], t)
                    dve.tensor_scalar(xn2[:], x1[:], mv2[:, 0:1], rs2[:], ALU.subtract, ALU.mult
                                      ).then_inc(S["xn2_s"], 1)
                t = i - 1
                if live(t):
                    dve.wait_ge(S["ffn_ps"], t + 1)
                    dve.wait_ge(S["x1b_s"], t + 1)
                    wait(dve, S["x2_stored"], 16 * t)
                    dve.tensor_tensor(x2[:], bank[7][:], x1b[:], ALU.add).then_inc(S["x2_s"], 1)
                t = i + 3
                if live(t):
                    dve.wait_ge(S["x_loaded"], 16 * (t + 1))
                    dve.bn_stats(bn1[:], x_in[:]).then_inc(S["bn1_s"], 1)
                    wait_alone(dve, S["bn1_s"], t + 1, S["x_loaded"], 16)
                    dve.bn_aggr(mv1[:], bn1[:]).then_inc(S["mv1_s"], 1)
                t = i + 1
                if live(t):
                    wait(dve, S["o_ps"], t)
                    dve.wait_ge(S["vf_s"], 4 * t + 4)
                    for n in range(4):
                        dve.wait_ge(S["wf_ps"], 2 * t + n // 2 + 1)
                        dve.tensor_tensor(prod2[:, n // 2, n % 2, :], bank[W_BANK[n // 2]][:],
                                          vf[:, n // 2, n % 2, :], ALU.mult).then_inc(S["prod2_s"], 1)
                t = i + 3
                if live(t):
                    dve.wait_ge(S["rs1_s"], t + 1)
                    wait(dve, S["x_lo"], t)
                    dve.tensor_scalar(xn1[:], x_in[:], mv1[:, 0:1], rs1[:], ALU.subtract, ALU.mult
                                      ).then_inc(S["xn1_s"], 1)
                t = i + 2
                if live(t):
                    corr = bank[4][:].rearrange("p (c s) -> p c s", s=SEQ)
                    wait_alone(dve, S["corr_ps"], t + 1, S["x_loaded"], 16)
                    for c in range(2 * DC):
                        top = dve.max(m8[:, c, :], corr[:, c, :])
                    top.then_inc(S["tops_s"], 1)
                t = i
                if live(t):
                    dve.wait_ge(S["xt_hi"], t + 1)
                    wait(dve, S["ffn_ps"], t)
                    dve.tensor_tensor(x1t_l[:], bank[5][:], x1t_h[:].bitcast(F32), ALU.subtract
                                      ).then_inc(S["xt_lo"], 1)
                t = i + 2
                if live(t):
                    wait(dve, S["wgt_s"], t)
                    dve.wait_ge(S["tops_s"], t + 1)
                    best = m8[:, :, 0:1]
                    dve.tensor_tensor(shifted[:, :, 0:SEQ], corr, best.to_broadcast([P, 2 * DC, SEQ]),
                                      ALU.subtract)
                    dve.tensor_tensor(shifted[:, :, SEQ:SEQ + TOP], m8[:], best.to_broadcast([P, 2 * DC, TOP]),
                                      ALU.subtract).then_inc(S["shift_s"], 1)
                    for c in range(2 * DC):
                        kept = dve.match_replace(kept_not[:, c, :], m8[:, c, :], corr[:, c, :], REMOVED)
                    kept.then_inc(S["rep_s"], 1)
                    dve.wait_ge(S["exp_s"], t + 1)
                    dve.wait_ge(S["rep_s"], t + 1)
                    dve.scalar_tensor_tensor(kept_not[:], kept_not[:], REMOVED_BELOW, shifted[:, :, 0:SEQ],
                                             ALU.is_lt, ALU.mult).then_inc(S["mask_s"], 1)
                    dve.tensor_reduce(total[:], shifted[:, :, SEQ:SEQ + TOP], AX.X, ALU.add).then_inc(S["sum_s"], 1)
                    dve.wait_ge(S["sum_s"], t + 1)
                    dve.reciprocal(total_inv[:], total[:]).then_inc(S["inv_s"], 1)
                    dve.wait_ge(S["inv_s"], t + 1)
                    dve.wait_ge(S["mask_s"], t + 1)
                    wait(dve, S["wt_ps"], t)
                    dve.tensor_tensor(wgt[:].rearrange("p (c s) -> p c s", s=SEQ), kept_not[:],
                                      total_inv[:].unsqueeze(2).to_broadcast([P, 2 * DC, SEQ]), ALU.mult
                                      ).then_inc(S["wgt_s"], 1)
                t = i + 1
                if live(t):
                    dve.wait_ge(S["o_ps"], t + 1)
                    dve.wait_ge(S["res_loaded"], 16 * (t + 1))
                    wait(dve, S["x1b_s"], t)
                    dve.tensor_tensor(x1[:], bank[6][:], x_res[:], ALU.add).then_inc(S["x1_s"], 1)
                    dve.wait_ge(S["x1_s"], t + 1)
                    dve.bn_stats(bn2[:], x1[:]).then_inc(S["bn2_s"], 1)
                    wait_alone(dve, S["bn2_s"], t + 1, S["x_loaded"], 16)
                    dve.bn_aggr(mv2[:], bn2[:]).then_inc(S["mv2_s"], 1)
                t = i + 2
                if live(t):
                    dve.wait_ge(S["wt_hi"], t + 1)
                    wait(dve, S["wf_ps"], 2 * t)
                    dve.tensor_tensor(wt_l[:], bank[5][:], wt_h[:].bitcast(F32), ALU.subtract
                                      ).then_inc(S["wt_lo"], 1)

            def peeled(i):
                if i == -3:
                    dve.wait_ge(S["dft_hi"], 1)
                    dve.tensor_tensor(dft_l[:], stage[0][:, 0:DFT], dft_h[:].bitcast(F32), ALU.subtract
                                      ).then_inc(S["dft_lo"], 1)
                if i == -2:
                    dve.wait_ge(S["bt_ps"], 1)
                    dve.tensor_scalar(b_t[:], bank[6][:], coef[:], LORA_SCALE, ALU.mult, ALU.mult
                                      ).then_inc(S["bt_ready"], 1)
                    for c in range(DC):
                        dve.wait_ge(S["w0_hi"], c + 1)
                        dve.tensor_tensor(w0_l[:, c * D:(c + 1) * D], bank[6 + c % 2][:],
                                          w0_h[:, c * D:(c + 1) * D].bitcast(F32), ALU.subtract
                                          ).then_inc(S["w0_lo"], 1)
                if i == -1:
                    dve.wait_ge(S["gate_split"], 1)
                    dve.tensor_tensor(gate_hl[:, :, 1, :], gate_raw[:], gate_hl[:, :, 0, :].bitcast(F32), ALU.subtract
                                      ).then_inc(S["gate_split"], 1)
                    for c in range(DC):
                        dve.wait_ge(S["rt_hi"], c + 1)
                        dve.tensor_tensor(rt_l[:, c * D:(c + 1) * D], bank[6 + c % 2][:],
                                          rt_h[:, c * D:(c + 1) * D].bitcast(F32), ALU.subtract
                                          ).then_inc(S["rt_lo"], 1)

            pass1_loop(dve, body, peeled)
            dve.wait_ge(S["x2_stored"], 16 * NT)
            dve.wait_ge(S["bcast_in"], 16 * 7)
            dve.memset(vbd[:], 0.0).then_inc(S["vbd_zero"], 1)
            dve.wait_ge(S["vbd_zero"], 1)

            def maxima(t, groups):
                for g in groups:
                    dve.wait_ge(S["g_ps"], 4 * t + g + 1)
                    dve.tensor_reduce(gmax[:, NKV * g:NKV * (g + 1)],
                                      bank[g % 2][:].rearrange("p (h k) -> p h k", h=NKV), AX.X, ALU.max
                                      ).then_inc(S["gmax_s"], 1)

            def body2(i):
                t = i + 1
                if live(t):
                    dve.wait_ge(S["t4_hi"], t + 1)
                    wait(dve, S["rt_out_ps"], t)
                    dve.tensor_tensor(t4_l[:], bank[4][:], t4_h[:].bitcast(F32), ALU.subtract).then_inc(S["t4_lo"], 1)
                t = i + 3
                if live(t):
                    dve.wait_ge(S["kt_hi"], t + 1)
                    wait(dve, S["kbd_s"], 6 * t)
                    dve.tensor_tensor(kt_l[:], bank[1][:, 0:P], kt_h[:].bitcast(F32), ALU.subtract).then_inc(S["kt_lo"], 1)
                    dve.wait_ge(S["qt_bs"], t + 1)
                    wait(dve, S["s_ps"], 2 * t)
                    dve.tensor_tensor(qt_l[:], bank[0][:], qt_h[:].bitcast(F32), ALU.subtract).then_inc(S["qt_lo"], 1)
                t = i
                if live(t):
                    dve.wait_ge(S["ht_hi"], 2 * t + 1)
                    wait(dve, S["dn_ps"], 2 * t)
                    dve.tensor_tensor(ht_l[:], bank[5][:], ht_h[:].bitcast(F32), ALU.subtract).then_inc(S["ht_lo"], 1)
                t = i + 4
                if live(t):
                    dve.wait_ge(S["ct_hi"], t + 1)
                    wait(dve, S["kv_ps"], t)
                    dve.tensor_tensor(ct_l[:], bank[7][:], ct_h[:].bitcast(F32), ALU.subtract).then_inc(S["ct_lo"], 1)
                    dve.wait_ge(S["tile_loaded"], 16 * (t + 1))
                    dve.bn_stats(bn3[:], xn3[:]).then_inc(S["bn3_s"], 1)
                    wait_alone(dve, S["bn3_s"], t + 1, S["x_loaded"], 16)
                    dve.bn_aggr(mv3[:], bn3[:]).then_inc(S["mv3_s"], 1)
                t = i + 3
                if live(t):
                    wait(dve, S["pv_ps"], 2 * t)
                    dve.wait_ge(S["kv_s"], t + 1)
                    for b in range(2):
                        for h in range(2):
                            v = kv_sb[SEQ * b:SEQ * (b + 1), KVW:2 * KVW].rearrange("k (p h d) -> k p h d", p=PAIRS, h=2)
                            last = dve.tensor_copy(vbd[SEQ * h:SEQ * (h + 1), b, :, h, :], v[:, :, h, :])
                    last.then_inc(S["vbd_s"], 1)
                t = i + 2
                if live(t):
                    wait(dve, S["y_lo"], t)
                    for b in range(2):
                        part = bank[2 + b][:].rearrange("p (n g q) -> p n g q", n=2, g=GROUPS)
                        dve.wait_ge(S["pv_ps"], 2 * t + b + 1)
                        dve.reciprocal(y[:, :, b, :], part[:, 1]).then_inc(S["den_s"], 1)
                        dve.wait_ge(S["den_s"], 2 * t + b + 1)
                        dve.tensor_tensor(y[:, :, b, :], part[:, 0], y[:, :, b, :], ALU.mult).then_inc(S["y_s"], 1)
                t = i + 4
                if live(t):
                    dve.wait_ge(S["rs3_s"], t + 1)
                    dve.tensor_scalar(xn3[:], xn3[:], mv3[:, 0:1], rs3[:], ALU.subtract, ALU.mult
                                      ).then_inc(S["xn3_s"], 1)
                t = i + 1
                if live(t):
                    dve.wait_ge(S["gate_ps"], t + 1)
                    dve.tensor_reduce(logits[:], bank[0][:, 0:2 * EXPERTS].rearrange("p (a e) -> p e a", a=2),
                                      AX.X, ALU.add).then_inc(S["lg_s"], 1)
                    wait_alone(dve, S["lg_s"], t + 1, S["x_loaded"], 16)
                    dve.max(lg[:], logits[:]).then_inc(S["top_s"], 1)
                    dve.wait_ge(S["top_s"], t + 1)
                    wait(dve, S["routed_s"], t)
                    dve.tensor_tensor(rw[:], lg[:, 0:1], lg[:, 1:2], ALU.add).then_inc(S["rw_s"], 1)
                t = i + 2
                if live(t):
                    dve.wait_ge(S["wo_ps"], t + 1)
                    dve.wait_ge(S["x2b_s"], t + 1)
                    wait(dve, S["x3b_s"], t)
                    dve.tensor_tensor(x3[:], bank[2][:], x2_res[:], ALU.add).then_inc(S["x3_s"], 1)
                    dve.wait_ge(S["x3_s"], t + 1)
                    dve.bn_stats(bn4[:], x3[:]).then_inc(S["bn4_s"], 1)
                    wait_alone(dve, S["bn4_s"], t + 1, S["x_loaded"], 16)
                    dve.bn_aggr(mv4[:], bn4[:]).then_inc(S["mv4_s"], 1)
                t = i + 3
                if live(t):
                    wait(dve, S["gmt_ps"], t)
                    maxima(t, (0, 1))
                t = i + 2
                if live(t):
                    dve.wait_ge(S["rs4_s"], t + 1)
                    wait(dve, S["t4_ps"], t)
                    dve.tensor_scalar(xn4[:], x3[:], mv4[:, 0:1], rs4[:], ALU.subtract, ALU.mult
                                      ).then_inc(S["xn4_s"], 1)
                t = i
                if live(t):
                    dve.wait_ge(S["ht_hi"], 2 * t + 2)
                    dve.wait_ge(S["dn_ps"], 2 * t + 1)
                    dve.tensor_tensor(ht_l[:], bank[5][:], ht_h[:].bitcast(F32), ALU.subtract).then_inc(S["ht_lo"], 1)
                t = i + 3
                if live(t):
                    maxima(t, (2, 3))
                t = i + 4
                if live(t):
                    dve.wait_ge(S["kv_ps"], t + 1)
                    wait(dve, S["qkt_ps"], t)
                    dve.tensor_tensor(kv_sb[:], bank[2][:, 0:2 * KVW], bkv_all[:], ALU.add).then_inc(S["kv_s"], 1)
                    dve.wait_ge(S["qx_hi"], t + 1)
                    wait(dve, S["qy_ps"], t)
                    dve.tensor_tensor(xt_l[:], bank[5][:], xt_h[:].bitcast(F32), ALU.subtract).then_inc(S["qx_lo"], 1)
                t = i
                if live(t):
                    dve.wait_ge(S["dn_ps"], 2 * t + 2)
                    dve.wait_ge(S["routed_s"], t + 1)
                    wait(dve, S["out_stored"], 16 * t)
                    dve.tensor_tensor(z[:], bank[3][:], routed[:], ALU.add).then_inc(S["z_s"], 1)
                    dve.wait_ge(S["z_s"], t + 1)
                    dve.bn_stats(bn5[:], z[:]).then_inc(S["bn5_s"], 1)
                    wait_alone(dve, S["bn5_s"], t + 1, S["x_loaded"], 16)
                    dve.bn_aggr(mv5[:], bn5[:]).then_inc(S["mv5_s"], 1)
                t = i + 4
                if live(t):
                    dve.wait_ge(S["qy_ps"], t + 1)
                    wait(dve, S["qkt_ps"], t)
                    dve.tensor_tensor(q_sb[:].rearrange("p (g h d) -> p h g d", g=GROUPS, h=NKV),
                                      bank[0][:].rearrange("p (h g d) -> p h g d", g=GROUPS, h=NKV),
                                      bq_all[:].rearrange("p (h g d) -> p h g d", g=GROUPS, h=NKV), ALU.add
                                      ).then_inc(S["q_s"], 1)
                t = i
                if live(t):
                    dve.wait_ge(S["rs5_s"], t + 1)
                    dve.tensor_scalar(z[:], z[:], mv5[:, 0:1], rs5[:], ALU.subtract, ALU.mult).then_inc(S["zn_s"], 1)

            pass2_loop(dve, body2, lambda i: None)

        @block.tensor
        def _(pe):
            def split_product(out_ps, w_hi, w_lo, m_hi, m_lo, start, stop):
                pe.matmul(out_ps, w_hi, m_hi, start=start, stop=False)
                pe.matmul(out_ps, w_hi, m_lo, start=False, stop=False)
                return pe.matmul(out_ps, w_lo, m_hi, start=False, stop=stop)

            pe.wait_ge(S["const_in"], 16)
            pe.wait_ge(S["first_in"], 16)
            pe.wait_ge(S["dft_lo"], 1)

            def transform(out_ps, col, hi, lo):
                w = slice(col, col + P)
                return split_product(out_ps[:], dft_h[:, w], dft_l[:, w], hi[:], lo[:], True, True)

            def body(i):
                t = i + 2
                if live(t):
                    pe.wait_ge(S["x_lo"], t + 1)
                    wait(pe, S["vf_s"], 4 * t)
                    transform(bank[0], Q0, x_h, x_l).then_inc(S["q_ps"], 1)
                    pe.wait_ge(S["c_lo"], t + 1)
                    for j in range(2):
                        transform(bank[1 + j], K0 + P * j, c_h, c_l).then_inc(S["k_ps"], 1)
                t = i + 1
                if live(t):
                    pe.wait_ge(S["wt_lo"], t + 1)
                    wait(pe, S["vf_s"], min_tiles(4, t + 1))
                    transform(bank[W_BANK[0]], W0, wt_h, wt_l).then_inc(S["wf_ps"], 1)
                    wait(pe, S["qf_s"], min_tiles(1, t + 2))
                    transform(bank[W_BANK[1]], W0 + P, wt_h, wt_l).then_inc(S["wf_ps"], 1)
                t = i + 2
                if live(t):
                    pe.wait_ge(S["prod_s"], 2 * (t + 1))
                    wait(pe, S["rep_s"], t)
                    for c in range(DC):
                        k = slice(c * P, (c + 1) * P)
                        for j in range(2):
                            last = pe.matmul(bank[4][:, k], prod[:, j, k], icorr[j], start=(j == 0), stop=(j == 1))
                    last.then_inc(S["corr_ps"], 1)
                    for n in (0, 1):
                        transform(bank[V_BANK[n]], V0 + P * n, c_h, c_l).then_inc(S["v_ps"], 1)
                t = i
                if live(t):
                    pe.wait_ge(S["xn2_s"], t + 1)
                    wait(pe, S["wt_lo"], min_tiles(1, t + 2))
                    for c in range(DC):
                        last = pe.transpose(bank[5][:, c * P:(c + 1) * P], xn2[:, c * P:(c + 1) * P], ident)
                    last.then_inc(S["xt_ps"], 1)
                t = i + 2
                if live(t):
                    for n in (2, 3):
                        wait(pe, S["prod2_s"], min_tiles(4, t - 1) + 2 * (n - 1) if not isinstance(t, int) or t else 0)
                        transform(bank[V_BANK[n]], V0 + P * n, c_h, c_l).then_inc(S["v_ps"], 1)
                t = i + 1
                if live(t):
                    pe.wait_ge(S["prod2_s"], 4 * (t + 1))
                    wait(pe, S["x1_s"], t)
                    if isinstance(t, int) and t <= 1:
                        pe.wait_ge(*((S["rt_lo"], DC) if t else (S["w0_lo"], DC)))
                    for j in range(2):
                        for b in range(2):
                            last = pe.matmul(bank[6][SEQ * b:SEQ * (b + 1), :], iout[j], prod2[:, b, j, :],
                                             start=(j == 0), stop=(j == 1))
                    last.then_inc(S["o_ps"], 1)
                t = i
                if live(t):
                    pe.wait_ge(S["xt_lo"], t + 1)
                    wait(pe, S["x2_s"], t)
                    for c in range(DC):
                        k = slice(c * P, (c + 1) * P)
                        n = slice(c * D, (c + 1) * D)
                        last = split_product(bank[7][:], x1t_h[:, k], x1t_l[:, k], w0_h[:, n], w0_l[:, n],
                                             c == 0, c == DC - 1)
                    last.then_inc(S["ffn_ps"], 1)
                t = i + 2
                if live(t):
                    pe.wait_ge(S["wgt_s"], t + 1)
                    wait(pe, S["xt_lo"], min_tiles(1, t - 1))
                    for c in range(DC):
                        last = pe.transpose(bank[5][:, c * P:(c + 1) * P], wgt[:, c * P:(c + 1) * P], ident)
                    last.then_inc(S["wt_ps"], 1)

            def peeled(i):
                if i == -2:
                    pe.wait_ge(S["lora_in"], 16 * (2 + DC + ADAPT))
                    for c in range(DC):
                        last = pe.transpose(bank[6][:, c * P:(c + 1) * P], b_raw[:, c, :], ident)
                    last.then_inc(S["bt_ps"], 1)
                    pe.wait_ge(S["bt_ready"], 1)
                    for c in range(DC):
                        if c >= 2:
                            pe.wait_ge(S["w0_lo"], c - 1)
                        ps = bank[6 + c % 2]
                        for o in range(DC):
                            pe.matmul(ps[:, o * P:(o + 1) * P], w0_raw[:, o, c * P:(c + 1) * P], ident,
                                      start=(o == 0), stop=False, skip_group_check=True)
                        pe.matmul(ps[:], a_raw[:, c * P:(c + 1) * P], b_t[:], start=False, stop=True,
                                  skip_group_check=True).then_inc(S["w0_ps"], 1)
                if i == -1:
                    pe.wait_ge(S["merge_in"], 64)
                    pe.wait_ge(S["w0_lo"], DC)
                    pe.wait_ge(S["x1_s"], 1)
                    for m in range(2):
                        for c in range(2):
                            last = pe.transpose(bank[7][:, LAT * m + P * c:LAT * m + P * (c + 1)],
                                                ex_raw[:, c, P * m:P * (m + 1)], ident)
                    last.then_inc(S["ext_ps"], 1)
                    pe.wait_ge(S["ext_ready"], 1)
                    for c in range(2):
                        for m in range(2):
                            last = pe.matmul(bank[6 + c][:], ex_t[:, m, P * c:P * (c + 1)], fc2_raw[:, m, :],
                                             start=(m == 0), stop=(m == 1))
                        last.then_inc(S["ef_ps"], 1)
                    for c in range(2):
                        pe.wait_ge(S["ef_ready"], c + 1)
                        for k in range(DC):
                            last = pe.transpose(bank[6 + c][:, P * k:P * (k + 1)], fc1_raw[:, k, P * c:P * (c + 1)], ident)
                        last.then_inc(S["fct_ps"], 1)
                    pe.wait_ge(S["fct_ready"], 2)
                    for c in range(DC):
                        if c >= 2:
                            pe.wait_ge(S["rt_lo"], c - 1)
                        for k in range(2):
                            last = pe.matmul(bank[6 + c % 2][:], fc1_t[:, k, P * c:P * (c + 1)], ex_fc2[:, k, :],
                                             start=(k == 0), stop=(k == 1))
                        last.then_inc(S["rt_ps"], 1)

            pass1_loop(pe, body, peeled)
            pe.wait_ge(S["x2_stored"], 16 * NT)
            pe.wait_ge(S["stage_lo"], 2 * len(WEIGHTS))

            def cols(w, c, n):
                return w[:, c * n:(c + 1) * n]

            def capped(n, t):
                return n * (min(max(t, 0), NT) if isinstance(t, int) else t)

            def body2(i):
                t = i + 1
                if live(t):
                    pe.wait_ge(S["xn4_s"], t + 1)
                    wait(pe, S["routed_s"], t)
                    for c in range(DC):
                        last = pe.transpose(cols(bank[4], c, P), cols(xn4, c, P), ident)
                    last.then_inc(S["t4_ps"], 1)
                t = i + 3
                if live(t):
                    pe.wait_ge(S["q_s"], t + 1)
                    pe.wait_ge(S["kv_s"], t + 1)
                    wait(pe, S["ngm_s"], t)
                    for g in range(GROUPS):
                        pe.transpose(cols(bank[0], g, P), cols(q_sb, g, P), ident)
                    pe.transpose(bank[1][:, 0:P], kv_sb[:, 0:KVW], ident).then_inc(S["qkt_ps"], 1)
                t = i
                if live(t):
                    pe.wait_ge(S["h_s"], t + 1)
                    wait(pe, S["qx_lo"], capped(1, t + 4))
                    for c in range(DC):
                        last = pe.transpose(cols(bank[5], c, P), cols(act2, c, P), ident)
                    last.then_inc(S["ht_ps"], 1)
                t = i + 4
                if live(t):
                    pe.wait_ge(S["ctx2_loaded"], 16 * (t + 1))
                    wait(pe, S["probs_s"], 2 * (t - 1))
                    for c in range(DC):
                        last = pe.transpose(cols(bank[7], c, P), cols(ctx2, c, P), ident)
                    last.then_inc(S["ct_ps"], 1)
                t = i + 2
                if live(t):
                    pe.wait_ge(S["vbd_s"], t + 1)
                    wait(pe, S["kv_s"], capped(1, t + 2))
                    wait(pe, S["z_s"], t - 2)
                    for b in range(2):
                        pe.wait_ge(S["probs_s"], 2 * t + b + 1)
                        for n in range(2):
                            for p in range(PAIRS):
                                lhs = ones_bd if n else vbd[:, b, p].rearrange("k h d -> k (h d)")
                                last = pe.matmul(bank[2 + b][32 * p:32 * (p + 1), 256 * n:256 * (n + 1)], lhs,
                                                 probs[:, b, p, :], start=True, stop=True)
                        last.then_inc(S["pv_ps"], 1)
                t = i + 1
                if live(t):
                    pe.wait_ge(S["t4_lo"], t + 1)
                    wait(pe, S["probs_s"], capped(2, t + 2))
                    for n in range(2):
                        if n == 1:
                            wait(pe, S["ct_lo"], capped(1, t + 4))
                        for c in range(DC):
                            w = slice(INNER * c + D * n, INNER * c + D * (n + 1))
                            last = split_product(bank[6 + n][:], cols(t4_h, c, P), cols(t4_l, c, P),
                                                 up_h[:, w], up_l[:, w], c == 0, c == DC - 1)
                        last.then_inc(S["u_ps"], 1)
                    wait(pe, S["qt_lo"], capped(1, t + 3))
                    wait(pe, S["qt_bs"], capped(1, t + 3))
                    for c in range(DC):
                        pe.matmul(bank[0][:, 0:2 * EXPERTS], cols(t4_h, c, P),
                                  gate_hl[:, c].rearrange("p a e -> p (a e)"), start=(c == 0), stop=False,
                                  skip_group_check=True)
                        last = pe.matmul(bank[0][:, 0:EXPERTS], cols(t4_l, c, P), gate_hl[:, c, 0, :],
                                         start=False, stop=(c == DC - 1), skip_group_check=True)
                    last.then_inc(S["gate_ps"], 1)
                def rough_scores(t, g):
                    for b in range(2):
                        last = pe.matmul(bank[g % 2][SEQ * b:SEQ * (b + 1), :],
                                         qt_b[:, P * g + SEQ * b:P * g + SEQ * (b + 1)], kbd_b[:, b, :],
                                         start=True, stop=True)
                    last.then_inc(S["g_ps"], 1)

                def down(t, part):
                    for c in range(DC):
                        last = split_product(bank[3][:], cols(ht_h, c, P), cols(ht_l, c, P),
                                             cols(down_h, DC * part + c, D), cols(down_l, DC * part + c, D),
                                             part == 0 and c == 0, part == 1 and c == DC - 1)
                    last.then_inc(S["dn_ps"], 1)

                t = i
                if live(t):
                    if isinstance(t, int) and t == 0:
                        pe.wait_ge(S["stage2_lo"], 2)
                    pe.wait_ge(S["ht_lo"], 2 * t + 1)
                    wait(pe, S["y_s"], capped(2, t + 3))
                    down(t, 0)
                t = i + 2
                if live(t):
                    pe.wait_ge(S["y_lo"], t + 1)
                    for g in range(GROUPS):
                        last = split_product(bank[2][:], cols(y_h, g, P), cols(y_l, g, P),
                                             cols(wo_h, g, D), cols(wo_l, g, D), g == 0, g == GROUPS - 1)
                    last.then_inc(S["wo_ps"], 1)
                t = i + 3
                if live(t):
                    pe.wait_ge(S["kbd_s"], 6 * t + 2)
                    pe.wait_ge(S["qt_bs"], t + 1)
                    pe.wait_ge(S["qt_lo"], t + 1)
                    wait(pe, S["lg_s"], t - 1)
                    pe.wait_ge(S["kt_lo"], t + 1)
                    for g in (0, 1):
                        rough_scores(t, g)
                t = i
                if live(t):
                    for c in range(DC):
                        last = pe.transpose(cols(bank[5], c, P), cols(act2, DC + c, P), ident)
                    last.then_inc(S["ht_ps"], 1)
                t = i + 1
                if live(t):
                    for c in range(DC):
                        last = split_product(bank[4][:], cols(t4_h, c, P), cols(t4_l, c, P),
                                             cols(rt_h, c, D), cols(rt_l, c, D), c == 0, c == DC - 1)
                    last.then_inc(S["rt_out_ps"], 1)
                t = i + 3
                if live(t):
                    for g in (2, 3):
                        pe.wait_ge(S["gmax_s"], 4 * t + g - 1)
                        rough_scores(t, g)
                t = i + 4
                if live(t):
                    pe.wait_ge(S["ct_lo"], t + 1)
                    wait(pe, S["x3_s"], t - 1)
                    for c in range(DC):
                        last = split_product(bank[2][:, 0:2 * KVW], cols(ct_h, c, P), cols(ct_l, c, P),
                                             cols(wkv_h, c, 2 * KVW), cols(wkv_l, c, 2 * KVW), c == 0, c == DC - 1)
                    last.then_inc(S["kv_ps"], 1)
                    pe.wait_ge(S["xn3_s"], t + 1)
                    wait(pe, S["ht_lo"], 2 * (t - 3))
                    for c in range(DC):
                        last = pe.transpose(cols(bank[5], c, P), cols(xn3, c, P), ident)
                    last.then_inc(S["qx_ps"], 1)
                t = i + 3
                if live(t):
                    pe.wait_ge(S["gmax_s"], 4 * t + 4)
                    for g in range(GROUPS):
                        last = pe.transpose(bank[1][0:NKV, P * g:P * (g + 1)], cols(gmax, g, NKV), ident)
                    last.then_inc(S["gmt_ps"], 1)
                t = i
                if live(t):
                    pe.wait_ge(S["ht_lo"], 2 * t + 2)
                    down(t, 1)

                def scores(t, b):
                    for p in range(PAIRS):
                        ps = wide[:, 256 * p:256 * (p + 1)]
                        k = slice(P * p, P * (p + 1))
                        by_group = lambda a: a[:].rearrange("r (g b q) -> r g b q", g=GROUPS, b=2)[:, :, b, :]
                        split_product(ps, kbd_h[:, b, k], kbd_l[:, b, k], by_group(qt_h), by_group(qt_l), True, False)
                        last = pe.matmul(ps, selb[:, k], by_group(ngm), start=False, stop=True)
                    last.then_inc(S["s_ps"], 1)

                t = i + 3
                if live(t):
                    pe.wait_ge(S["kbd_s"], 6 * t + 6)
                    pe.wait_ge(S["qt_lo"], t + 1)
                    pe.wait_ge(S["ngm_s"], t + 1)
                    wait(pe, S["relu_s"], 2 * (t - 1))
                    scores(t, 0)
                t = i + 4
                if live(t):
                    pe.wait_ge(S["qx_lo"], t + 1)
                    wait(pe, S["gmax_s"], 4 * t)
                    for c in range(DC):
                        last = split_product(bank[0][:], cols(xt_h, c, P), cols(xt_l, c, P),
                                             cols(wq_h, c, D), cols(wq_l, c, D), c == 0, c == DC - 1)
                    last.then_inc(S["qy_ps"], 1)
                t = i + 3
                if live(t):
                    pe.wait_ge(S["probs_s"], 2 * t + 1)
                    scores(t, 1)

            pass2_loop(pe, body2, lambda i: None)


_INS = ["x", "ctx_4096", "L0_ffn_lora_A", "L0_ffn_lora_B", "L0_ffn_W", "L0_ffn_bias", "L0_ffn_lora_weights",
        "L1_xattn_Wq", "L1_xattn_bq", "L1_xattn_Wk", "L1_xattn_bk", "L1_xattn_Wv", "L1_xattn_bv",
        "L1_xattn_Wo", "L1_xattn_bo", "L1_ffn_gate_w", "L1_ffn_up_w", "L1_ffn_down_w", "L1_ffn_fc1_w",
        "L1_ffn_fc2_w", "L1_ffn_expert_w", "L1_ffn_ln_gamma", "L1_ffn_ln_beta"]


def kernel(**inputs):
    import numpy as _np
    import concourse.bacc as _bacc
    from concourse import mybir as _mybir
    from concourse.bass_utils import run_bass_kernel_spmd as _run

    nc = _bacc.Bacc("TRN2", target_bir_lowering=False, num_devices=1)
    arrays, args = {}, []
    dft, small = constants()
    named = [(name, _np.ascontiguousarray(inputs[name])) for name in _INS] + [("dft", dft), ("small", small)]
    for name, a in named:
        arrays[f"in_{name}"] = a
        args.append(nc.dram_tensor(f"in_{name}", a.shape, _mybir.dt.from_np(a.dtype), kind="ExternalInput").ap())
    out = nc.dram_tensor("out", (BATCHES, SEQ, D), _mybir.dt.float32, kind="ExternalOutput").ap()
    build(nc, *args, out)
    return _run(nc, [arrays], core_ids=[0]).results[0]["out"]
```

```python
from contextlib import ExitStack

import concourse.bass as bass
import numpy as np
from concourse import mybir

ALU = mybir.AluOpType
ACT = mybir.ActivationFunctionType
AX = mybir.AxisListType
F32 = mybir.dt.float32
F32R = mybir.dt.float32r
BF16 = mybir.dt.bfloat16

P = 128
BATCHES, SEQ, D = 32, 64, 512
TOKENS = BATCHES * SEQ
NT = TOKENS // P
DC = D // P
TOP = 8
ADAPT, RANK = 8, 16
LORA_SCALE = 32 / RANK
NKV, GROUPS, HD = 8, 4, 16
KVW = NKV * HD
PAIRS = NKV // 2
INNER, LAT, EXPERTS = 1024, 256, 8
IC = INNER // P
EPS = 1e-5
REMOVED = -3.0e38
REMOVED_BELOW = -1.0e38

Q0, K0, V0, W0, DFT = 0, P, 3 * P, 5 * P, 7 * P
ICORR0, IOUT0, FIRST = 0, 256, 384
IDENT0, HEAD0, PAIR0, ONES0, HALF0, EPS0, MINUS0, SEL0 = 384, 512, 520, 522, 554, 555, 556, 557
SMALL = SEL0 + PAIRS * P
STACK = 2 * HD
GUARD = 3 * STACK


def transform(n, inputs, swapped):
    h = n // 2
    m = np.zeros((inputs, n))
    s = np.arange(inputs)
    for f in range(h + 1):
        m[:, f] = np.cos(2 * np.pi * ((f * s) % n) / n)
    for f in range(1, h):
        m[:, h + f] = -np.sin(2 * np.pi * ((f * s) % n) / n)
    return np.roll(m, h, axis=1) if swapped else m


def inverse(n, outputs, swapped, sign=0):
    h = n // 2
    m = np.zeros((n, outputs))
    s = np.arange(outputs)
    for f in range(h + 1):
        weight = (1.0 if f in (0, h) else 2.0) / n
        angle = 2 * np.pi * ((f * s) % n) / n
        if not swapped:
            m[f] = weight * np.cos(angle)
            if 0 < f < h:
                m[h + f] = weight * np.cos(angle)
        elif 0 < f < h:
            m[f], m[h + f] = sign * weight * np.sin(angle), -sign * weight * np.sin(angle)
    return m


def constants():
    dft = np.zeros((P, DFT))
    ends = lambda m: np.concatenate([m[:SEQ - 1], m[SEQ - 1:].sum(0, keepdims=True)])
    small = np.zeros((P, SMALL))
    for b in range(2):
        rows = slice(SEQ * b, SEQ * b + SEQ)
        dft[rows, Q0 + SEQ * b:Q0 + SEQ * (b + 1)] = transform(SEQ, SEQ, False)
        for j in range(2):
            dft[rows, K0 + P * j + SEQ * b:K0 + P * j + SEQ * (b + 1)] = transform(SEQ, SEQ, j)
            small[rows, ICORR0 + P * j + SEQ * b:ICORR0 + P * j + SEQ * (b + 1)] = inverse(SEQ, SEQ, j, 1)
        dft[rows, V0 + P * b:V0 + P * (b + 1)] = ends(transform(2 * SEQ, 2 * SEQ - 1, False))
        dft[rows, W0 + P * b:W0 + P * (b + 1)] = transform(2 * SEQ, SEQ, False)
    for j in range(2):
        small[:, IOUT0 + SEQ * j:IOUT0 + SEQ * (j + 1)] = inverse(2 * SEQ, SEQ, j, -1)
    small[:, IDENT0:IDENT0 + P] = np.eye(P)
    small[:, HEAD0:HEAD0 + NKV] = np.repeat(np.eye(NKV), HD, axis=0)
    small[:, ONES0:ONES0 + 2 * HD] = np.kron(np.eye(2), np.ones((SEQ, HD)))
    for p in range(PAIRS):
        for h in range(2):
            small[GUARD + 2 * p + h, SEL0 + P * p + SEQ * h:SEL0 + P * p + SEQ * (h + 1)] = 1.0
    small[:, PAIR0:PAIR0 + 2] = np.tile(np.repeat(np.eye(2), HD, axis=0), (PAIRS, 1))
    small[:, HALF0], small[:, EPS0], small[:, MINUS0] = -0.5, EPS, -1.0
    return dft.astype(np.float32), small.astype(np.float32)


def wait(eng, sem, value):
    if not (isinstance(value, int) and value <= 0):
        eng.wait_ge(sem, value)


def build(nc, x, ctx_in, lora_a, lora_b, w0, b0, lora_w, wq, bq, wk, bk, wv, bv, wo, bo,
          gate_w, up_w, down_w, fc1_w, fc2_w, expert_w, gamma, beta, dft_in, small_in, out):
    x_rows = x.rearrange("b s d -> (b s) d")
    ctx_rows = ctx_in.rearrange("b s d -> (b s) d")
    out_rows = out.rearrange("b s d -> (b s) d")
    x2_rows = nc.dram_tensor("x2_rows", [TOKENS, D], F32, kind="Internal").ap()

    with ExitStack() as ctx:
        def sb(name, shape, dt=F32, stack=ctx):
            return stack.enter_context(nc.sbuf_tensor(name, shape, dt))

        def sem(name):
            return ctx.enter_context(nc.semaphore(name))

        bank = [ctx.enter_context(nc.psum_tensor(f"bank{i}", [P, 512], F32)) for i in range(6)]
        wide = ctx.enter_context(nc.psum_tensor("wide", [P, 1024], F32))
        bank += [wide[:, 0:512], wide[:, 512:1024]]

        small = sb("small", [P, SEL0 - FIRST])
        ident = small[:, IDENT0 - FIRST:IDENT0 - FIRST + P]
        head_of = small[:, HEAD0 - FIRST:HEAD0 - FIRST + NKV]
        head_of_pair = small[:, PAIR0 - FIRST:PAIR0 - FIRST + 2]
        ones_bd = small[:, ONES0 - FIRST:ONES0 - FIRST + 2 * HD]
        half, eps, minus = (small[:, c - FIRST:c - FIRST + 1] for c in (HALF0, EPS0, MINUS0))
        bq_all = sb("bq_all", [P, D])
        bkv_all = sb("bkv_all", [P, 2 * KVW])
        bo_all = sb("bo_all", [P, D])
        gamma_all = sb("gamma_all", [P, D])
        beta_all = sb("beta_all", [P, D])
        wq_h, wq_l = sb("wq_h", [P, DC * D], F32R), sb("wq_l", [P, DC * D], F32R)
        wkv_h, wkv_l = sb("wkv_h", [P, DC * 2 * KVW], F32R), sb("wkv_l", [P, DC * 2 * KVW], F32R)
        wo_h, wo_l = sb("wo_h", [P, DC * D], F32R), sb("wo_l", [P, DC * D], F32R)
        rt_h, rt_l = sb("rt_h", [P, DC * D], F32R), sb("rt_l", [P, DC * D], F32R)
        gate_hl = sb("gate_hl", [P, DC, 2, EXPERTS], F32R)
        with ExitStack() as tmp:
            w0_raw = sb("w0_raw", [P, DC, D], stack=tmp)
            a_raw = sb("a_raw", [P, D], stack=tmp)
            b_raw = sb("b_raw", [P, DC, P], stack=tmp)
            b_t = sb("b_t", [P, D], stack=tmp)
            ex_raw = sb("ex_raw", [P, 2, LAT], stack=tmp)
            ex_t = sb("ex_t", [P, 2, LAT], stack=tmp)
            fc2_raw = sb("fc2_raw", [P, 2, D], stack=tmp)
            ex_fc2 = sb("ex_fc2", [P, 2, D], stack=tmp)
            fc1_raw = sb("fc1_raw", [P, DC, LAT], stack=tmp)
            fc1_t = w0_raw[:, 0:2, :]
            gate_raw = sb("gate_raw", [P, DC, EXPERTS], stack=tmp)
        up_h, up_l = sb("up_h", [P, DC * INNER], F32R), sb("up_l", [P, DC * INNER], F32R)

        x_in, ctx_t = sb("x_in", [P, D]), sb("ctx_t", [P, D])
        x_h, x_l = sb("x_h", [P, D], F32R), sb("x_l", [P, D], F32R)
        c_h, c_l = sb("c_h", [P, D], F32R), sb("c_l", [P, D], F32R)
        xn1, qf, x2 = sb("xn1", [P, D]), sb("qf", [P, D]), sb("x2", [P, D])
        xn3, ctx2, ct_h, ct_l, xt_h, xt_l = x_in, ctx_t, c_h, c_l, x_h, x_l
        kv_sb, q_sb = xn1[:, 0:2 * KVW], qf
        bn3, mv3, va3, rs3 = (sb(n, [P, w]) for n, w in (("bn3", 6), ("mv3", 2), ("va3", 1), ("rs3", 1)))

        pass1 = ExitStack()
        one = lambda name, shape, dt=F32: sb(name, shape, dt, pass1)
        stage = [one(f"stage{i}", [P, 2048]) for i in range(1)]
        dft_h, dft_l = one("dft_h", [P, DFT], F32R), one("dft_l", [P, DFT], F32R)
        w0_h, w0_l = one("w0_h", [P, DC * D], F32R), one("w0_l", [P, DC * D], F32R)
        b0_all = one("b0_all", [P, D])
        first = one("first", [P, FIRST])
        icorr = [first[:, ICORR0 + P * j:ICORR0 + P * (j + 1)] for j in range(2)]
        iout = [first[:, IOUT0 + SEQ * j:IOUT0 + SEQ * (j + 1)] for j in range(2)]
        coef, coef_scaled = one("coef", [P, 1]), one("coef_scaled", [P, 1])
        prod = one("prod", [P, 2, D])
        m8 = one("m8", [P, 2 * DC, TOP])
        kept_not = one("kept_not", [P, 2 * DC, SEQ])
        shifted = one("shifted", [P, 2 * DC, SEQ + TOP])
        total, total_inv = one("total", [P, 2 * DC]), one("total_inv", [P, 2 * DC])
        wgt = one("wgt", [P, 2 * DC * SEQ])
        wt_h, wt_l = one("wt_h", [P, D], F32R), one("wt_l", [P, D], F32R)
        vf = one("vf", [P, 2, 2, D])
        prod2 = one("prod2", [P, 2, 2, D])
        x_res, x1 = one("x_res", [P, D]), one("x1", [P, D])
        x1b = one("x1b", [P, D])
        xn2 = one("xn2", [P, D])
        x1t_h, x1t_l = one("x1t_h", [P, D], F32R), one("x1t_l", [P, D], F32R)
        bn1, mv1, va1, rs1 = one("bn1", [P, 6]), one("mv1", [P, 2]), one("va1", [P, 1]), one("rs1", [P, 1])
        nm1, nb1, nm2, nb2 = (one(n, [P, 1]) for n in ("nm1", "nb1", "nm2", "nb2"))
        bn2, mv2, va2, rs2 = one("bn2", [P, 6]), one("mv2", [P, 2]), one("va2", [P, 1]), one("rs2", [P, 1])
        pass1.close()

        down_h, down_l = sb("down_h", [P, IC * D], F32R), sb("down_l", [P, IC * D], F32R)
        qt_h, qt_l = sb("qt_h", [P, D], F32R), sb("qt_l", [P, D], F32R)
        qt_b = sb("qt_b", [P, D], BF16)
        kt_h, kt_l = sb("kt_h", [P, P], F32R), sb("kt_l", [P, P], F32R)
        k_pairs = x2[0:GUARD].rearrange("r (p n) -> r p n", p=PAIRS)
        k_stack = sb("k_stack", [P, PAIRS, 2, P], F32R)
        q_stack = sb("q_stack", [P, PAIRS, D], F32R)
        kbd_b = sb("kbd_b", [P, 2, D], BF16)
        gmax = sb("gmax", [P, GROUPS * NKV])
        probs = sb("probs", [P, 2, PAIRS, GROUPS * SEQ])
        zero_col = sb("zero_col", [P, 1])
        vbd = sb("vbd", [P, 2, PAIRS, 2, HD])
        with ExitStack() as tmp:
            y = sb("y", [P, GROUPS, 2, SEQ], stack=tmp)
        y_l = sb("y_l", [P, D], F32R)
        y_flat = y[:].rearrange("p g b q -> p (g b q)")
        y_h = sb("y_h", [P, D], F32R)
        x2_res, x3, x3b, x3c, xn4 = (sb(n, [P, D]) for n in ("x2_res", "x3", "x3b", "x3c", "xn4"))
        t4_h, t4_l = sb("t4_h", [P, D], F32R), sb("t4_l", [P, D], F32R)
        logits, lg, rw = sb("logits", [P, EXPERTS]), sb("lg", [P, TOP]), sb("rw", [P, 1])
        stage2 = sb("stage2", [P, INNER + 2 * D])
        act2, routed, z = stage2[:, 0:INNER], stage2[:, INNER:INNER + D], stage2[:, INNER + D:]
        ht_h, ht_l = sb("ht_h", [P, D], F32R), sb("ht_l", [P, D], F32R)
        bn4, mv4, va4, rs4 = (sb(n, [P, w]) for n, w in (("bn4", 6), ("mv4", 2), ("va4", 1), ("rs4", 1)))
        bn5, mv5, va5, rs5 = (sb(n, [P, w]) for n, w in (("bn5", 6), ("mv5", 2), ("va5", 1), ("rs5", 1)))

        SEMS = """stage2_in stage2_hi stage2_lo vbd_zero
            tile_loaded ctx2_loaded res2_loaded out_stored
            bn3_s mv3_s va3_s rs3_s xn3_s bn4_s mv4_s va4_s rs4_s xn4_s bn5_s mv5_s va5_s rs5_s zn_s
            ct_ps ct_hi ct_lo kv_ps kv_s qx_ps qx_hi qx_lo qy_ps q_s
            sel_in sel_s qs_s kp_s qkt_ps kt_hi kt_lo qt_hi qt_lo qt_bs kbd_s vbd_s g_ps gmax_s gmt_ps ngm_s s_ps probs_s
            pv_ps den_s y_s y_hi y_lo wo_ps x2b_s x3_s x3b_s x3c_s
            t4_ps t4_hi t4_lo u_ps relu_s h_s gate_ps lg_s top_s rw_s rt_out_ps routed_s
            ht_ps ht_hi ht_lo dn_ps z_s zg_s o_s
            const_in dft_loaded first_in merge_in lora_in bcast_in stage_in dft_hi dft_lo  gate_split
            bt_ps coef_ready bt_ready ext_ps ext_ready ef_ps ef_ready w0_ps w0_hi w0_lo rt_ps rt_hi rt_lo
            fct_ps fct_ready stage_hi stage_lo
            nm1_s nb1_s nm2_s nb2_s x_loaded ctx_loaded res_loaded bn1_s mv1_s va1_s rs1_s xn1_s x_hi x_lo c_hi c_lo
            q_ps qf_s k_ps prod_s v_ps vf_s corr_ps tops_s rep_s shift_s exp_s mask_s sum_s inv_s wgt_s
            wt_ps wt_hi wt_lo wf_ps prod2_s o_ps x1_s bn2_s mv2_s va2_s rs2_s xn2_s x1b_s
            xt_ps xt_hi xt_lo ffn_ps x2_s x2_stored""".split()
        S = {name: sem(name) for name in SEMS}

        block = ctx.enter_context(nc.Block())

        def rows(dram, t):
            return dram[bass.ts(t, P), :]

        LEAD, PEELED = 3, 4

        def pass1_loop(eng, body, peeled=lambda i: None):
            for i in range(-LEAD, PEELED):
                body(i)
                peeled(i)
            with eng.Fori(PEELED, NT - LEAD - 1) as i:
                body(i)
            for i in range(NT - LEAD - 1, NT + 1):
                body(i)
                peeled(i)

        W_BANK, V_BANK = (3, 0), (1, 2)

        def live(t):
            return not isinstance(t, int) or 0 <= t < NT

        def min_tiles(n, t):
            return n * (min(t, NT) if isinstance(t, int) else t)

        LEAD2 = 4
        EARLY = NT - 2

        def early(i, later=0):
            return isinstance(i, int) and i == EARLY + later

        def turned_bank(t, bank_of_ctx):
            first_tile = isinstance(t, int) and t == 0
            return bank[(1 if first_tile else 7) if bank_of_ctx else (4 if first_tile else 5)]

        def down_staged(i):
            return isinstance(i, int) and i < 3 - LEAD2

        def pass2_loop(eng, body, peeled=lambda i: None):
            for i in range(1 - LEAD2, 2):
                body(i)
                peeled(i)
            with eng.Fori(2, NT - LEAD2) as i:
                body(i)
            for i in range(NT - LEAD2, NT + 1):
                body(i)

        wo_v = wo.rearrange("(h g d) n -> h d g n", h=NKV, g=GROUPS)
        up_v = up_w.rearrange("(c p) n -> p c n", p=P)
        down_v = down_w.rearrange("(c p) n -> p c n", p=P)
        stage3 = stage[0][:].rearrange("p (c n) -> p c n", c=DC)
        stage_kv = stage[0][:, 0:DC * 2 * KVW].rearrange("p (c n) -> p c n", c=DC)
        stage_up = stage[0][:].rearrange("p (c n) -> p c n", c=2)
        half_up = DC * INNER // 2
        WEIGHTS = {
            -2: ([(stage3, wq.rearrange("(c p) n -> p c n", p=P))], wq_h[:], wq_l[:]),
            -1: ([(stage3[HD * h:HD * (h + 1)], wo_v[h]) for h in range(NKV)], wo_h[:], wo_l[:]),
            0: ([(stage_kv[:, :, 0:KVW], wk.rearrange("(c p) n -> p c n", p=P)),
                 (stage_kv[:, :, KVW:2 * KVW], wv.rearrange("(c p) n -> p c n", p=P))], wkv_h[:], wkv_l[:]),
            1: ([(stage_up, up_v[:, 0:2, :])], up_h[:, 0:half_up], up_l[:, 0:half_up]),
            2: ([(stage_up, up_v[:, 2:4, :])], up_h[:, half_up:], up_l[:, half_up:]),
        }
        STAGED = {i: n + 1 for n, i in enumerate(WEIGHTS)}
        LANDED = {i: 16 * sum(len(w[0]) for k, w in WEIGHTS.items() if k <= i) for i in WEIGHTS}

        def staged_before(i):
            return isinstance(i, int) and i - 1 in WEIGHTS


        @block.sync
        def _(sp):
            sp.dma_start(small[:], small_in[:, FIRST:SEL0]).then_inc(S["const_in"], 16)
            sp.dma_start(x_in[:], rows(x_rows, 0)).then_inc(S["x_loaded"], 16)
            sp.dma_start(stage[0][:, 0:DFT], dft_in).then_inc(S["dft_loaded"], 16)
            sp.dma_start(ctx_t[:], rows(ctx_rows, 0)).then_inc(S["ctx_loaded"], 16)
            sp.dma_start(first[:], small_in[:, 0:FIRST]).then_inc(S["first_in"], 16)

            def load2(t):
                if live(t):
                    if isinstance(t, int) and t < 2:
                        sp.wait_ge(S["x2_stored"], 16 * (t + 1))
                        sp.wait_ge(S["x_hi"], NT)
                        sp.wait_ge(S["c_lo"], NT)
                    wait(sp, S["qx_ps"], t)
                    sp.dma_start(xn3[:], rows(x2_rows, t)).then_inc(S["tile_loaded"], 16)
                    wait(sp, S["ct_ps"], t)
                    sp.dma_start(ctx2[:], rows(ctx_rows, t)).then_inc(S["ctx2_loaded"], 16)

            def body(i):
                if early(i):
                    load2(0)
                t = i + 1
                if live(t):
                    wait(sp, S["x1_s"], t)
                    sp.dma_start(x_res[:], rows(x_rows, t)).then_inc(S["res_loaded"], 16)
                t = i - 1
                if live(t):
                    sp.wait_ge(S["x2_s"], t + 1)
                    sp.dma_start(rows(x2_rows, t), x2[:]).then_inc(S["x2_stored"], 16)
                if early(i, 1):
                    load2(1)
                t = i + 4
                if live(t):
                    sp.wait_ge(S["x_hi"], t)
                    sp.dma_start(x_in[:], rows(x_rows, t)).then_inc(S["x_loaded"], 16)
                if isinstance(i, int) and i in WEIGHTS:
                    sp.wait_ge(S["dft_lo"], 1)
                    wait(sp, S["stage_lo"], 2 * (STAGED[i] - 1))
                    for tile, dram in WEIGHTS[i][0]:
                        sp.dma_start(tile, dram).then_inc(S["stage_in"], 16)
                t = i + 4
                if live(t):
                    sp.wait_ge(S["c_lo"], t)
                    sp.dma_start(ctx_t[:], rows(ctx_rows, t)).then_inc(S["ctx_loaded"], 16)

            def peeled(i):
                if i == -3:
                    sp.dma_start(w0_raw[:], w0.rearrange("(c p) d -> p c d", p=P)).then_inc(S["lora_in"], 16)
                    sp.dma_start(a_raw[:], lora_a.rearrange("n r d -> (n r) d")).then_inc(S["lora_in"], 16)
                    for c in range(DC):
                        sp.dma_start(b_raw[:, c, :].rearrange("p (n r) -> p n r", n=ADAPT),
                                     lora_b[:, c * P:(c + 1) * P, :].rearrange("n o r -> o n r")
                                     ).then_inc(S["lora_in"], 16)
                    for n in range(ADAPT):
                        sp.dma_start(coef[n * RANK:(n + 1) * RANK, :],
                                     lora_w[n:n + 1].rearrange("(a b) -> a b", a=1).to_broadcast([RANK, 1])
                                     ).then_inc(S["lora_in"], 16)
                    sp.dma_start(b0_all[:], b0.rearrange("(a n) -> a n", a=1).to_broadcast([P, D])
                                 ).then_inc(S["bcast_in"], 16)
                if i == -2:
                    sp.dma_start(ex_raw[:], expert_w.rearrange("(c p) n -> p c n", p=P)).then_inc(S["merge_in"], 16)
                    sp.dma_start(fc2_raw[:], fc2_w.rearrange("(c p) n -> p c n", p=P)).then_inc(S["merge_in"], 16)
                    sp.dma_start(fc1_raw[:], fc1_w.rearrange("(c p) n -> p c n", p=P)).then_inc(S["merge_in"], 16)
                    sp.dma_start(gate_raw[:], gate_w.rearrange("(c p) n -> p c n", p=P)).then_inc(S["merge_in"], 16)
                    for tile, dram in ((bq_all[:], bq), (bkv_all[:, 0:KVW], bk), (bkv_all[:, KVW:2 * KVW], bv),
                                       (bo_all[:], bo), (gamma_all[:], gamma), (beta_all[:], beta)):
                        sp.dma_start(tile, dram.rearrange("(a n) -> a n", a=1).to_broadcast([P, tile.shape[1]])
                                     ).then_inc(S["bcast_in"], 16)


            pass1_loop(sp, body, peeled)

            def body2(i):
                if not isinstance(i, int) or i + 4 >= 2:
                    load2(i + 4)
                t = i + 2
                if live(t):
                    wait(sp, S["x3_s"], t)
                    if isinstance(t, int) and t == 0:
                        sp.wait_ge(S["sel_s"], 3)
                    sp.dma_start(x2_res[:], rows(x2_rows, t)).then_inc(S["res2_loaded"], 16)
                t = i - 1
                if live(t):
                    sp.wait_ge(S["o_s"], t + 1)
                    sp.dma_start(rows(out_rows, t), z[:]).then_inc(S["out_stored"], 16)

            def peeled2(i):
                if i == 1 - LEAD2:
                    sp.wait_ge(S["x2_stored"], 16 * NT)
                    sp.wait_ge(S["stage_lo"], 2 * len(WEIGHTS))
                    sp.dma_start(x2_res[GUARD:, :], small_in[GUARD:, SEL0:SMALL]).then_inc(S["sel_in"], 16)
                if down_staged(i):
                    c = i + LEAD2 - 1
                    wait(sp, S["stage2_lo"], c)
                    sp.dma_start(stage2[:].rearrange("p (c n) -> p c n", c=DC), down_v[:, DC * c:DC * (c + 1), :]
                                 ).then_inc(S["stage2_in"], 16)

            pass2_loop(sp, body2, peeled2)
            sp.wait_ge(S["out_stored"], 16 * NT)

        @block.scalar
        def _(act):
            act.wait_ge(S["dft_loaded"], 16)
            act.activation(dft_h[:], stage[0][:, 0:DFT], ACT.Copy).then_inc(S["dft_hi"], 1)

            def stack(out, halves, parts):
                for part in parts:
                    for p in range(PAIRS):
                        last = act.activation(out[STACK * part:STACK * (part + 1), p, :],
                                              halves[STACK * p:STACK * (p + 1), :].bitcast(F32), ACT.Copy)
                return last

            def context_high(t):
                if live(t):
                    act.wait_ge(S["ct_ps"], t + 1)
                    wait(act, S["kv_ps"], t)
                    act.activation(ct_h[:], turned_bank(t, True)[:], ACT.Copy).then_inc(S["ct_hi"], 1)

            def query_high(t):
                if live(t):
                    act.wait_ge(S["qx_ps"], t + 1)
                    wait(act, S["qy_ps"], t)
                    act.activation(xt_h[:], turned_bank(t, False)[:], ACT.Copy).then_inc(S["qx_hi"], 1)

            def value_spectrum(t, b):
                act.wait_ge(S["v_ps"], 2 * t + b + 1)
                ps = bank[V_BANK[b]]
                act.activation(vf[:, b, 0, :], ps[:], ACT.Copy).then_inc(S["vf_s"], 1)
                act.activation(vf[0:SEQ, b, 1, :], ps[SEQ:P, :], ACT.Copy)
                act.activation(vf[SEQ:P, b, 1, :], ps[0:SEQ, :], ACT.Copy).then_inc(S["vf_s"], 1)

            def body(i):
                t = i + 2
                if live(t):
                    act.wait_ge(S["q_ps"], t + 1)
                    wait(act, S["prod_s"], 2 * t)
                    act.activation(qf[:], bank[0][:], ACT.Copy).then_inc(S["qf_s"], 1)
                t = i
                if live(t):
                    act.wait_ge(S["nb2_s"], t + 1)
                    wait(act, S["xt_ps"], t)
                    act.activation(xn2[:], x1[:], ACT.Identity, bias=nb2[:], scale=rs2[:]).then_inc(S["xn2_s"], 1)
                if staged_before(i):
                    act.wait_ge(S["stage_in"], LANDED[i - 1])
                    if i > 1:
                        act.wait_ge(S["rt_lo"], DC)
                    target = WEIGHTS[i - 1][1]
                    act.activation(target, stage[0][:, 0:target.shape[1]], ACT.Copy).then_inc(S["stage_hi"], 1)
                t = i + 3
                if live(t):
                    act.wait_ge(S["nb1_s"], t + 1)
                    wait(act, S["x_lo"], t)
                    act.activation(xn1[:], x_in[:], ACT.Identity, bias=nb1[:], scale=rs1[:]).then_inc(S["xn1_s"], 1)
                    wait(act, S["q_ps"], t)
                    act.activation(x_h[:], x_in[:], ACT.Identity, bias=nb1[:], scale=rs1[:]).then_inc(S["x_hi"], 1)
                t = i
                if live(t):
                    act.wait_ge(S["xt_ps"], t + 1)
                    wait(act, S["ffn_ps"], t)
                    act.activation(x1t_h[:], bank[5][:], ACT.Copy).then_inc(S["xt_hi"], 1)
                if early(i):
                    context_high(0)
                    query_high(0)
                t = i + 2
                if live(t):
                    wait(act, S["prod2_s"], 4 * t)
                    value_spectrum(t, 0)
                t = i + 2
                if live(t):
                    act.wait_ge(S["shift_s"], t + 1)
                    act.activation(shifted[:], shifted[:], ACT.Exp).then_inc(S["exp_s"], 1)
                    value_spectrum(t, 1)
                t = i + 3
                if live(t):
                    act.wait_ge(S["ctx_loaded"], 16 * (t + 1))
                    wait(act, S["v_ps"], 2 * t)
                    act.activation(c_h[:], ctx_t[:], ACT.Copy).then_inc(S["c_hi"], 1)
                t = i
                if live(t):
                    act.wait_ge(S["ffn_ps"], t + 1)
                    wait(act, S["x2_stored"], 16 * t)
                    act.activation(x2[:], bank[7][:], ACT.Copy).then_inc(S["x2_s"], 1)
                if isinstance(i, int) and i == -2:
                    act.wait_ge(S["lora_in"], 16 * (2 + DC + ADAPT))
                    act.activation(coef_scaled[:], coef[:], ACT.Copy, scale=float(LORA_SCALE)).then_inc(S["coef_ready"], 1)
                    act.wait_ge(S["coef_ready"], 1)
                    act.wait_ge(S["bt_ps"], 1)
                    act.activation(b_t[:], bank[6][:], ACT.Copy, scale=coef_scaled[:]).then_inc(S["bt_ready"], 1)
                t = i + 2
                if live(t):
                    act.wait_ge(S["wt_ps"], t + 1)
                    wait(act, S["wf_ps"], 2 * t)
                    act.activation(wt_h[:], bank[5][:], ACT.Copy).then_inc(S["wt_hi"], 1)

            def peeled(i):
                if i == -2:
                    for c in range(DC):
                        act.wait_ge(S["w0_ps"], c + 1)
                        act.activation(w0_h[:, c * D:(c + 1) * D], bank[6 + c % 2][:], ACT.Copy
                                       ).then_inc(S["w0_hi"], 1)
                    act.wait_ge(S["ext_ps"], 1)
                    act.activation(ex_t[:].rearrange("p a b -> p (a b)"), bank[7][:], ACT.Copy).then_inc(S["ext_ready"], 1)
                if i == -1:
                    act.wait_ge(S["merge_in"], 64)
                    act.activation(gate_hl[:, :, 0, :], gate_raw[:], ACT.Copy).then_inc(S["gate_split"], 1)
                    for c in range(2):
                        act.wait_ge(S["ef_ps"], c + 1)
                        act.activation(ex_fc2[:, c, :], bank[6 + c][:], ACT.Copy).then_inc(S["ef_ready"], 1)
                    for c in range(2):
                        act.wait_ge(S["fct_ps"], c + 1)
                        act.activation(fc1_t[:, c, :], bank[6 + c][:], ACT.Copy).then_inc(S["fct_ready"], 1)
                    for c in range(DC):
                        act.wait_ge(S["rt_ps"], c + 1)
                        act.activation(rt_h[:, c * D:(c + 1) * D], bank[6 + c % 2][:], ACT.Copy
                                       ).then_inc(S["rt_hi"], 1)

            pass1_loop(act, body, peeled)
            act.wait_ge(S["x2_s"], NT)

            def body2(i):
                t = i + 1
                if live(t):
                    act.wait_ge(S["t4_ps"], t + 1)
                    wait(act, S["rt_out_ps"], t)
                    act.activation(t4_h[:], bank[4][:], ACT.Copy).then_inc(S["t4_hi"], 1)
                t = i + 3
                if live(t):
                    act.wait_ge(S["qkt_ps"], t + 1)
                    wait(act, S["kbd_s"], 3 * t)
                    act.activation(kt_h[:], bank[1][:, 0:P], ACT.Copy).then_inc(S["kt_hi"], 1)
                    wait(act, S["qt_lo"], t)
                    act.activation(qt_h[:], bank[0][:], ACT.Copy).then_inc(S["qt_hi"], 1)
                    wait(act, S["g_ps"], 4 * t)
                    act.activation(qt_b[:], bank[0][:], ACT.Copy).then_inc(S["qt_bs"], 1)
                t = i
                if live(t):
                    act.wait_ge(S["ht_ps"], 2 * t + 1)
                    wait(act, S["dn_ps"], 2 * t)
                    act.activation(ht_h[:], bank[5][:], ACT.Copy).then_inc(S["ht_hi"], 1)
                    wait(act, S["o_s"], t)
                    act.wait_ge(S["x3b_s"], t + 1)
                    act.activation(x3c[:], x3b[:], ACT.Copy).then_inc(S["x3c_s"], 1)
                context_high(i + 4)
                t = i + 3
                if live(t):
                    if isinstance(t, int) and t == 0:
                        act.wait_ge(S["x2_stored"], 16 * NT)
                    wait(act, S["kbd_s"], 3 * t)
                    act.wait_ge(S["kt_hi"], t + 1)
                    stack(k_pairs, kt_h, (0, 2))
                    act.wait_ge(S["kt_lo"], t + 1)
                    stack(k_pairs, kt_l, (1,)).then_inc(S["kp_s"], 1)
                    wait(act, S["s_ps"], 2 * t)
                    act.wait_ge(S["qt_hi"], t + 1)
                    stack(q_stack, qt_h, (0,))
                t = i + 2
                if live(t):
                    act.wait_ge(S["y_s"], 2 * t + 2)
                    wait(act, S["wo_ps"], t)
                    act.activation(y_h[:], y_flat, ACT.Copy).then_inc(S["y_hi"], 1)
                t = i + 3
                if live(t):
                    stack(q_stack, qt_h, (1,))
                    act.wait_ge(S["qt_lo"], t + 1)
                    stack(q_stack, qt_l, (2,)).then_inc(S["qs_s"], 1)
                t = i + 1
                if live(t):
                    if isinstance(t, int) and t == 0:
                        act.wait_ge(S["stage2_lo"], 2)
                    wait(act, S["ht_ps"], 2 * t)
                    for c in range(2):
                        act.wait_ge(S["u_ps"], 2 * t + c + 1)
                        act.activation(act2[:, c * D:(c + 1) * D], bank[6 + c][:], ACT.Relu).then_inc(S["relu_s"], 1)
                t = i
                if live(t):
                    act.wait_ge(S["ht_ps"], 2 * t + 2)
                    act.wait_ge(S["dn_ps"], 2 * t + 1)
                    act.activation(ht_h[:], bank[5][:], ACT.Copy).then_inc(S["ht_hi"], 1)
                query_high(i + 4)
                t = i + 3
                if live(t):
                    act.wait_ge(S["gmt_ps"], t + 1)
                    wait(act, S["s_ps"], 2 * t)
                    act.wait_ge(S["sel_s"], 3)
                    for p in range(PAIRS):
                        last = act.activation(q_stack[GUARD:GUARD + NKV, p, :], bank[1][0:NKV, :],
                                              ACT.Copy, scale=-1.0)
                    last.then_inc(S["ngm_s"], 1)
                    act.wait_ge(S["s_ps"], 2 * t + 1)
                    wait(act, S["pv_ps"], 2 * t)
                    act.activation(probs[:, 0].rearrange("p a b -> p (a b)"), wide[:], ACT.Exp, scale=HD ** -0.5
                                   ).then_inc(S["probs_s"], 1)
                if down_staged(i):
                    c = i + LEAD2 - 1
                    act.wait_ge(S["stage2_in"], 16 * (c + 1))
                    act.activation(down_h[:, DC * D * c:DC * D * (c + 1)], stage2[:], ACT.Copy).then_inc(S["stage2_hi"], 1)
                t = i + 1
                if live(t):
                    act.wait_ge(S["rt_out_ps"], t + 1)
                    act.wait_ge(S["rw_s"], t + 1)
                    wait(act, S["z_s"], t)
                    act.activation(routed[:], bank[4][:], ACT.Copy, scale=rw[:]).then_inc(S["routed_s"], 1)
                t = i + 3
                if live(t):
                    act.wait_ge(S["s_ps"], 2 * t + 2)
                    act.activation(probs[:, 1].rearrange("p a b -> p (a b)"), wide[:], ACT.Exp, scale=HD ** -0.5
                                   ).then_inc(S["probs_s"], 1)

            pass2_loop(act, body2)

        @block.gpsimd
        def _(pool):
            def rstd(t, mv, var, rs, n):
                pool.wait_ge(S[f"mv{n}_s"], t + 1)
                pool.tensor_tensor(var[:], mv[:, 1:2], eps, ALU.add).then_inc(S[f"va{n}_s"], 1)
                pool.wait_ge(S[f"va{n}_s"], t + 1)
                pool.tensor_tensor(rs[:], var[:], half, ALU.pow).then_inc(S[f"rs{n}_s"], 1)

            def normaliser(t, mv, var, rs, nm, nb, n):
                rstd(t, mv, var, rs, n)
                pool.tensor_tensor(nm[:], mv[:, 0:1], minus, ALU.mult).then_inc(S[f"nm{n}_s"], 1)
                pool.wait_ge(S[f"rs{n}_s"], t + 1)
                pool.wait_ge(S[f"nm{n}_s"], t + 1)
                pool.tensor_tensor(nb[:], nm[:], rs[:], ALU.mult).then_inc(S[f"nb{n}_s"], 1)

            pool.wait_ge(S["const_in"], 16)

            def body(i):
                t = i + 3
                if live(t):
                    wait(pool, S["x_hi"], t)
                    normaliser(t, mv1, va1, rs1, nm1, nb1, 1)
                if staged_before(i):
                    low_half(i - 1, 0)
                if live(t):
                    pool.wait_ge(S["xn1_s"], t + 1)
                    pool.wait_ge(S["x_hi"], t + 1)
                    wait(pool, S["q_ps"], t)
                    pool.tensor_tensor(x_l[:], xn1[:], x_h[:].bitcast(F32), ALU.subtract).then_inc(S["x_lo"], 1)
                if staged_before(i):
                    low_half(i - 1, 1)
                t = i + 3
                if live(t):
                    pool.wait_ge(S["c_hi"], t + 1)
                    wait(pool, S["v_ps"], 2 * t)
                    pool.tensor_tensor(c_l[:], ctx_t[:], c_h[:].bitcast(F32), ALU.subtract).then_inc(S["c_lo"], 1)
                if early(i):
                    rstd(0, mv3, va3, rs3, 3)
                t = i + 1
                if live(t):
                    wait(pool, S["xn2_s"], t)
                    normaliser(t, mv2, va2, rs2, nm2, nb2, 2)
                    pool.wait_ge(S["x1_s"], t + 1)
                    wait(pool, S["ffn_ps"], t)
                    pool.tensor_tensor(x1b[:], x1[:], b0_all[:], ALU.add).then_inc(S["x1b_s"], 1)

            def low_half(i, part):
                hi, lo = WEIGHTS[i][1:]
                n = lo.shape[1] // 2
                k = slice(n * part, n * (part + 1))
                pool.wait_ge(S["stage_hi"], STAGED[i])
                pool.tensor_tensor(lo[:, k], stage[0][:, k], hi[:, k].bitcast(F32), ALU.subtract
                                   ).then_inc(S["stage_lo"], 1)

            pass1_loop(pool, body)
            pool.wait_ge(S["x2_s"], NT)

            heads = head_of.unsqueeze(2).to_broadcast([P, NKV, SEQ])

            def body2(i):
                t = i - 1
                if live(t):
                    pool.wait_ge(S["zn_s"], t + 1)
                    pool.tensor_tensor(z[:], z[:], gamma_all[:], ALU.mult).then_inc(S["zg_s"], 1)
                    pool.wait_ge(S["zg_s"], t + 1)
                    pool.wait_ge(S["x3c_s"], t + 1)
                    pool.tensor_tensor(z[:], z[:], x3c[:], ALU.add).then_inc(S["o_s"], 1)
                t = i + 3
                if live(t):
                    def spread(out, kt, b):
                        k = kt[:, SEQ * b:SEQ * (b + 1)].bitcast(F32).unsqueeze(1).to_broadcast([P, NKV, SEQ])
                        pool.tensor_tensor(out[:, b, :].rearrange("p (h k) -> p h k", h=NKV), k, heads, ALU.mult
                                           ).then_inc(S["kbd_s"], 1)

                    pool.wait_ge(S["kt_hi"], t + 1)
                    wait(pool, S["g_ps"], 4 * t)
                    spread(kbd_b, kt_h, 0)
                    spread(kbd_b, kt_h, 1)
                t = i + 4
                if live(t):
                    rstd(t, mv3, va3, rs3, 3)
                t = i + 2
                if live(t):
                    pool.wait_ge(S["y_hi"], t + 1)
                    wait(pool, S["wo_ps"], t)
                    pool.tensor_tensor(y_l[:], y_flat, y_h[:].bitcast(F32),
                                       ALU.subtract).then_inc(S["y_lo"], 1)
                    pool.wait_ge(S["res2_loaded"], 16 * (t + 1))
                    pool.tensor_tensor(x2_res[:], x2_res[:], bo_all[:], ALU.add).then_inc(S["x2b_s"], 1)
                t = i + 1
                if live(t):
                    pool.wait_ge(S["x3_s"], t + 1)
                    wait(pool, S["x3c_s"], t)
                    pool.tensor_tensor(x3b[:], x3[:], beta_all[:], ALU.add).then_inc(S["x3b_s"], 1)
                t = i + 3
                if live(t):
                    pool.wait_ge(S["kp_s"], t + 1)
                    wait(pool, S["s_ps"], 2 * t)
                    pool.tensor_tensor(k_stack[0:GUARD].rearrange("r p b (h k) -> r (p b) h k", h=2),
                                       k_pairs.rearrange("r p (b k) -> r (p b) k", b=2).unsqueeze(2)
                                       .to_broadcast([GUARD, 2 * PAIRS, 2, SEQ]),
                                       head_of_pair[0:GUARD].unsqueeze(1).unsqueeze(3)
                                       .to_broadcast([GUARD, 2 * PAIRS, 2, SEQ]), ALU.mult).then_inc(S["kbd_s"], 1)
                t = i + 2
                if live(t):
                    rstd(t, mv4, va4, rs4, 4)
                t = i + 1
                if live(t):
                    pool.wait_ge(S["relu_s"], 2 * t + 2)
                    pool.tensor_tensor(act2[:], act2[:], act2[:], ALU.mult).then_inc(S["h_s"], 1)
                t = i
                if live(t):
                    rstd(t, mv5, va5, rs5, 5)

            pass2_loop(pool, body2)


        def wait_alone(eng, sem, value, done, times):
            value = value if isinstance(value, int) else eng.snap(eng.to_reg(value))
            eng.wait_ge(done, times)
            wait(eng, sem, value)

        @block.vector
        def _(dve):
            def context_low(t):
                if live(t):
                    dve.wait_ge(S["ct_hi"], t + 1)
                    wait(dve, S["kv_ps"], t)
                    dve.tensor_tensor(ct_l[:], turned_bank(t, True)[:], ct_h[:].bitcast(F32), ALU.subtract
                                      ).then_inc(S["ct_lo"], 1)
                    dve.wait_ge(S["tile_loaded"], 16 * (t + 1))
                    dve.bn_stats(bn3[:], xn3[:]).then_inc(S["bn3_s"], 1)
                    wait_alone(dve, S["bn3_s"], t + 1, S["x_loaded"], 16)
                    dve.bn_aggr(mv3[:], bn3[:]).then_inc(S["mv3_s"], 1)

            def normalised(t):
                if live(t):
                    dve.wait_ge(S["rs3_s"], t + 1)
                    dve.tensor_scalar(xn3[:], xn3[:], mv3[:, 0:1], rs3[:], ALU.subtract, ALU.mult
                                      ).then_inc(S["xn3_s"], 1)

            def keys_values(t):
                if live(t):
                    dve.wait_ge(S["kv_ps"], t + 1)
                    wait(dve, S["qkt_ps"], t)
                    wait(dve, S["vbd_s"], t)
                    dve.tensor_tensor(kv_sb[:], bank[2][:, 0:2 * KVW], bkv_all[:], ALU.add).then_inc(S["kv_s"], 1)
                    dve.wait_ge(S["qx_hi"], t + 1)
                    wait(dve, S["qy_ps"], t)
                    dve.tensor_tensor(xt_l[:], turned_bank(t, False)[:], xt_h[:].bitcast(F32), ALU.subtract
                                      ).then_inc(S["qx_lo"], 1)

            def queries(t):
                if live(t):
                    dve.wait_ge(S["qy_ps"], t + 1)
                    wait(dve, S["qkt_ps"], t)
                    dve.tensor_tensor(q_sb[:].rearrange("p (g h d) -> p h g d", g=GROUPS, h=NKV),
                                      bank[0][:].rearrange("p (h g d) -> p h g d", g=GROUPS, h=NKV),
                                      bq_all[:].rearrange("p (h g d) -> p h g d", g=GROUPS, h=NKV), ALU.add
                                      ).then_inc(S["q_s"], 1)

            def body(i):
                t = i + 2
                if live(t):
                    dve.wait_ge(S["qf_s"], t + 1)
                    wait(dve, S["corr_ps"], t)
                    for j in range(2):
                        dve.wait_ge(S["k_ps"], 2 * t + j + 1)
                        dve.tensor_tensor(prod[:, j, :], bank[1 + j][:], qf[:], ALU.mult
                                          ).then_inc(S["prod_s"], 1)
                t = i + 3
                if live(t):
                    dve.wait_ge(S["x_loaded"], 16 * (t + 1))
                    wait(dve, S["nb1_s"], t)
                    dve.bn_stats(bn1[:], x_in[:]).then_inc(S["bn1_s"], 1)
                    wait_alone(dve, S["bn1_s"], t + 1, S["x_loaded"], 16)
                    dve.bn_aggr(mv1[:], bn1[:]).then_inc(S["mv1_s"], 1)
                t = i + 1
                if live(t):
                    wait(dve, S["o_ps"], t)
                    dve.wait_ge(S["vf_s"], 4 * t + 4)
                    for n in range(4):
                        dve.wait_ge(S["wf_ps"], 2 * t + n // 2 + 1)
                        dve.tensor_tensor(prod2[:, n // 2, n % 2, :], bank[W_BANK[n // 2]][:],
                                          vf[:, n // 2, n % 2, :], ALU.mult).then_inc(S["prod2_s"], 1)
                t = i + 2
                if live(t):
                    corr = bank[4][:].rearrange("p (c s) -> p c s", s=SEQ)
                    wait_alone(dve, S["corr_ps"], t + 1, S["x_loaded"], 16)
                    for c in range(2 * DC):
                        top = dve.max(m8[:, c, :], corr[:, c, :])
                    top.then_inc(S["tops_s"], 1)
                t = i
                if live(t):
                    dve.wait_ge(S["xt_hi"], t + 1)
                    wait(dve, S["ffn_ps"], t)
                    dve.tensor_tensor(x1t_l[:], bank[5][:], x1t_h[:].bitcast(F32), ALU.subtract
                                      ).then_inc(S["xt_lo"], 1)
                if early(i):
                    dve.wait_ge(S["bcast_in"], 16 * 7)
                    context_low(0)
                if early(i, 1):
                    queries(0)
                t = i + 2
                if live(t):
                    wait(dve, S["wgt_s"], t)
                    dve.wait_ge(S["tops_s"], t + 1)
                    best = m8[:, :, 0:1]
                    dve.tensor_tensor(shifted[:, :, 0:SEQ], corr, best.to_broadcast([P, 2 * DC, SEQ]),
                                      ALU.subtract)
                    dve.tensor_tensor(shifted[:, :, SEQ:SEQ + TOP], m8[:], best.to_broadcast([P, 2 * DC, TOP]),
                                      ALU.subtract).then_inc(S["shift_s"], 1)
                    for c in range(2 * DC):
                        kept = dve.match_replace(kept_not[:, c, :], m8[:, c, :], corr[:, c, :], REMOVED)
                    kept.then_inc(S["rep_s"], 1)
                    dve.wait_ge(S["exp_s"], t + 1)
                    dve.tensor_reduce(total[:], shifted[:, :, SEQ:SEQ + TOP], AX.X, ALU.add).then_inc(S["sum_s"], 1)
                    dve.wait_ge(S["rep_s"], t + 1)
                    dve.scalar_tensor_tensor(kept_not[:], kept_not[:], REMOVED_BELOW, shifted[:, :, 0:SEQ],
                                             ALU.is_lt, ALU.mult).then_inc(S["mask_s"], 1)
                    dve.wait_ge(S["sum_s"], t + 1)
                    dve.reciprocal(total_inv[:], total[:]).then_inc(S["inv_s"], 1)
                    dve.wait_ge(S["inv_s"], t + 1)
                    dve.wait_ge(S["mask_s"], t + 1)
                    wait(dve, S["wt_ps"], t)
                    dve.tensor_tensor(wgt[:].rearrange("p (c s) -> p c s", s=SEQ), kept_not[:],
                                      total_inv[:].unsqueeze(2).to_broadcast([P, 2 * DC, SEQ]), ALU.mult
                                      ).then_inc(S["wgt_s"], 1)
                t = i + 1
                if live(t):
                    dve.wait_ge(S["o_ps"], t + 1)
                    dve.wait_ge(S["res_loaded"], 16 * (t + 1))
                    wait(dve, S["x1b_s"], t)
                    wait(dve, S["xn2_s"], t)
                    wait(dve, S["nb2_s"], t)
                    dve.tensor_tensor(x1[:], bank[6][:], x_res[:], ALU.add).then_inc(S["x1_s"], 1)
                    dve.wait_ge(S["x1_s"], t + 1)
                    dve.bn_stats(bn2[:], x1[:]).then_inc(S["bn2_s"], 1)
                    wait_alone(dve, S["bn2_s"], t + 1, S["x_loaded"], 16)
                    dve.bn_aggr(mv2[:], bn2[:]).then_inc(S["mv2_s"], 1)
                if early(i):
                    normalised(0)
                    keys_values(0)
                t = i + 2
                if live(t):
                    dve.wait_ge(S["wt_hi"], t + 1)
                    wait(dve, S["wf_ps"], 2 * t)
                    dve.tensor_tensor(wt_l[:], bank[5][:], wt_h[:].bitcast(F32), ALU.subtract
                                      ).then_inc(S["wt_lo"], 1)

            def peeled(i):
                if i == -3:
                    dve.wait_ge(S["dft_hi"], 1)
                    dve.tensor_tensor(dft_l[:], stage[0][:, 0:DFT], dft_h[:].bitcast(F32), ALU.subtract
                                      ).then_inc(S["dft_lo"], 1)
                if i == -2:
                    for c in range(DC):
                        dve.wait_ge(S["w0_hi"], c + 1)
                        dve.tensor_tensor(w0_l[:, c * D:(c + 1) * D], bank[6 + c % 2][:],
                                          w0_h[:, c * D:(c + 1) * D].bitcast(F32), ALU.subtract
                                          ).then_inc(S["w0_lo"], 1)
                if i == -1:
                    dve.wait_ge(S["gate_split"], 1)
                    dve.tensor_tensor(gate_hl[:, :, 1, :], gate_raw[:], gate_hl[:, :, 0, :].bitcast(F32), ALU.subtract
                                      ).then_inc(S["gate_split"], 1)
                    for c in range(DC):
                        dve.wait_ge(S["rt_hi"], c + 1)
                        dve.tensor_tensor(rt_l[:, c * D:(c + 1) * D], bank[6 + c % 2][:],
                                          rt_h[:, c * D:(c + 1) * D].bitcast(F32), ALU.subtract
                                          ).then_inc(S["rt_lo"], 1)

            pass1_loop(dve, body, peeled)
            dve.wait_ge(S["x2_s"], NT)
            dve.memset(vbd[:], 0.0).then_inc(S["vbd_zero"], 1)
            dve.memset(zero_col[:], 0.0).then_inc(S["vbd_zero"], 1)
            dve.wait_ge(S["vbd_zero"], 2)

            def maxima(t, groups):
                for g in groups:
                    dve.wait_ge(S["g_ps"], 4 * t + g + 1)
                    dve.tensor_reduce(gmax[:, NKV * g:NKV * (g + 1)],
                                      bank[g % 2][:].rearrange("p (h k) -> p h k", h=NKV), AX.X, ALU.max
                                      ).then_inc(S["gmax_s"], 1)

            def body2(i):
                t = i + 1
                if live(t):
                    dve.wait_ge(S["t4_hi"], t + 1)
                    wait(dve, S["rt_out_ps"], t)
                    dve.tensor_tensor(t4_l[:], bank[4][:], t4_h[:].bitcast(F32), ALU.subtract).then_inc(S["t4_lo"], 1)
                t = i + 3
                if live(t):
                    dve.wait_ge(S["kt_hi"], t + 1)
                    wait(dve, S["kbd_s"], 3 * t)
                    dve.tensor_tensor(kt_l[:], bank[1][:, 0:P], kt_h[:].bitcast(F32), ALU.subtract).then_inc(S["kt_lo"], 1)
                    dve.wait_ge(S["qt_bs"], t + 1)
                    wait(dve, S["qs_s"], t)
                    dve.tensor_tensor(qt_l[:], bank[0][:], qt_h[:].bitcast(F32), ALU.subtract).then_inc(S["qt_lo"], 1)
                t = i
                if live(t):
                    dve.wait_ge(S["ht_hi"], 2 * t + 1)
                    wait(dve, S["dn_ps"], 2 * t)
                    dve.tensor_tensor(ht_l[:], bank[5][:], ht_h[:].bitcast(F32), ALU.subtract).then_inc(S["ht_lo"], 1)
                context_low(i + 4)
                t = i + 2
                if live(t):
                    wait(dve, S["wo_ps"], t)
                    for b in range(2):
                        part = bank[2 + b][:].rearrange("p (n g q) -> p n g q", n=2, g=GROUPS)
                        dve.wait_ge(S["pv_ps"], 2 * t + b + 1)
                        dve.reciprocal(y[:, :, b, :], part[:, 1]).then_inc(S["den_s"], 1)
                        dve.wait_ge(S["den_s"], 2 * t + b + 1)
                        dve.tensor_tensor(y[:, :, b, :], part[:, 0], y[:, :, b, :], ALU.mult).then_inc(S["y_s"], 1)
                normalised(i + 4)
                t = i + 1
                if live(t):
                    dve.wait_ge(S["gate_ps"], t + 1)
                    dve.tensor_reduce(logits[:], bank[4][:, 0:2 * EXPERTS].rearrange("p (a e) -> p e a", a=2),
                                      AX.X, ALU.add).then_inc(S["lg_s"], 1)
                    wait_alone(dve, S["lg_s"], t + 1, S["x_loaded"], 16)
                    dve.max(lg[:], logits[:]).then_inc(S["top_s"], 1)
                    dve.wait_ge(S["top_s"], t + 1)
                    wait(dve, S["routed_s"], t)
                    dve.tensor_tensor(rw[:], lg[:, 0:1], lg[:, 1:2], ALU.add).then_inc(S["rw_s"], 1)
                t = i + 3
                if live(t):
                    wait(dve, S["gmt_ps"], t)
                    maxima(t, (0, 1))
                t = i + 2
                if live(t):
                    dve.wait_ge(S["wo_ps"], t + 1)
                    dve.wait_ge(S["x2b_s"], t + 1)
                    wait(dve, S["x3b_s"], t)
                    dve.tensor_tensor(x3[:], bank[2][:], x2_res[:], ALU.add).then_inc(S["x3_s"], 1)
                    dve.wait_ge(S["x3_s"], t + 1)
                    dve.bn_stats(bn4[:], x3[:]).then_inc(S["bn4_s"], 1)
                    wait_alone(dve, S["bn4_s"], t + 1, S["x_loaded"], 16)
                    dve.bn_aggr(mv4[:], bn4[:]).then_inc(S["mv4_s"], 1)
                t = i + 3
                if live(t):
                    maxima(t, (2, 3))
                t = i
                if live(t):
                    dve.wait_ge(S["ht_hi"], 2 * t + 2)
                    dve.wait_ge(S["dn_ps"], 2 * t + 1)
                    dve.tensor_tensor(ht_l[:], bank[5][:], ht_h[:].bitcast(F32), ALU.subtract).then_inc(S["ht_lo"], 1)
                t = i + 2
                if live(t):
                    dve.wait_ge(S["rs4_s"], t + 1)
                    wait(dve, S["t4_ps"], t)
                    dve.tensor_scalar(xn4[:], x3[:], mv4[:, 0:1], rs4[:], ALU.subtract, ALU.mult
                                      ).then_inc(S["xn4_s"], 1)
                t = i + 3
                if live(t):
                    wait(dve, S["pv_ps"], 2 * t)
                    dve.wait_ge(S["kv_s"], t + 1)
                    for b in range(2):
                        for h in range(2):
                            v = kv_sb[SEQ * b:SEQ * (b + 1), KVW:2 * KVW].rearrange("k (p h d) -> k p h d", p=PAIRS, h=2)
                            last = dve.tensor_copy(vbd[SEQ * h:SEQ * (h + 1), b, :, h, :], v[:, :, h, :])
                    last.then_inc(S["vbd_s"], 1)
                    if isinstance(t, int) and t == 0:
                        dve.wait_ge(S["sel_in"], 16)
                        for b in range(2):
                            dve.tensor_copy(k_stack[GUARD:, :, b, :], x2_res[GUARD:, :].rearrange("r (p n) -> r p n", p=PAIRS)
                                            ).then_inc(S["sel_s"], 1)
                        zeros = zero_col[GUARD:, :].unsqueeze(2).to_broadcast([P - GUARD, PAIRS, D])
                        dve.tensor_tensor(q_stack[GUARD:], zeros, zeros, ALU.mult).then_inc(S["sel_s"], 1)
                keys_values(i + 4)
                t = i
                if live(t):
                    dve.wait_ge(S["dn_ps"], 2 * t + 2)
                    dve.wait_ge(S["routed_s"], t + 1)
                    wait(dve, S["out_stored"], 16 * t)
                    dve.tensor_tensor(z[:], bank[3][:], routed[:], ALU.add).then_inc(S["z_s"], 1)
                    dve.wait_ge(S["z_s"], t + 1)
                    dve.bn_stats(bn5[:], z[:]).then_inc(S["bn5_s"], 1)
                    wait_alone(dve, S["bn5_s"], t + 1, S["x_loaded"], 16)
                    dve.bn_aggr(mv5[:], bn5[:]).then_inc(S["mv5_s"], 1)
                queries(i + 4)
                if down_staged(i):
                    c = i + LEAD2 - 1
                    part = slice(DC * D * c, DC * D * (c + 1))
                    dve.wait_ge(S["stage2_hi"], c + 1)
                    dve.tensor_tensor(down_l[:, part], stage2[:], down_h[:, part].bitcast(F32), ALU.subtract
                                      ).then_inc(S["stage2_lo"], 1)
                t = i
                if live(t):
                    dve.wait_ge(S["rs5_s"], t + 1)
                    dve.tensor_scalar(z[:], z[:], mv5[:, 0:1], rs5[:], ALU.subtract, ALU.mult).then_inc(S["zn_s"], 1)

            pass2_loop(dve, body2)

        @block.tensor
        def _(pe):
            def split_product(out_ps, w_hi, w_lo, m_hi, m_lo, start, stop):
                pe.matmul(out_ps, w_hi, m_hi, start=start, stop=False)
                pe.matmul(out_ps, w_hi, m_lo, start=False, stop=False)
                return pe.matmul(out_ps, w_lo, m_hi, start=False, stop=stop)

            pe.wait_ge(S["const_in"], 16)
            pe.wait_ge(S["first_in"], 16)
            pe.wait_ge(S["dft_lo"], 1)

            def cols(w, c, n):
                return w[:, c * n:(c + 1) * n]

            def turn_context(t):
                if live(t):
                    pe.wait_ge(S["ctx2_loaded"], 16 * (t + 1))
                    wait(pe, S["probs_s"], 2 * (t - 1))
                    if isinstance(t, int) and t == 0:
                        pe.wait_ge(S["vf_s"], 4 * NT)
                        pe.wait_ge(S["rep_s"], NT)
                    for c in range(DC):
                        last = pe.transpose(cols(turned_bank(t, True), c, P), cols(ctx2, c, P), ident)
                    last.then_inc(S["ct_ps"], 1)

            def keys_values(t):
                if live(t):
                    pe.wait_ge(S["ct_lo"], t + 1)
                    wait(pe, S["x3_s"], t - 1)
                    for c in range(DC):
                        last = split_product(bank[2][:, 0:2 * KVW], cols(ct_h, c, P), cols(ct_l, c, P),
                                             cols(wkv_h, c, 2 * KVW), cols(wkv_l, c, 2 * KVW), c == 0, c == DC - 1)
                    last.then_inc(S["kv_ps"], 1)
                    pe.wait_ge(S["xn3_s"], t + 1)
                    wait(pe, S["ht_lo"], 2 * (t - 3))
                    for c in range(DC):
                        last = pe.transpose(cols(turned_bank(t, False), c, P), cols(xn3, c, P), ident)
                    last.then_inc(S["qx_ps"], 1)

            def queries(t):
                if live(t):
                    pe.wait_ge(S["qx_lo"], t + 1)
                    wait(pe, S["gmax_s"], 4 * t)
                    for c in range(DC):
                        last = split_product(bank[0][:], cols(xt_h, c, P), cols(xt_l, c, P),
                                             cols(wq_h, c, D), cols(wq_l, c, D), c == 0, c == DC - 1)
                    last.then_inc(S["qy_ps"], 1)

            def transform(out_ps, col, hi, lo):
                w = slice(col, col + P)
                return split_product(out_ps[:], dft_h[:, w], dft_l[:, w], hi[:], lo[:], True, True)

            def body(i):
                t = i + 2
                if live(t):
                    pe.wait_ge(S["x_lo"], t + 1)
                    wait(pe, S["prod2_s"], 4 * (t - 1))
                    wait(pe, S["vf_s"], 4 * t)
                    transform(bank[0], Q0, x_h, x_l).then_inc(S["q_ps"], 1)
                    pe.wait_ge(S["c_lo"], t + 1)
                    for j in range(2):
                        transform(bank[1 + j], K0 + P * j, c_h, c_l).then_inc(S["k_ps"], 1)
                t = i + 1
                if live(t):
                    pe.wait_ge(S["wt_lo"], t + 1)
                    wait(pe, S["prod2_s"], 4 * t)
                    transform(bank[W_BANK[0]], W0, wt_h, wt_l).then_inc(S["wf_ps"], 1)
                    wait(pe, S["qf_s"], min_tiles(1, t + 2))
                    transform(bank[W_BANK[1]], W0 + P, wt_h, wt_l).then_inc(S["wf_ps"], 1)
                t = i + 2
                if live(t):
                    pe.wait_ge(S["prod_s"], 2 * (t + 1))
                    wait(pe, S["rep_s"], t)
                    for c in range(DC):
                        k = slice(c * P, (c + 1) * P)
                        for j in range(2):
                            last = pe.matmul(bank[4][:, k], prod[:, j, k], icorr[j], start=(j == 0), stop=(j == 1))
                    last.then_inc(S["corr_ps"], 1)
                    transform(bank[V_BANK[0]], V0, c_h, c_l).then_inc(S["v_ps"], 1)
                t = i
                if live(t):
                    pe.wait_ge(S["xn2_s"], t + 1)
                    wait(pe, S["wt_lo"], min_tiles(1, t + 2))
                    for c in range(DC):
                        last = pe.transpose(bank[5][:, c * P:(c + 1) * P], xn2[:, c * P:(c + 1) * P], ident)
                    last.then_inc(S["xt_ps"], 1)
                if early(i):
                    turn_context(0)
                if early(i, 1):
                    queries(0)
                t = i + 2
                if live(t):
                    transform(bank[V_BANK[1]], V0 + P, c_h, c_l).then_inc(S["v_ps"], 1)
                t = i + 1
                if live(t):
                    pe.wait_ge(S["prod2_s"], 4 * (t + 1))
                    wait(pe, S["x1_s"], t)
                    if isinstance(t, int) and t <= 1:
                        pe.wait_ge(*((S["rt_lo"], DC) if t else (S["w0_lo"], DC)))
                    for j in range(2):
                        for b in range(2):
                            last = pe.matmul(bank[6][SEQ * b:SEQ * (b + 1), :], iout[j], prod2[:, b, j, :],
                                             start=(j == 0), stop=(j == 1))
                    last.then_inc(S["o_ps"], 1)
                t = i
                if live(t):
                    pe.wait_ge(S["xt_lo"], t + 1)
                    wait(pe, S["x2_s"], t)
                    for c in range(DC):
                        k = slice(c * P, (c + 1) * P)
                        n = slice(c * D, (c + 1) * D)
                        split_product(bank[7][:], x1t_h[:, k], x1t_l[:, k], w0_h[:, n], w0_l[:, n], c == 0, False)
                    pe.wait_ge(S["x1b_s"], t + 1)
                    pe.matmul(bank[7][:], ident, x1b[:], start=False, stop=True).then_inc(S["ffn_ps"], 1)
                if early(i):
                    keys_values(0)
                if isinstance(i, int) and i == -2:
                    pe.wait_ge(S["lora_in"], 16 * (2 + DC + ADAPT))
                    for c in range(DC):
                        last = pe.transpose(bank[6][:, c * P:(c + 1) * P], b_raw[:, c, :], ident)
                    last.then_inc(S["bt_ps"], 1)
                t = i + 2
                if live(t):
                    pe.wait_ge(S["wgt_s"], t + 1)
                    wait(pe, S["xt_lo"], min_tiles(1, t - 1))
                    for c in range(DC):
                        last = pe.transpose(bank[5][:, c * P:(c + 1) * P], wgt[:, c * P:(c + 1) * P], ident)
                    last.then_inc(S["wt_ps"], 1)

            def peeled(i):
                if i == -2:
                    pe.wait_ge(S["bt_ready"], 1)
                    for c in range(DC):
                        if c >= 2:
                            pe.wait_ge(S["w0_lo"], c - 1)
                        ps = bank[6 + c % 2]
                        for o in range(DC):
                            pe.matmul(ps[:, o * P:(o + 1) * P], w0_raw[:, o, c * P:(c + 1) * P], ident,
                                      start=(o == 0), stop=False, skip_group_check=True)
                        pe.matmul(ps[:], a_raw[:, c * P:(c + 1) * P], b_t[:], start=False, stop=True,
                                  skip_group_check=True).then_inc(S["w0_ps"], 1)
                    pe.wait_ge(S["merge_in"], 64)
                    pe.wait_ge(S["w0_lo"], DC)
                    for m in range(2):
                        for c in range(2):
                            last = pe.transpose(bank[7][:, LAT * m + P * c:LAT * m + P * (c + 1)],
                                                ex_raw[:, c, P * m:P * (m + 1)], ident)
                    last.then_inc(S["ext_ps"], 1)
                if i == -1:
                    pe.wait_ge(S["ext_ready"], 1)
                    pe.wait_ge(S["x1_s"], 1)
                    for c in range(2):
                        for m in range(2):
                            last = pe.matmul(bank[6 + c][:], ex_t[:, m, P * c:P * (c + 1)], fc2_raw[:, m, :],
                                             start=(m == 0), stop=(m == 1))
                        last.then_inc(S["ef_ps"], 1)
                    for c in range(2):
                        pe.wait_ge(S["ef_ready"], c + 1)
                        for k in range(DC):
                            last = pe.transpose(bank[6 + c][:, P * k:P * (k + 1)], fc1_raw[:, k, P * c:P * (c + 1)], ident)
                        last.then_inc(S["fct_ps"], 1)
                    pe.wait_ge(S["fct_ready"], 2)
                    for c in range(DC):
                        if c >= 2:
                            pe.wait_ge(S["rt_lo"], c - 1)
                        for k in range(2):
                            last = pe.matmul(bank[6 + c % 2][:], fc1_t[:, k, P * c:P * (c + 1)], ex_fc2[:, k, :],
                                             start=(k == 0), stop=(k == 1))
                        last.then_inc(S["rt_ps"], 1)

            pass1_loop(pe, body, peeled)
            pe.wait_ge(S["x2_s"], NT)
            pe.wait_ge(S["stage_lo"], 2 * len(WEIGHTS))

            def capped(n, t):
                return n * (min(max(t, 0), NT) if isinstance(t, int) else t)

            def body2(i):
                t = i + 1
                if live(t):
                    pe.wait_ge(S["xn4_s"], t + 1)
                    wait(pe, S["routed_s"], t)
                    for c in range(DC):
                        last = pe.transpose(cols(bank[4], c, P), cols(xn4, c, P), ident)
                    last.then_inc(S["t4_ps"], 1)
                t = i + 3
                if live(t):
                    pe.wait_ge(S["q_s"], t + 1)
                    pe.wait_ge(S["kv_s"], t + 1)
                    wait(pe, S["ngm_s"], t)
                    for g in range(GROUPS):
                        pe.transpose(cols(bank[0], g, P), cols(q_sb, g, P), ident)
                    pe.transpose(bank[1][:, 0:P], kv_sb[:, 0:KVW], ident).then_inc(S["qkt_ps"], 1)
                t = i
                if live(t):
                    pe.wait_ge(S["h_s"], t + 1)
                    wait(pe, S["qx_lo"], capped(1, t + 4))
                    for c in range(DC):
                        last = pe.transpose(cols(bank[5], c, P), cols(act2, c, P), ident)
                    last.then_inc(S["ht_ps"], 1)
                turn_context(i + 4)
                t = i + 2
                if live(t):
                    pe.wait_ge(S["vbd_s"], t + 1)
                    wait(pe, S["kv_s"], capped(1, t + 2))
                    wait(pe, S["z_s"], t - 2)
                    for b in range(2):
                        pe.wait_ge(S["probs_s"], 2 * t + b + 1)
                        for n in range(2):
                            for p in range(PAIRS):
                                lhs = ones_bd if n else vbd[:, b, p].rearrange("k h d -> k (h d)")
                                last = pe.matmul(bank[2 + b][32 * p:32 * (p + 1), 256 * n:256 * (n + 1)], lhs,
                                                 probs[:, b, p, :], start=True, stop=True)
                        last.then_inc(S["pv_ps"], 1)
                t = i + 1
                if live(t):
                    pe.wait_ge(S["t4_lo"], t + 1)
                    wait(pe, S["probs_s"], capped(2, t + 2))
                    for n in range(2):
                        if n == 1:
                            wait(pe, S["ct_lo"], capped(1, t + 4))
                        for c in range(DC):
                            w = slice(INNER * c + D * n, INNER * c + D * (n + 1))
                            last = split_product(bank[6 + n][:], cols(t4_h, c, P), cols(t4_l, c, P),
                                                 up_h[:, w], up_l[:, w], c == 0, c == DC - 1)
                        last.then_inc(S["u_ps"], 1)
                    for c in range(DC):
                        pe.matmul(bank[4][:, 0:2 * EXPERTS], cols(t4_h, c, P),
                                  gate_hl[:, c].rearrange("p a e -> p (a e)"), start=(c == 0), stop=False,
                                  skip_group_check=True)
                        last = pe.matmul(bank[4][:, 0:EXPERTS], cols(t4_l, c, P), gate_hl[:, c, 0, :],
                                         start=False, stop=(c == DC - 1), skip_group_check=True)
                    last.then_inc(S["gate_ps"], 1)
                def rough_scores(t, g):
                    for b in range(2):
                        last = pe.matmul(bank[g % 2][SEQ * b:SEQ * (b + 1), :],
                                         qt_b[:, P * g + SEQ * b:P * g + SEQ * (b + 1)], kbd_b[:, b, :],
                                         start=True, stop=True)
                    last.then_inc(S["g_ps"], 1)

                def down(t, part):
                    for c in range(DC):
                        last = split_product(bank[3][:], cols(ht_h, c, P), cols(ht_l, c, P),
                                             cols(down_h, DC * part + c, D), cols(down_l, DC * part + c, D),
                                             part == 0 and c == 0, part == 1 and c == DC - 1)
                    last.then_inc(S["dn_ps"], 1)

                t = i + 3
                if live(t):
                    pe.wait_ge(S["kbd_s"], 3 * t + 2)
                    pe.wait_ge(S["qt_bs"], t + 1)
                    pe.wait_ge(S["qt_lo"], t + 1)
                    pe.wait_ge(S["kt_lo"], t + 1)
                    for g in (0, 1):
                        rough_scores(t, g)
                t = i
                if live(t):
                    if isinstance(t, int) and t == 0:
                        pe.wait_ge(S["stage2_lo"], 2)
                    pe.wait_ge(S["ht_lo"], 2 * t + 1)
                    wait(pe, S["y_s"], capped(2, t + 3))
                    down(t, 0)
                t = i + 2
                if live(t):
                    pe.wait_ge(S["y_lo"], t + 1)
                    for g in range(GROUPS):
                        last = split_product(bank[2][:], cols(y_h, g, P), cols(y_l, g, P),
                                             cols(wo_h, g, D), cols(wo_l, g, D), g == 0, g == GROUPS - 1)
                    last.then_inc(S["wo_ps"], 1)
                t = i
                if live(t):
                    for c in range(DC):
                        last = pe.transpose(cols(bank[5], c, P), cols(act2, DC + c, P), ident)
                    last.then_inc(S["ht_ps"], 1)
                t = i + 3
                if live(t):
                    for g in (2, 3):
                        pe.wait_ge(S["gmax_s"], 4 * t + g - 1)
                        rough_scores(t, g)
                t = i + 1
                if live(t):
                    pe.wait_ge(S["lg_s"], t + 1)
                    for c in range(DC):
                        last = split_product(bank[4][:], cols(t4_h, c, P), cols(t4_l, c, P),
                                             cols(rt_h, c, D), cols(rt_l, c, D), c == 0, c == DC - 1)
                    last.then_inc(S["rt_out_ps"], 1)
                keys_values(i + 4)
                t = i + 3
                if live(t):
                    pe.wait_ge(S["gmax_s"], 4 * t + 4)
                    for g in range(GROUPS):
                        last = pe.transpose(bank[1][0:NKV, P * g:P * (g + 1)], cols(gmax, g, NKV), ident)
                    last.then_inc(S["gmt_ps"], 1)
                t = i
                if live(t):
                    pe.wait_ge(S["ht_lo"], 2 * t + 2)
                    down(t, 1)

                def scores(t, b):
                    for p in range(PAIRS):
                        last = pe.matmul(wide[:, 256 * p:256 * (p + 1)], k_stack[:, p, b, :],
                                         q_stack[:, p, :].rearrange("r (g b q) -> r g b q", g=GROUPS, b=2)[:, :, b, :],
                                         start=True, stop=True)
                    last.then_inc(S["s_ps"], 1)

                t = i + 3
                if live(t):
                    pe.wait_ge(S["kbd_s"], 3 * t + 3)
                    pe.wait_ge(S["sel_s"], 3)
                    pe.wait_ge(S["qs_s"], t + 1)
                    pe.wait_ge(S["ngm_s"], t + 1)
                    wait(pe, S["relu_s"], 2 * (t - 1))
                    scores(t, 0)
                queries(i + 4)
                t = i + 3
                if live(t):
                    pe.wait_ge(S["probs_s"], 2 * t + 1)
                    scores(t, 1)

            pass2_loop(pe, body2)


_INS = ["x", "ctx_4096", "L0_ffn_lora_A", "L0_ffn_lora_B", "L0_ffn_W", "L0_ffn_bias", "L0_ffn_lora_weights",
        "L1_xattn_Wq", "L1_xattn_bq", "L1_xattn_Wk", "L1_xattn_bk", "L1_xattn_Wv", "L1_xattn_bv",
        "L1_xattn_Wo", "L1_xattn_bo", "L1_ffn_gate_w", "L1_ffn_up_w", "L1_ffn_down_w", "L1_ffn_fc1_w",
        "L1_ffn_fc2_w", "L1_ffn_expert_w", "L1_ffn_ln_gamma", "L1_ffn_ln_beta"]


def kernel(**inputs):
    import numpy as _np
    import concourse.bacc as _bacc
    from concourse import mybir as _mybir
    from concourse.bass_utils import run_bass_kernel_spmd as _run

    nc = _bacc.Bacc("TRN2", target_bir_lowering=False, num_devices=1)
    arrays, args = {}, []
    dft, small = constants()
    named = [(name, _np.ascontiguousarray(inputs[name])) for name in _INS] + [("dft", dft), ("small", small)]
    for name, a in named:
        arrays[f"in_{name}"] = a
        args.append(nc.dram_tensor(f"in_{name}", a.shape, _mybir.dt.from_np(a.dtype), kind="ExternalInput").ap())
    out = nc.dram_tensor("out", (BATCHES, SEQ, D), _mybir.dt.float32, kind="ExternalOutput").ap()
    build(nc, *args, out)
    return _run(nc, [arrays], core_ids=[0]).results[0]["out"]
```
